# Optimizing a Trainium2 kernel written in Bass

```python
import numpy as np
import jax
import jax.numpy as jnp

def _softmax(x, axis=-1):
    return jax.nn.softmax(x, axis=axis)

def _gelu(x):
    return jax.nn.gelu(x, approximate=True)

def _silu(x):
    return jax.nn.silu(x)

def _sigmoid(x):
    return jax.nn.sigmoid(x)

def _layernorm(x, axis=-1, eps=1e-05):
    m = jnp.mean(x, axis=axis, keepdims=True)
    v = jnp.var(x, axis=axis, keepdims=True)
    return (x - m) / jnp.sqrt(v + eps)

def _scatter_add(tgt, idx, src, axis=0):
    return tgt.at[idx].add(src)

def _segment_sum(src, seg, n):
    return jax.ops.segment_sum(src, seg, n)
kernel_name = 'mk_decoder_postln_d2_seqx_r8_7b1a79'

def setup_inputs(seed: int=0):
    np.random.seed(seed)
    _w = jnp.asarray

    def _rec_inputs():
        import jax
        import jax.numpy as jnp
        _rk = jax.random.key(seed)
        x = 2.818e-05 + 1 * jax.random.normal(jax.random.fold_in(_rk, 1), (32, 128, 128), jnp.float32)
        _lenS = 128 - jax.random.randint(jax.random.fold_in(_rk, 7), (32,), 0, max(1, 128 // 4) + 1, jnp.int32)
        _lenS2 = 77 - jax.random.randint(jax.random.fold_in(_rk, 8), (32,), 0, max(1, 77 // 4) + 1, jnp.int32)
        _ctx_1024P = jax.random.normal(jax.random.fold_in(_rk, 11), (32, 16, 128), jnp.float32)
        _ctx_1024c = jax.random.dirichlet(jax.random.fold_in(_rk, 511), 0.3 * jnp.ones((16,), jnp.float32), (32, 77))
        _ctx_1024t = jnp.einsum('bsk,bkd->bsd', _ctx_1024c, _ctx_1024P)
        _ctx_1024t = _ctx_1024t * jax.lax.rsqrt(jnp.mean(jnp.square(_ctx_1024t)) + 1e-12) * 0.953939
        ctx_1024 = -0.000125008 + 0.999885 * (_ctx_1024t + 0.3 * jax.random.normal(jax.random.fold_in(_rk, 611), (32, 77, 128), jnp.float32))
        fside_Bx16xSxS2_0 = 9.80324e-06 + 0.100009 * jax.random.normal(jax.random.fold_in(_rk, 12), (32, 16, 128, 77), jnp.float32)
        fside_SxS2_0 = -2.64403e-05 + 0.100002 * jax.random.normal(jax.random.fold_in(_rk, 14), (128, 77), jnp.float32)
        _validS = jnp.arange(128)[None, :] < _lenS[:, None]
        _validS2 = jnp.arange(77)[None, :] < _lenS2[:, None]
        _causal = jnp.tril(jnp.ones((128, 128), dtype=bool))
        mask_BxS2_bf0 = jnp.logical_not(jnp.ones((32, 77), dtype=bool))
        return (x, ctx_1024, fside_Bx16xSxS2_0, fside_SxS2_0, mask_BxS2_bf0)
    x, ctx_1024, fside_Bx16xSxS2_0, fside_SxS2_0, mask_BxS2_bf0 = _rec_inputs()

    def _L0_attn_setup():
        import jax, jax.numpy as jnp
        import numpy as np
        import math
        D_MODEL = 128
        NUM_HEADS = 16
        THETA = 10000.0

        def _rope(x, theta):
            n, d_k = (x.shape[-2], x.shape[-1])
            powers = jnp.arange(0, d_k, 2, dtype=jnp.float32) / d_k
            freqs = 1.0 / theta ** powers
            t = jnp.arange(n, dtype=jnp.float32)
            angles = jnp.outer(t, freqs)
            cos = jnp.cos(angles).astype(x.dtype)
            sin = jnp.sin(angles).astype(x.dtype)
            x_even = x[..., 0::2]
            x_odd = x[..., 1::2]
            rot_even = x_even * cos - x_odd * sin
            rot_odd = x_even * sin + x_odd * cos
            return jnp.stack([rot_even, rot_odd], axis=-1).reshape(x.shape)
        key = jax.random.key(seed)
        ks = jax.random.split(key, 5)
        B, N, D = (2, 256, D_MODEL)
        std = math.sqrt(2.0 / (D + D))
        x = jax.random.normal(ks[0], (B, N, D), dtype=jnp.float32)
        wq = jax.random.normal(ks[1], (D, D), dtype=jnp.float32) * std
        wk = jax.random.normal(ks[2], (D, D), dtype=jnp.float32) * std
        wv = jax.random.normal(ks[3], (D, D), dtype=jnp.float32) * std
        wo = jax.random.normal(ks[4], (D, D), dtype=jnp.float32) * std
        return {'x': x, 'wq': wq, 'wk': wk, 'wv': wv, 'wo': wo}
    _L0_attn_all = _L0_attn_setup()
    _L0_attn_in = {k: v for k, v in _L0_attn_all.items() if k in ('wq', 'wk', 'wv', 'wo')}
    del _L0_attn_all

    def _L0_xattn_setup():
        import jax, jax.numpy as jnp
        import numpy as np
        H = 8
        D = 128
        DQ = D // H
        BN = 64
        HID = 128
        B = 16
        S_T = 128
        S_M = 256
        SCALE = DQ ** 0.25
        EPS = 1e-05

        def _ln(x, g, b):
            m = jnp.mean(x, axis=-1, keepdims=True)
            v = jnp.mean(jnp.square(x - m), axis=-1, keepdims=True)
            return (x - m) * jax.lax.rsqrt(v + EPS) * g + b

        def _mhla(xq, xk, xv, Wq, Wk, Wv, Wo, masked):
            Q = jnp.einsum('bsq,hqd->bhsd', xq, Wq)
            K = jnp.einsum('bsq,hqd->bhsd', xk, Wk)
            V = jnp.einsum('bsq,hqd->bhsd', xv, Wv)
            if masked:
                s, d = (Q.shape[-2], Q.shape[-1])
                m = jnp.where(jnp.arange(d)[None, :] <= jnp.arange(s)[:, None], 0.0, -jnp.inf)
                Q = Q + m.astype(Q.dtype)
            A = jnp.einsum('bhsd,bhse->bhde', jax.nn.softmax(K / SCALE, axis=-1), V)
            Bm = jnp.einsum('bhsd,bhde->bhse', jax.nn.softmax(Q / SCALE, axis=-1), A)
            b, h, w, dd = Bm.shape
            Bm = Bm.reshape(b, w, h * dd)
            return Bm @ Wo.T
        key = jax.random.key(seed)
        ks = jax.random.split(key, 24)
        r = lambda k, sh, s=0.02: jax.random.normal(k, sh, jnp.float32) * s
        return {'mem': jax.random.normal(ks[0], (B, S_M, D), jnp.float32), 'y': jax.random.normal(ks[1], (B, S_T, D), jnp.float32), 'Wq1': r(ks[2], (H, D, DQ)), 'Wk1': r(ks[3], (H, D, DQ)), 'Wv1': r(ks[4], (H, D, DQ)), 'Wo1': r(ks[5], (D, D)), 'Wq2': r(ks[6], (H, D, DQ)), 'Wk2': r(ks[7], (H, D, DQ)), 'Wv2': r(ks[8], (H, D, DQ)), 'Wo2': r(ks[9], (D, D)), 'E1': r(ks[10], (BN, D)), 'D1': r(ks[11], (HID, BN)), 'E2': r(ks[12], (BN, HID)), 'D2': r(ks[13], (D, BN)), 'g1': jnp.ones((D,), jnp.float32), 'b1': jnp.zeros((D,), jnp.float32), 'g2': jnp.ones((D,), jnp.float32), 'b2': jnp.zeros((D,), jnp.float32), 'g3': jnp.ones((D,), jnp.float32), 'b3': jnp.zeros((D,), jnp.float32)}
    _L0_xattn_all = _L0_xattn_setup()
    _L0_xattn_in = {k: v for k, v in _L0_xattn_all.items() if k in ('Wq1', 'Wk1', 'Wv1', 'Wo1', 'Wq2', 'Wk2', 'Wv2', 'Wo2', 'E1', 'D1', 'E2', 'D2', 'g1', 'b1', 'g2', 'b2', 'g3', 'b3')}
    del _L0_xattn_all

    def _L0_ffn_setup():
        import jax, jax.numpy as jnp
        import numpy as np
        D_MODEL = 128
        H_SHARED = 256
        H_ROUTED = 128
        N_EXPERTS = 8
        TOP_K = 2
        key = jax.random.key(seed)
        ks = jax.random.split(key, 8)
        B, T = (2, 256)
        sc_d = 1.0 / np.sqrt(D_MODEL)
        sc_hs = 1.0 / np.sqrt(H_SHARED)
        sc_hr = 1.0 / np.sqrt(H_ROUTED)
        return {'x': jax.random.normal(ks[0], (B, T, D_MODEL), dtype=jnp.float32), 'router_w': jax.random.normal(ks[1], (N_EXPERTS, D_MODEL), dtype=jnp.float32) * sc_d, 'router_bias': jnp.zeros((N_EXPERTS,), dtype=jnp.float32), 'sw1': jax.random.normal(ks[2], (D_MODEL, H_SHARED), dtype=jnp.float32) * sc_d, 'sw3': jax.random.normal(ks[3], (D_MODEL, H_SHARED), dtype=jnp.float32) * sc_d, 'sw2': jax.random.normal(ks[4], (H_SHARED, D_MODEL), dtype=jnp.float32) * sc_hs, 'ew1': jax.random.normal(ks[5], (N_EXPERTS, D_MODEL, H_ROUTED), dtype=jnp.float32) * sc_d, 'ew2': jax.random.normal(ks[6], (N_EXPERTS, H_ROUTED, D_MODEL), dtype=jnp.float32) * sc_hr}
    _L0_ffn_all = _L0_ffn_setup()
    _L0_ffn_in = {k: v for k, v in _L0_ffn_all.items() if k in ('router_w', 'router_bias', 'sw1', 'sw3', 'sw2', 'ew1', 'ew2')}
    del _L0_ffn_all

    def _L1_attn_setup():
        import jax, jax.numpy as jnp
        import numpy as np
        from jax import lax
        D_MODEL = 128
        D_STATE = 16
        D_CONV = 4
        EXPAND = 2
        D_INNER = EXPAND * D_MODEL
        DT_RANK = (D_MODEL + 15) // 16
        B, L = (4, 256)

        def _silu(v):
            return v * jax.nn.sigmoid(v)

        def _mamba_forward(x, ln_w, ln_b, W_in, conv_w, conv_b, W_xproj, W_dt, b_dt, A_log, D_param, W_out):
            eps = 1e-05
            mu = jnp.mean(x, axis=-1, keepdims=True)
            var = jnp.mean(jnp.square(x - mu), axis=-1, keepdims=True)
            xn = (x - mu) * lax.rsqrt(var + eps) * ln_w + ln_b
            xz = jnp.einsum('bld,de->ble', xn, W_in)
            x_in, z = jnp.split(xz, 2, axis=-1)
            xt = jnp.transpose(x_in, (0, 2, 1))
            xc = lax.conv_general_dilated(xt, conv_w, window_strides=(1,), padding=[(D_CONV - 1, 0)], feature_group_count=D_INNER, dimension_numbers=('NCH', 'OIH', 'NCH'))
            xc = _silu(xc + conv_b[None, :, None])
            xc = jnp.transpose(xc, (0, 2, 1))
            xdbl = jnp.einsum('bld,de->ble', xc, W_xproj)
            dt_r = xdbl[..., :DT_RANK]
            Bm = xdbl[..., DT_RANK:DT_RANK + D_STATE]
            Cm = xdbl[..., DT_RANK + D_STATE:]
            dt = jax.nn.softplus(jnp.einsum('blr,rd->bld', dt_r, W_dt) + b_dt)
            A = -jnp.exp(A_log)

            def step(h, inp):
                dt_t, B_t, C_t, u_t = inp
                dA = jnp.exp(dt_t[:, :, None] * A)
                h = h * dA + dt_t[:, :, None] * B_t[:, None, :] * u_t[:, :, None]
                y = jnp.einsum('bdn,bn->bd', h, C_t)
                return (h, y)
            h0 = jnp.zeros((x.shape[0], D_INNER, D_STATE), x.dtype)
            xs = (jnp.swapaxes(dt, 0, 1), jnp.swapaxes(Bm, 0, 1), jnp.swapaxes(Cm, 0, 1), jnp.swapaxes(xc, 0, 1))
            _, ys = lax.scan(step, h0, xs)
            y = jnp.swapaxes(ys, 0, 1) + xc * D_param
            y = y * _silu(z)
            out = jnp.einsum('bld,de->ble', y, W_out)
            return x + out
        key = jax.random.key(seed)
        ks = jax.random.split(key, 12)
        g = lambda k, sh, s: jax.random.normal(k, sh, dtype=jnp.float32) * s
        A_log = jnp.log(jnp.tile(jnp.arange(1, D_STATE + 1, dtype=jnp.float32)[None, :], (D_INNER, 1)))
        return {'x': g(ks[0], (B, L, D_MODEL), 1.0), 'ln_w': jnp.ones((D_MODEL,), jnp.float32), 'ln_b': jnp.zeros((D_MODEL,), jnp.float32), 'W_in': g(ks[1], (D_MODEL, 2 * D_INNER), 0.02), 'conv_w': g(ks[2], (D_INNER, 1, D_CONV), 0.1), 'conv_b': g(ks[3], (D_INNER,), 0.02), 'W_xproj': g(ks[4], (D_INNER, DT_RANK + 2 * D_STATE), 0.02), 'W_dt': g(ks[5], (DT_RANK, D_INNER), 0.02), 'b_dt': g(ks[6], (D_INNER,), 0.5), 'A_log': A_log, 'D_param': jnp.ones((D_INNER,), jnp.float32), 'W_out': g(ks[7], (D_INNER, D_MODEL), 0.02)}
    _L1_attn_all = _L1_attn_setup()
    _L1_attn_in = {k: v for k, v in _L1_attn_all.items() if k in ('ln_w', 'ln_b', 'W_in', 'conv_w', 'conv_b', 'W_xproj', 'W_dt', 'b_dt', 'A_log', 'D_param', 'W_out')}
    del _L1_attn_all

    def _L1_xattn_setup():
        import jax, jax.numpy as jnp
        import numpy as np
        E = 128
        H = 16
        D = E // H
        key = jax.random.key(seed)
        ks = jax.random.split(key, 12)
        B, T, S = (2, 256, 256)
        inp = {'query': jax.random.normal(ks[0], (B, T, E), jnp.float32), 'key': jax.random.normal(ks[1], (B, S, E), jnp.float32), 'value': jax.random.normal(ks[2], (B, S, E), jnp.float32), 'spatial_bias': jax.random.normal(ks[3], (B, H, T, S), jnp.float32) * 0.1, 'directional_bias': jax.random.normal(ks[4], (B, H, T, S), jnp.float32) * 0.1, 'key_padding_mask': jnp.zeros((B, S), dtype=bool), 'attn_mask': jax.random.normal(ks[5], (T, S), jnp.float32) * 0.1, 'Wq': jax.random.normal(ks[6], (E, E), jnp.float32) / np.sqrt(E), 'bq': jnp.zeros((E,), jnp.float32), 'Wk': jax.random.normal(ks[7], (E, E), jnp.float32) / np.sqrt(E), 'bk': jnp.zeros((E,), jnp.float32), 'Wv': jax.random.normal(ks[8], (E, E), jnp.float32) / np.sqrt(E), 'bv': jnp.zeros((E,), jnp.float32), 'Wo': jax.random.normal(ks[9], (E, E), jnp.float32) / np.sqrt(E), 'bo': jnp.zeros((E,), jnp.float32)}
        return inp
    _L1_xattn_all = _L1_xattn_setup()
    _L1_xattn_in = {k: v for k, v in _L1_xattn_all.items() if k in ('Wq', 'bq', 'Wk', 'bk', 'Wv', 'bv', 'Wo', 'bo')}
    del _L1_xattn_all

    def _L1_ffn_setup():
        import jax, jax.numpy as jnp
        import numpy as np
        EPS = 0.05
        N_ITERS = 20
        TOP_K = 2

        def _sinkhorn(cost, n_iters=N_ITERS, epsilon=EPS):
            la = cost / epsilon
            for _ in range(n_iters):
                la = la - jax.scipy.special.logsumexp(la, axis=-1, keepdims=True)
                la = la - jax.scipy.special.logsumexp(la, axis=-2, keepdims=True)
            return jnp.exp(la)
        key = jax.random.key(seed)
        k0, k1, k2, k3, k4 = jax.random.split(key, 5)
        B, T, D, F, E = (2, 256, 128, 512, 8)
        x = jax.random.normal(k0, (B, T, D), dtype=jnp.float32)
        gate_W = jax.random.normal(k1, (E, D), dtype=jnp.float32) * 0.02
        W_gate = jax.random.normal(k2, (E, F, D), dtype=jnp.float32) * 0.02
        W_up = jax.random.normal(k3, (E, F, D), dtype=jnp.float32) * 0.02
        W_down = jax.random.normal(k4, (E, D, F), dtype=jnp.float32) * 0.02
        return {'x': x, 'gate_W': gate_W, 'W_gate': W_gate, 'W_up': W_up, 'W_down': W_down}
    _L1_ffn_all = _L1_ffn_setup()
    _L1_ffn_in = {k: v for k, v in _L1_ffn_all.items() if k in ('gate_W', 'W_gate', 'W_up', 'W_down')}
    del _L1_ffn_all
    return {'x': x, 'ctx_1024': ctx_1024, 'fside_Bx16xSxS2_0': fside_Bx16xSxS2_0, 'fside_SxS2_0': fside_SxS2_0, 'mask_BxS2_bf0': mask_BxS2_bf0, 'L0_attn_wq': _L0_attn_in['wq'], 'L0_attn_wk': _L0_attn_in['wk'], 'L0_attn_wv': _L0_attn_in['wv'], 'L0_attn_wo': _L0_attn_in['wo'], 'L0_xattn_Wq1': _L0_xattn_in['Wq1'], 'L0_xattn_Wk1': _L0_xattn_in['Wk1'], 'L0_xattn_Wv1': _L0_xattn_in['Wv1'], 'L0_xattn_Wo1': _L0_xattn_in['Wo1'], 'L0_xattn_Wq2': _L0_xattn_in['Wq2'], 'L0_xattn_Wk2': _L0_xattn_in['Wk2'], 'L0_xattn_Wv2': _L0_xattn_in['Wv2'], 'L0_xattn_Wo2': _L0_xattn_in['Wo2'], 'L0_xattn_E1': _L0_xattn_in['E1'], 'L0_xattn_D1': _L0_xattn_in['D1'], 'L0_xattn_E2': _L0_xattn_in['E2'], 'L0_xattn_D2': _L0_xattn_in['D2'], 'L0_xattn_g1': _L0_xattn_in['g1'], 'L0_xattn_b1': _L0_xattn_in['b1'], 'L0_xattn_g2': _L0_xattn_in['g2'], 'L0_xattn_b2': _L0_xattn_in['b2'], 'L0_xattn_g3': _L0_xattn_in['g3'], 'L0_xattn_b3': _L0_xattn_in['b3'], 'L0_ffn_router_w': _L0_ffn_in['router_w'], 'L0_ffn_router_bias': _L0_ffn_in['router_bias'], 'L0_ffn_sw1': _L0_ffn_in['sw1'], 'L0_ffn_sw3': _L0_ffn_in['sw3'], 'L0_ffn_sw2': _L0_ffn_in['sw2'], 'L0_ffn_ew1': _L0_ffn_in['ew1'], 'L0_ffn_ew2': _L0_ffn_in['ew2'], 'L1_attn_ln_w': _L1_attn_in['ln_w'], 'L1_attn_ln_b': _L1_attn_in['ln_b'], 'L1_attn_W_in': _L1_attn_in['W_in'], 'L1_attn_conv_w': _L1_attn_in['conv_w'], 'L1_attn_conv_b': _L1_attn_in['conv_b'], 'L1_attn_W_xproj': _L1_attn_in['W_xproj'], 'L1_attn_W_dt': _L1_attn_in['W_dt'], 'L1_attn_b_dt': _L1_attn_in['b_dt'], 'L1_attn_A_log': _L1_attn_in['A_log'], 'L1_attn_D_param': _L1_attn_in['D_param'], 'L1_attn_W_out': _L1_attn_in['W_out'], 'L1_xattn_Wq': _L1_xattn_in['Wq'], 'L1_xattn_bq': _L1_xattn_in['bq'], 'L1_xattn_Wk': _L1_xattn_in['Wk'], 'L1_xattn_bk': _L1_xattn_in['bk'], 'L1_xattn_Wv': _L1_xattn_in['Wv'], 'L1_xattn_bv': _L1_xattn_in['bv'], 'L1_xattn_Wo': _L1_xattn_in['Wo'], 'L1_xattn_bo': _L1_xattn_in['bo'], 'L1_ffn_gate_W': _L1_ffn_in['gate_W'], 'L1_ffn_W_gate': _L1_ffn_in['W_gate'], 'L1_ffn_W_up': _L1_ffn_in['W_up'], 'L1_ffn_W_down': _L1_ffn_in['W_down']}

def reference(x, ctx_1024, fside_Bx16xSxS2_0, fside_SxS2_0, mask_BxS2_bf0, L0_attn_wq, L0_attn_wk, L0_attn_wv, L0_attn_wo, L0_xattn_Wq1, L0_xattn_Wk1, L0_xattn_Wv1, L0_xattn_Wo1, L0_xattn_Wq2, L0_xattn_Wk2, L0_xattn_Wv2, L0_xattn_Wo2, L0_xattn_E1, L0_xattn_D1, L0_xattn_E2, L0_xattn_D2, L0_xattn_g1, L0_xattn_b1, L0_xattn_g2, L0_xattn_b2, L0_xattn_g3, L0_xattn_b3, L0_ffn_router_w, L0_ffn_router_bias, L0_ffn_sw1, L0_ffn_sw3, L0_ffn_sw2, L0_ffn_ew1, L0_ffn_ew2, L1_attn_ln_w, L1_attn_ln_b, L1_attn_W_in, L1_attn_conv_w, L1_attn_conv_b, L1_attn_W_xproj, L1_attn_W_dt, L1_attn_b_dt, L1_attn_A_log, L1_attn_D_param, L1_attn_W_out, L1_xattn_Wq, L1_xattn_bq, L1_xattn_Wk, L1_xattn_bk, L1_xattn_Wv, L1_xattn_bv, L1_xattn_Wo, L1_xattn_bo, L1_ffn_gate_W, L1_ffn_W_gate, L1_ffn_W_up, L1_ffn_W_down):
    import jax
    import jax.numpy as jnp

    def _L0_attn_ref(x, wq, wk, wv, wo):
        import jax, jax.numpy as jnp
        import numpy as np
        import math
        D_MODEL = 128
        NUM_HEADS = 16
        THETA = 10000.0

        def _rope(x, theta):
            n, d_k = (x.shape[-2], x.shape[-1])
            powers = jnp.arange(0, d_k, 2, dtype=jnp.float32) / d_k
            freqs = 1.0 / theta ** powers
            t = jnp.arange(n, dtype=jnp.float32)
            angles = jnp.outer(t, freqs)
            cos = jnp.cos(angles).astype(x.dtype)
            sin = jnp.sin(angles).astype(x.dtype)
            x_even = x[..., 0::2]
            x_odd = x[..., 1::2]
            rot_even = x_even * cos - x_odd * sin
            rot_odd = x_even * sin + x_odd * cos
            return jnp.stack([rot_even, rot_odd], axis=-1).reshape(x.shape)
        B, N, D = x.shape
        H = NUM_HEADS
        d_k = D // H

        def split_heads(t):
            return t.reshape(B, N, H, d_k).transpose(0, 2, 1, 3)
        Q = split_heads(x @ wq.T)
        K = split_heads(x @ wk.T)
        V = split_heads(x @ wv.T)
        Q = _rope(Q, THETA)
        K = _rope(K, THETA)
        scale = 1.0 / math.sqrt(d_k)
        scores = jnp.einsum('bhqd,bhkd->bhqk', Q, K) * scale
        causal_mask = jnp.triu(jnp.ones((N, N), dtype=bool), k=1)
        scores = jnp.where(causal_mask, -jnp.inf, scores)
        attn = jax.nn.softmax(scores, axis=-1)
        out = jnp.einsum('bhqk,bhkd->bhqd', attn, V)
        out = out.transpose(0, 2, 1, 3).reshape(B, N, D)
        return out @ wo.T

    def _L0_xattn_ref(mem, y, Wq1, Wk1, Wv1, Wo1, Wq2, Wk2, Wv2, Wo2, E1, D1, E2, D2, g1, b1, g2, b2, g3, b3):
        import jax, jax.numpy as jnp
        import numpy as np
        H = 8
        D = 128
        DQ = D // H
        BN = 64
        HID = 128
        B = 16
        S_T = 128
        S_M = 256
        SCALE = DQ ** 0.25
        EPS = 1e-05

        def _ln(x, g, b):
            m = jnp.mean(x, axis=-1, keepdims=True)
            v = jnp.mean(jnp.square(x - m), axis=-1, keepdims=True)
            return (x - m) * jax.lax.rsqrt(v + EPS) * g + b

        def _mhla(xq, xk, xv, Wq, Wk, Wv, Wo, masked):
            Q = jnp.einsum('bsq,hqd->bhsd', xq, Wq)
            K = jnp.einsum('bsq,hqd->bhsd', xk, Wk)
            V = jnp.einsum('bsq,hqd->bhsd', xv, Wv)
            if masked:
                s, d = (Q.shape[-2], Q.shape[-1])
                m = jnp.where(jnp.arange(d)[None, :] <= jnp.arange(s)[:, None], 0.0, -jnp.inf)
                Q = Q + m.astype(Q.dtype)
            A = jnp.einsum('bhsd,bhse->bhde', jax.nn.softmax(K / SCALE, axis=-1), V)
            Bm = jnp.einsum('bhsd,bhde->bhse', jax.nn.softmax(Q / SCALE, axis=-1), A)
            b, h, w, dd = Bm.shape
            Bm = Bm.reshape(b, w, h * dd)
            return Bm @ Wo.T
        y = y + _mhla(y, y, y, Wq1, Wk1, Wv1, Wo1, masked=True)
        y = _ln(y, g1, b1)
        y = y + _mhla(y, mem, mem, Wq2, Wk2, Wv2, Wo2, masked=False)
        y = _ln(y, g2, b2)
        h = y @ E1.T @ D1.T
        h = h * jax.nn.sigmoid(h)
        ffn = h @ E2.T @ D2.T
        y = _ln(y + ffn, g3, b3)
        return y

    def _L0_ffn_ref(x, router_w, router_bias, sw1, sw3, sw2, ew1, ew2):
        import jax, jax.numpy as jnp
        import numpy as np
        D_MODEL = 128
        H_SHARED = 256
        H_ROUTED = 128
        N_EXPERTS = 8
        TOP_K = 2
        B, T, C = x.shape
        xf = x.reshape(-1, C)
        shared_out = jax.nn.silu(xf @ sw1) * (xf @ sw3) @ sw2
        s = jax.nn.sigmoid((xf @ router_w.T).astype(jnp.float32))
        sel_scores = s + router_bias.astype(jnp.float32)
        _, topk_idx = jax.lax.top_k(sel_scores, TOP_K)
        s_sel = jnp.take_along_axis(s, topk_idx, axis=1)
        denom = s_sel.sum(axis=1, keepdims=True)
        gates = jnp.where(denom > 1e-09, s_sel / (denom + 1e-09), 1.0 / TOP_K).astype(x.dtype)
        one_hot = jax.nn.one_hot(topk_idx, N_EXPERTS, dtype=x.dtype)
        comb = jnp.einsum('nke,nk->ne', one_hot, gates)
        h = jax.nn.gelu(jnp.einsum('nd,edh->neh', xf, ew1), approximate=False)
        y = jnp.einsum('neh,ehd->ned', h, ew2)
        routed_out = jnp.einsum('ned,ne->nd', y, comb)
        return (shared_out + routed_out).reshape(B, T, C)

    def _L1_attn_ref(x, ln_w, ln_b, W_in, conv_w, conv_b, W_xproj, W_dt, b_dt, A_log, D_param, W_out):
        import jax, jax.numpy as jnp
        import numpy as np
        from jax import lax
        D_MODEL = 128
        D_STATE = 16
        D_CONV = 4
        EXPAND = 2
        D_INNER = EXPAND * D_MODEL
        DT_RANK = (D_MODEL + 15) // 16
        B, L = (4, 256)

        def _silu(v):
            return v * jax.nn.sigmoid(v)

        def _mamba_forward(x, ln_w, ln_b, W_in, conv_w, conv_b, W_xproj, W_dt, b_dt, A_log, D_param, W_out):
            eps = 1e-05
            mu = jnp.mean(x, axis=-1, keepdims=True)
            var = jnp.mean(jnp.square(x - mu), axis=-1, keepdims=True)
            xn = (x - mu) * lax.rsqrt(var + eps) * ln_w + ln_b
            xz = jnp.einsum('bld,de->ble', xn, W_in)
            x_in, z = jnp.split(xz, 2, axis=-1)
            xt = jnp.transpose(x_in, (0, 2, 1))
            xc = lax.conv_general_dilated(xt, conv_w, window_strides=(1,), padding=[(D_CONV - 1, 0)], feature_group_count=D_INNER, dimension_numbers=('NCH', 'OIH', 'NCH'))
            xc = _silu(xc + conv_b[None, :, None])
            xc = jnp.transpose(xc, (0, 2, 1))
            xdbl = jnp.einsum('bld,de->ble', xc, W_xproj)
            dt_r = xdbl[..., :DT_RANK]
            Bm = xdbl[..., DT_RANK:DT_RANK + D_STATE]
            Cm = xdbl[..., DT_RANK + D_STATE:]
            dt = jax.nn.softplus(jnp.einsum('blr,rd->bld', dt_r, W_dt) + b_dt)
            A = -jnp.exp(A_log)

            def step(h, inp):
                dt_t, B_t, C_t, u_t = inp
                dA = jnp.exp(dt_t[:, :, None] * A)
                h = h * dA + dt_t[:, :, None] * B_t[:, None, :] * u_t[:, :, None]
                y = jnp.einsum('bdn,bn->bd', h, C_t)
                return (h, y)
            h0 = jnp.zeros((x.shape[0], D_INNER, D_STATE), x.dtype)
            xs = (jnp.swapaxes(dt, 0, 1), jnp.swapaxes(Bm, 0, 1), jnp.swapaxes(Cm, 0, 1), jnp.swapaxes(xc, 0, 1))
            _, ys = lax.scan(step, h0, xs)
            y = jnp.swapaxes(ys, 0, 1) + xc * D_param
            y = y * _silu(z)
            out = jnp.einsum('bld,de->ble', y, W_out)
            return x + out
        return _mamba_forward(x, ln_w, ln_b, W_in, conv_w, conv_b, W_xproj, W_dt, b_dt, A_log, D_param, W_out)

    def _L1_xattn_ref(query, key, value, spatial_bias, directional_bias, key_padding_mask, attn_mask, Wq, bq, Wk, bk, Wv, bv, Wo, bo):
        import jax, jax.numpy as jnp
        import numpy as np
        E = 128
        H = 16
        D = E // H
        B, T, _ = query.shape
        S = key.shape[1]
        scale = D ** (-0.5)
        q = (query @ Wq.T + bq).reshape(B, T, H, D).transpose(0, 2, 1, 3)
        k = (key @ Wk.T + bk).reshape(B, S, H, D).transpose(0, 2, 1, 3)
        v = (value @ Wv.T + bv).reshape(B, S, H, D).transpose(0, 2, 1, 3)
        scores = jnp.einsum('bhtd,bhsd->bhts', q, k) * scale
        scores = scores + attn_mask[None, None, :, :]
        pad = key_padding_mask[:, None, None, :]
        scores = jnp.where(pad, -jnp.inf, scores)
        if T == S:
            scores = scores + spatial_bias + directional_bias
        probs = jax.nn.softmax(scores, axis=-1)
        out = jnp.einsum('bhts,bhsd->bhtd', probs, v)
        out = out.transpose(0, 2, 1, 3).reshape(B, T, E)
        return out @ Wo.T + bo

    def _L1_ffn_ref(x, gate_W, W_gate, W_up, W_down):
        import jax, jax.numpy as jnp
        import numpy as np
        EPS = 0.05
        N_ITERS = 20
        TOP_K = 2

        def _sinkhorn(cost, n_iters=N_ITERS, epsilon=EPS):
            la = cost / epsilon
            for _ in range(n_iters):
                la = la - jax.scipy.special.logsumexp(la, axis=-1, keepdims=True)
                la = la - jax.scipy.special.logsumexp(la, axis=-2, keepdims=True)
            return jnp.exp(la)
        B, T, D = x.shape
        xf = x.reshape(B * T, D)
        logits = xf @ gate_W.T
        pi = _sinkhorn(-logits)
        _, top_idx = jax.lax.top_k(pi, TOP_K)
        g = jnp.einsum('nd,efd->enf', xf, W_gate)
        u = jnp.einsum('nd,efd->enf', xf, W_up)
        y = jnp.einsum('enf,edf->end', jax.nn.silu(g) * u, W_down)
        n_ar = jnp.arange(xf.shape[0])
        out = jnp.zeros_like(xf)
        for k in range(TOP_K):
            out = out + y[top_idx[:, k], n_ar] * pi[:, k:k + 1]
        return out.reshape(B, T, D)
    x = _layernorm(x + _L0_attn_ref(x, L0_attn_wq, L0_attn_wk, L0_attn_wv, L0_attn_wo), axis=-1)
    x = _layernorm(x + _L0_xattn_ref(ctx_1024, x, L0_xattn_Wq1, L0_xattn_Wk1, L0_xattn_Wv1, L0_xattn_Wo1, L0_xattn_Wq2, L0_xattn_Wk2, L0_xattn_Wv2, L0_xattn_Wo2, L0_xattn_E1, L0_xattn_D1, L0_xattn_E2, L0_xattn_D2, L0_xattn_g1, L0_xattn_b1, L0_xattn_g2, L0_xattn_b2, L0_xattn_g3, L0_xattn_b3), axis=-1)
    x = _layernorm(x + _L0_ffn_ref(x, L0_ffn_router_w, L0_ffn_router_bias, L0_ffn_sw1, L0_ffn_sw3, L0_ffn_sw2, L0_ffn_ew1, L0_ffn_ew2), axis=-1)
    x = _layernorm(x + _L1_attn_ref(x, L1_attn_ln_w, L1_attn_ln_b, L1_attn_W_in, L1_attn_conv_w, L1_attn_conv_b, L1_attn_W_xproj, L1_attn_W_dt, L1_attn_b_dt, L1_attn_A_log, L1_attn_D_param, L1_attn_W_out), axis=-1)
    x = _layernorm(x + _L1_xattn_ref(x, ctx_1024, ctx_1024, fside_Bx16xSxS2_0, fside_Bx16xSxS2_0, mask_BxS2_bf0, fside_SxS2_0, L1_xattn_Wq, L1_xattn_bq, L1_xattn_Wk, L1_xattn_bk, L1_xattn_Wv, L1_xattn_bv, L1_xattn_Wo, L1_xattn_bo), axis=-1)
    x = _layernorm(x + _L1_ffn_ref(x, L1_ffn_gate_W, L1_ffn_W_gate, L1_ffn_W_up, L1_ffn_W_down), axis=-1)
    return x

_drawn_inputs = setup_inputs


def setup_inputs(seed=0):
    import zlib

    import numpy as np

    out = dict(_drawn_inputs(seed))
    spreads = {'L0_xattn_g1': (1.0, 0.2),
     'L0_xattn_b1': (0.0, 0.1),
     'L0_xattn_g2': (1.0, 0.2),
     'L0_xattn_b2': (0.0, 0.1),
     'L0_xattn_g3': (1.0, 0.2),
     'L0_xattn_b3': (0.0, 0.1),
     'L0_ffn_router_bias': (0.0, 0.1),
     'L1_attn_ln_w': (1.0, 0.6),
     'L1_attn_ln_b': (0.0, 0.8),
     'L1_attn_D_param': (1.0, 0.6),
     'L1_xattn_bq': (0.0, 0.393),
     'L1_xattn_bk': (0.0, 2.0),
     'L1_xattn_bv': (0.0, 0.1),
     'L1_xattn_bo': (0.0, 0.1)}
    factors = {'fside_SxS2_0': 4.714,
     'L0_xattn_Wq1': 8.0,
     'L0_xattn_Wk1': 8.0,
     'L0_xattn_Wq2': 8.0,
     'L0_xattn_Wk2': 8.0,
     'L0_xattn_E1': 8.0,
     'L0_xattn_D1': 8.0,
     'L0_xattn_E2': 8.0,
     'L0_xattn_D2': 8.0,
     'L1_attn_W_in': 8.0,
     'L1_attn_conv_w': 8.0,
     'L1_attn_conv_b': 8.0,
     'L1_attn_W_xproj': 8.0,
     'L1_attn_W_dt': 8.0,
     'L1_attn_b_dt': 8.0,
     'L1_attn_A_log': 8.0,
     'L1_attn_W_out': 8.0,
     'L1_ffn_gate_W': 60.014,
     'L1_ffn_W_gate': 64.0,
     'L1_ffn_W_up': 58.255,
     'L1_ffn_W_down': 58.332}
    for name, (base, spread) in spreads.items():
        noise = np.random.default_rng([zlib.crc32(name.encode()), seed]).standard_normal(out[name].shape)
        drawn = base * np.exp(spread * noise) if base else spread * noise
        out[name] = jnp.asarray(drawn.astype(out[name].dtype))
    for name, factor in factors.items():
        out[name] = (out[name] * factor).astype(out[name].dtype)
    return out
```

```python
from contextlib import ExitStack

import concourse.bass as bass
import numpy as np
from concourse import mybir

F32 = mybir.dt.float32
BF16 = mybir.dt.bfloat16
ALU = mybir.AluOpType
ACT = mybir.ActivationFunctionType
AX_X = mybir.AxisListType.X

P = 128
B = 32
D = 128
GB = 4
NG = B // GB
T = GB * P
S2 = 77
EPS = 1e-5
BIG = 1e30
UPTO = 6


class Core:

    def __init__(self, nc, ctx, dram):
        self.nc, self.ctx, self.dram, self.phase = nc, ctx, dram, []

    def sb(self, name, shape, dt=F32, ctx=None):
        return (ctx or self.ctx).enter_context(self.nc.sbuf_tensor(name, shape, dt))

    def sem(self, name):
        return self.ctx.enter_context(self.nc.semaphore(name))

    def sems(self, prefix, names):
        made = {n: self.nc.alloc_semaphore(name=prefix + n) for n in names.split()}
        self.phase += made.values()
        return made

    def end_phase(self, ctx):
        ctx.close()
        self.nc.clear_and_free_semaphores(self.phase)
        self.nc.all_engine_barrier()
        self.phase = []


def group(c, g):
    return c.X[:, bass.ds(g * GB, GB), :]


def flat(ap):
    return ap.rearrange("p b d -> p (b d)")



def ln_stats(dve, nc, src, ln, s, n):
    for b in range(GB):
        ins = nc.vector.bn_stats(ln["st"][:, b, :], src[:, b, :])
    dve.drain()
    for b in range(GB):
        ins = nc.vector.bn_aggr(ln["mv"][:, b, :], ln["st"][:, b, :])
    ins.then_inc(s["mv"], 1)


def ln_rstd(pool, nc, ln, s, n):
    pool.wait_ge(s["mv"], n)
    nc.gpsimd.tensor_tensor(ln["lv"][:, :], ln["mv"][:, :, 1], ln["eps"][:, :], ALU.add).then_inc(s["lv"], 1)
    pool.wait_ge(s["lv"], n)
    nc.gpsimd.tensor_tensor(ln["rs"][:, :], ln["lv"][:, :], ln["half"][:, :], ALU.pow).then_inc(s["rs"], 1)


def ln_apply(dve, nc, out, src, ln, s, n, done):
    dve.wait_ge(s["rs"], n)
    for b in range(GB):
        ins = nc.vector.tensor_scalar(out[:, b, :], src[:, b, :], ln["mv"][:, b, 0:1], ln["rs"][:, b:b + 1],
                                      ALU.subtract, ALU.mult)
    ins.then_inc(done, 1)


LN_SEMS = "st mv lv rs"



def attention(c, tag, cross, W, wsem, wcount, xsem=None):
    nc, X, PS = c.nc, c.X, c.PS
    H, DH, HG = 16, 8, 4
    KL = S2 if cross else P
    HU = 8
    UN = 2 * GB
    SCALE = DH ** -0.5
    s = c.sems(tag, "xs xTp xT qkv q k bd v vb s_ready mx d e ptp pt o_ready rc o oTp oT y y2 xw b5 cs cTp cT am padb amb " + LN_SEMS)
    ctx = ExitStack()
    sb = lambda n, sh, dt=F32: c.sb(tag + n, sh, dt, ctx)
    Xs = sb("Xs", [P, GB, D])
    xT = sb("xT", [D, T])
    qT = sb("qT", [D, T])
    kT = sb("kT", [D, GB, KL])
    BD = sb("BD", [D, HG, GB, KL])
    V = sb("V", [KL, GB, H, DH + 1])
    R = sb("R", [D, 4, T])
    DD = sb("DD", [P, 2, HU, KL])
    E = sb("E", [P, 2, HU, KL])
    PT = sb("PT", [KL, 2, HU, P])
    mx = sb("mx", [P, 2, HU])
    rc = sb("rc", [P, 2, HU])
    O = sb("O", [P, GB, D])
    oT = sb("oT", [D, T])
    Y = sb("Y", [P, GB, D])
    if cross:
        Cs = sb("Cs", [S2, GB, D])
        cT = sb("cT", [D, GB, S2])
        am8 = sb("am8", [P, S2])
        padr = sb("padr", [P, B, S2])
        am = sb("am", [P, 2, S2])
    ln = c.ln

    def bank(i, rows=P, n=512):
        return PS[0:rows, i, 0:n]

    def scores(gp):
        return PS[:, gp, 0:HG * KL].rearrange("p (j k) -> p j k", j=HG)

    def units(hf):
        return PS[:, 2 * hf:2 * hf + 2, 0:HG * KL].rearrange("p i (j k) -> p i j k", j=HG)

    def o_of(u):
        return PS[:, 6 + u % 2, 0:HU * (DH + 1)].rearrange("p (h d) -> p h d", h=HU)

    with nc.Block() as block:

        @block.sync
        def _(sp):
            if cross:
                sp.dma_start(Cs[:, :, :], c.dram["ctx"][:, 0:GB, :]).then_inc(s["cs"], 16)
                with sp.Fori(1, NG) as g:
                    sp.wait_ge(s["cTp"], g)
                    sp.dma_start(Cs[:, :, :], c.dram["ctx"][:, bass.ds(g * GB, GB), :]).then_inc(s["cs"], 16)

        @block.gpsimd
        def _(pool):
            nc.gpsimd.memset(V[:, :, :, DH], 1.0).then_inc(s["vb"], 1)
            if xsem is not None:
                pool.wait_ge(xsem, 16)
            nc.gpsimd.tensor_copy(Xs[:, :, :], X[:, 0:GB, :]).then_inc(s["xs"], 1)
            if cross:
                pool.wait_ge(wsem, wcount)
                nc.gpsimd.tensor_scalar(am8[:, :], W["amask"][:, :], float(np.sqrt(DH)), 0.0, ALU.mult, ALU.add).then_inc(s["am"], 1)
                nc.gpsimd.tensor_scalar(padr[:, :, :], W["pad"][:, :, :], -BIG, 0.0, ALU.mult, ALU.add).then_inc(s["padb"], 1)
            if xsem is not None:
                pool.wait_ge(xsem, 32)
            with pool.Fori(0, NG - 1) as g:
                if not cross:
                    pool.wait_ge(s["k"], g + 1)
                    for j in (2, 3):
                        nc.gpsimd.tensor_tensor(flat(BD[:, j]), flat(kT[:, :, :]), W["hmask"][:, j:j + 1].to_broadcast([D, GB * KL]), ALU.mult).then_inc(s["bd"], 1)
                pool.wait_ge(s["xTp"], g + 1)
                nc.gpsimd.tensor_copy(Xs[:, :, :], group(c, g + 1)).then_inc(s["xs"], 1)
                ln_rstd(pool, nc, ln, s, g + 1)
            if not cross:
                pool.wait_ge(s["k"], NG)
                for j in (2, 3):
                    nc.gpsimd.tensor_tensor(flat(BD[:, j]), flat(kT[:, :, :]), W["hmask"][:, j:j + 1].to_broadcast([D, GB * KL]), ALU.mult).then_inc(s["bd"], 1)
            ln_rstd(pool, nc, ln, s, NG)

        @block.scalar
        def _(act):
            act.wait_ge(wsem, wcount)
            with act.Fori(0, NG) as g:
                act.wait_ge(s["xTp"], g + 1)
                nc.scalar.copy(xT[:, :], bank(0)).then_inc(s["xT"], 1)
                if cross:
                    act.wait_ge(s["cTp"], g + 1)
                    nc.scalar.copy(flat(cT[:, :, :]), bank(1, D, GB * S2)).then_inc(s["cT"], 1)
                act.wait_ge(s["qkv"], g + 1)
                if cross:
                    nc.scalar.activation(qT[:, :], bank(2), ACT.Identity, bias=W["bq"][:, 0:1]).then_inc(s["q"], 1)
                    nc.scalar.activation(flat(kT[:, :, :]), bank(4, D, GB * S2), ACT.Identity, bias=W["bk"][:, 0:1]).then_inc(s["k"], 1)
                    act.wait_ge(s["k"], g + 1)
                    for j in range(HG):
                        nc.scalar.activation(flat(BD[:, j]), flat(kT[:, :, :]), ACT.Copy, scale=W["hmask"][:, j:j + 1]).then_inc(s["bd"], 1)
                else:
                    nc.scalar.copy(V[:, :, :, 0:DH], bank(7).rearrange("p (b h d) -> p b h d", b=GB, h=H)).then_inc(s["v"], 1)
                    act.wait_ge(s["k"], g + 1)
                    for j in (0, 1):
                        nc.scalar.activation(flat(BD[:, j]), flat(kT[:, :, :]), ACT.Copy, scale=W["hmask"][:, j:j + 1]).then_inc(s["bd"], 1)

                def exps(u):
                    act.wait_ge(s["d"], g * UN + (u + 1))
                    if u >= 2:
                        act.wait_ge(s["ptp"], g * UN + (u - 1))
                    nc.scalar.activation(E[:, u % 2], DD[:, u % 2], ACT.Exp, scale=SCALE).then_inc(s["e"], 1)

                exps(0)
                for u in range(UN):
                    if u + 1 < UN:
                        exps(u + 1)
                    act.wait_ge(s["ptp"], g * UN + (u + 1))
                    if u >= 2:
                        act.wait_ge(s["o_ready"], g * UN + (u - 1))
                    nc.scalar.copy(PT[:, u % 2], PS[0:KL, 4:6, :].rearrange("p i (h q) -> p (i h) q", q=P)).then_inc(s["pt"], 1)
                act.wait_ge(s["oTp"], g + 1)
                nc.scalar.copy(oT[:, :], bank(4)).then_inc(s["oT"], 1)

        @block.vector
        def _(dve):
            dve.wait_ge(wsem, wcount)
            dve.wait_ge(s["vb"], 1)
            if xsem is not None:
                dve.wait_ge(xsem, 32)
            if cross:
                dve.wait_ge(s["padb"], 1)
                dve.wait_ge(s["am"], 1)
            dve.sem_inc(s["b5"], 1)
            with dve.Fori(0, NG) as g:
                dve.wait_ge(s["qkv"], g + 1)
                if cross:
                    nc.vector.tensor_tensor(V[:, :, :, 0:DH], bank(7, S2).rearrange("p (b h d) -> p b h d", b=GB, h=H),
                                            W["bv"][0:S2, :].rearrange("p (o h d) -> p o h d", o=1, h=H).to_broadcast([S2, GB, H, DH]), ALU.add).then_inc(s["v"], 1)
                else:
                    cos = W["cos"][:, :].rearrange("p (o k) -> p o k", o=1).to_broadcast([D, GB, P])
                    sin = W["sin"][:, :].rearrange("p (o k) -> p o k", o=1).to_broadcast([D, GB, P])
                    for i, (out, done) in enumerate(((flat(kT[:, :, :]), "k"), (qT[:, :], "q"))):
                        t4 = lambda ap: ap.rearrange("p (b k) -> p b k", b=GB)
                        nc.vector.tensor_tensor(t4(R[:, 2 * i, :]), t4(bank(4 - 2 * i)), cos, ALU.mult)
                        nc.vector.tensor_tensor(t4(R[:, 2 * i + 1, :]), t4(bank(5 - 2 * i)), sin, ALU.mult).then_inc(s["rc"], 1)
                        dve.wait_ge(s["rc"], g * (UN + 2) + i + 1)
                        nc.vector.tensor_tensor(out, R[:, 2 * i, :], R[:, 2 * i + 1, :], ALU.add).then_inc(s[done], 1)

                def less_max(u):
                    hf, b = u % 2, u // 2
                    d = DD[:, u % 2].rearrange("p (i j) k -> p i j k", i=2)
                    m = mx[:, u % 2, :].rearrange("p (i j) -> p i j", i=2)
                    mb = mx[:, u % 2, :].rearrange("p (i j o) -> p i j o", i=2, o=1).to_broadcast([P, 2, HG, KL])
                    if cross and hf == 0:
                        nc.vector.tensor_tensor(am[:, b % 2, :], am8[:, :], padr[:, bass.ds(g * GB + b, 1), :].rearrange("p o k -> p (o k)"), ALU.add).then_inc(s["amb"], 1)
                        dve.wait_ge(s["amb"], g * GB + (b + 1))
                    dve.wait_ge(s["s_ready"], g * UN + (u + 1))
                    if u >= 2:
                        dve.wait_ge(s["e"], g * UN + (u - 1))
                    if cross:
                        amb = am[:, b % 2, :].rearrange("p (i j k) -> p i j k", i=1, j=1).to_broadcast([P, 2, HG, KL])
                        nc.vector.tensor_tensor(d, units(hf), amb, ALU.add).then_inc(s["y2"], 1)
                        dve.wait_ge(s["y2"], g * UN + (u + 1))
                        nc.vector.tensor_reduce(m, d, AX_X, ALU.max).then_inc(s["mx"], 1)
                        dve.wait_ge(s["mx"], g * UN + (u + 1))
                        nc.vector.tensor_tensor(d, d, mb, ALU.subtract).then_inc(s["d"], 1)
                    else:
                        nc.vector.tensor_reduce(m, units(hf), AX_X, ALU.max).then_inc(s["mx"], 1)
                        dve.wait_ge(s["mx"], g * UN + (u + 1))
                        nc.vector.tensor_tensor(d, units(hf), mb, ALU.subtract).then_inc(s["d"], 1)

                def normalise(u):
                    dve.wait_ge(s["o_ready"], g * UN + (u + 1))
                    nc.vector.reciprocal(rc[:, u % 2, :], o_of(u)[:, :, DH]).then_inc(s["rc"], 1)
                    dve.wait_ge(s["rc"], (g * UN + (u + 1)) if cross else (g * (UN + 2) + (u + 3)))
                    o = O[:, u // 2, (u % 2) * HU * DH:(u % 2 + 1) * HU * DH].rearrange("p (h d) -> p h d", h=HU)
                    nc.vector.tensor_tensor(o, o_of(u)[:, :, 0:DH], rc[:, u % 2, :].rearrange("p (h o) -> p h o", o=1).to_broadcast([P, HU, DH]),
                                            ALU.mult).then_inc(s["o"], 1)

                less_max(0)
                less_max(1)
                for u in range(UN):
                    if u + 2 < UN:
                        less_max(u + 2)
                    normalise(u)
                dve.wait_ge(s["y"], g + 1)
                nc.vector.tensor_tensor(flat(Y[:, :, :]), bank(5), flat(group(c, g)), ALU.add).then_inc(s["b5"], 1)
                dve.wait_ge(s["b5"], g + 2)
                if cross:
                    nc.vector.tensor_tensor(Y[:, :, :], Y[:, :, :], W["bo"][:, :].rearrange("p (o d) -> p o d", o=1).to_broadcast([P, GB, D]), ALU.add).then_inc(s["xw"], 1)
                    dve.wait_ge(s["xw"], g * 2 + 1)
                ln_stats(dve, nc, Y, ln, s, g + 1)
                ln_apply(dve, nc, group(c, g), Y, ln, s, g + 1, s["xw"])

        @block.tensor
        def _(pe):
            pe.wait_ge(wsem, wcount)
            with pe.Fori(0, NG) as g:
                pe.wait_ge(s["xs"], g + 1)
                for b in range(GB):
                    ins = nc.tensor.transpose(PS[:, 0, b * P:(b + 1) * P], Xs[:, b, :], c.identf[:, :])
                ins.then_inc(s["xTp"], 1)
                if cross:
                    pe.wait_ge(s["cs"], g * 16 + 16)
                    for b in range(GB):
                        ins = nc.tensor.transpose(PS[0:D, 1, b * S2:(b + 1) * S2], Cs[:, b, :], c.identf[0:S2, 0:S2])
                    ins.then_inc(s["cTp"], 1)
                pe.wait_ge(s["xT"], g + 1)
                pe.wait_ge(s["b5"], g + 1)
                nc.tensor.matmul(bank(2), W["wq"][:, :], xT[:, :], start=True, stop=True)
                if cross:
                    pe.wait_ge(s["cT"], g + 1)
                    nc.tensor.matmul(bank(4, D, GB * S2), W["wk"][:, :], flat(cT[:, :, :]), start=True, stop=True)
                    for b in range(GB):
                        ins = nc.tensor.matmul(PS[0:S2, 7, b * D:(b + 1) * D], cT[:, b, :], W["wv"][:, :], start=True, stop=True)
                else:
                    nc.tensor.matmul(bank(3), W["wqp"][:, :], xT[:, :], start=True, stop=True)
                    nc.tensor.matmul(bank(4), W["wk"][:, :], xT[:, :], start=True, stop=True)
                    nc.tensor.matmul(bank(5), W["wkp"][:, :], xT[:, :], start=True, stop=True)
                    for b in range(GB):
                        ins = nc.tensor.matmul(PS[:, 7, b * D:(b + 1) * D], xT[:, b * P:(b + 1) * P], W["wv"][:, :], start=True, stop=True)
                ins.then_inc(s["qkv"], 1)

                def score(u):
                    hf, b = u % 2, u // 2
                    if u == 0:
                        pe.wait_ge(s["q"], g + 1)
                        pe.wait_ge(s["bd"], g * HG + HG)
                    if u >= 2:
                        pe.wait_ge(s["d"], g * UN + (u - 1))
                    for gp in (2 * hf, 2 * hf + 1):
                        r = slice(32 * gp, 32 * gp + 32)
                        ins = nc.tensor.matmul(scores(gp), qT[r, b * P:(b + 1) * P], BD[r, :, b, :], start=True, stop=cross)
                    if not cross:
                        for gp in (2 * hf, 2 * hf + 1):
                            ins = nc.tensor.matmul(scores(gp), c.identb[:, :], W["cmask"][:, :].rearrange("p (o k) -> p o k", o=1).to_broadcast([P, HG, P]),
                                                   start=False, stop=True)
                    ins.then_inc(s["s_ready"], 1)

                score(0)
                score(1)
                for u in range(UN):
                    pe.wait_ge(s["e"], g * UN + (u + 1))
                    if u == 0:
                        pe.wait_ge(s["v"], g + 1)
                    else:
                        pe.wait_ge(s["pt"], g * UN + u)
                    for h in range(HU):
                        ins = nc.tensor.transpose(PS[0:KL, 4 + h // 4, (h % 4) * P:(h % 4 + 1) * P], E[:, u % 2, h, :], c.identf[:, :])
                    ins.then_inc(s["ptp"], 1)
                    if u + 2 < UN:
                        score(u + 2)
                    pe.wait_ge(s["pt"], g * UN + (u + 1))
                    if u >= 2:
                        pe.wait_ge(s["o"], g * UN + (u - 1))
                    for h in range(HU):
                        ins = nc.tensor.matmul(o_of(u)[:, h, :], PT[:, u % 2, h, :], V[:, u // 2, (u % 2) * HU + h, :], start=True, stop=True)
                    ins.then_inc(s["o_ready"], 1)
                pe.wait_ge(s["o"], g * UN + UN)
                for b in range(GB):
                    ins = nc.tensor.transpose(PS[:, 4, b * P:(b + 1) * P], O[:, b, :], c.identf[:, :])
                ins.then_inc(s["oTp"], 1)
                pe.wait_ge(s["oT"], g + 1)
                for b in range(GB):
                    ins = nc.tensor.matmul(PS[:, 5, b * D:(b + 1) * D], oT[:, b * P:(b + 1) * P], W["wo"][:, :], start=True, stop=True)
                ins.then_inc(s["y"], 1)
    c.end_phase(ctx)


PHASES = {}



def linear_attention_block(c, W, wsem, wcount, out):
    nc, X, PS = c.nc, c.X, c.PS
    H, DH, HID, BN = 8, 16, 128, 64
    W8 = 8
    W16 = P // W8
    KL = {1: P, 2: S2}
    step = ("yTp yT q kv vs mx d e sm rc pk pq a bda sT sTp bm tt o y2 n g b ")
    s = {k: c.sems(f"x{k}_", step + LN_SEMS) for k in (1, 2)}
    f = c.sems("xf_", "yTp yT e1 h1 d1 ex p1 rc si hs e2 h2 d2 y2 n g b " + LN_SEMS)
    o = c.sems("xo_", "y2 x " + LN_SEMS)
    ys, cs, cTp, cT = c.sems("x_", "ys cs cTp cT").values()
    ctx = ExitStack()
    sb = lambda n, sh, dt=F32: c.sb("x_" + n, sh, dt, ctx)
    Y = sb("Y", [P, GB, D])
    Y2 = sb("Y2", [P, GB, D])
    YT = sb("YT", [D, T])
    Cs = sb("Cs", [S2, GB, D])
    cTt = sb("cT", [D, GB, S2])
    DD = sb("DD", [P, 2, GB, D])
    E = sb("E", [P, 2, GB, D])
    mx = sb("mx", [P, 2, GB * H])
    sm = sb("sm", [P, 2, GB * H])
    V = sb("V", [P, GB, D])
    BDA = sb("BDA", [D, GB, D])
    sT = sb("sT", [D, T])
    TT = sb("TT", [P, 2, GB * 4, W16])
    h1 = sb("h1", [BN, T])
    hs = sb("hs", [HID, 3, T])
    h2 = sb("h2", [BN, T])
    ln = c.ln
    bank = lambda i, r=P: PS[0:r, i, :]
    bd = lambda ap: ap.rearrange("p (b d) -> p b d", b=GB)
    row = lambda ap: ap.rearrange("p (o d) -> p o d", o=1).to_broadcast([P, GB, D])

    with nc.Block() as block:

        @block.sync
        def _(sp):
            sp.dma_start(Cs[:, :, :], c.dram["ctx"][:, 0:GB, :]).then_inc(cs, 16)
            with sp.Fori(1, NG) as g:
                sp.wait_ge(cTp, g)
                sp.dma_start(Cs[:, :, :], c.dram["ctx"][:, bass.ds(g * GB, GB), :]).then_inc(cs, 16)

        @block.gpsimd
        def _(pool):
            nc.gpsimd.tensor_copy(Y[:, :, :], X[:, 0:GB, :]).then_inc(ys, 1)

            def keys(g, k):
                pool.wait_ge(s[k]["rc"], g)
                K = KL[k]
                nc.gpsimd.tensor_tensor(DD[0:K, 1].rearrange("p b (h d) -> p (b h) d", h=H), E[0:K, 1].rearrange("p b (h d) -> p (b h) d", h=H),
                                        sm[0:K, 1, :].rearrange("p (m o) -> p m o", o=1).to_broadcast([K, GB * H, DH]), ALU.mult).then_inc(s[k]["pk"], 1)

            with pool.Fori(0, NG - 1) as g:
                keys(g + 1, 1)
                ln_rstd(pool, nc, ln, s[1], g + 1)
                keys(g + 1, 2)
                for q in (s[2], f, o):
                    ln_rstd(pool, nc, ln, q, g + 1)
                pool.wait_ge(o["y2"], g + 1)
                nc.gpsimd.tensor_copy(Y[:, :, :], group(c, g + 1)).then_inc(ys, 1)
            keys(NG, 1)
            ln_rstd(pool, nc, ln, s[1], NG)
            keys(NG, 2)
            for q in (s[2], f, o):
                ln_rstd(pool, nc, ln, q, NG)

        @block.scalar
        def _(act):
            act.wait_ge(wsem, wcount)
            with act.Fori(0, NG) as g:
                act.wait_ge(cTp, g + 1)
                nc.scalar.copy(flat(cTt[:, :, :]), PS[:, 7, 0:GB * S2]).then_inc(cT, 1)
                for k in (1, 2):
                    q, K = s[k], KL[k]
                    act.wait_ge(q["yTp"], g + 1)
                    nc.scalar.copy(YT[:, :].rearrange("p (b w a) -> p b w a", b=GB, w=W8), bank(0).rearrange("p (b a w) -> p b w a", b=GB, w=W8)).then_inc(q["yT"], 1)
                    act.wait_ge(q["kv"], g + 1)
                    nc.scalar.copy(flat(V[0:K, :, :]), bank(3, K)).then_inc(q["vs"], 1)
                    act.wait_ge(q["d"], g * 2 + 2)
                    nc.scalar.activation(flat(E[:, 0]), flat(DD[:, 0]), ACT.Exp, scale=DH ** -0.25).then_inc(q["e"], 1)
                    nc.scalar.activation(flat(E[0:K, 1]), flat(DD[0:K, 1]), ACT.Exp, scale=DH ** -0.25).then_inc(q["e"], 1)
                    act.wait_ge(q["sTp"], g + 1)
                    nc.scalar.copy(sT[:, :], bank(5)).then_inc(q["sT"], 1)
                act.wait_ge(f["yTp"], g + 1)
                nc.scalar.copy(YT[:, :], bank(0)).then_inc(f["yT"], 1)
                act.wait_ge(f["e1"], g + 1)
                nc.scalar.copy(h1[:, :], bank(1, BN)).then_inc(f["h1"], 1)
                act.wait_ge(f["d1"], g + 1)
                nc.scalar.activation(hs[:, 0, :], bank(2), ACT.Exp, scale=-1.0).then_inc(f["ex"], 1)
                act.wait_ge(f["e2"], g + 1)
                nc.scalar.copy(h2[:, :], bank(3, BN)).then_inc(f["h2"], 1)

        @block.vector
        def _(dve):
            dve.wait_ge(wsem, wcount)
            with dve.Fori(0, NG) as g:

                def post_norm(q, gamma, beta):
                    dve.wait_ge(q["y2"], g + 1)
                    ln_stats(dve, nc, Y2, ln, q, g + 1)
                    ln_apply(dve, nc, Y2, Y2, ln, q, g + 1, q["n"])
                    dve.wait_ge(q["n"], g + 1)
                    nc.vector.tensor_tensor(Y2[:, :, :], Y2[:, :, :], row(gamma), ALU.mult).then_inc(q["g"], 1)
                    dve.wait_ge(q["g"], g + 1)
                    nc.vector.tensor_tensor(Y[:, :, :], Y2[:, :, :], row(beta), ALU.add).then_inc(q["b"], 1)

                for k in (1, 2):
                    q, K = s[k], KL[k]
                    dve.wait_ge(q["q"], g + 1)
                    dve.wait_ge(q["kv"], g + 1)
                    for i, n in ((0, P), (1, K)):
                        nc.vector.tensor_reduce(mx[0:n, i, :], PS[0:n, 1 + i, :].rearrange("p (m d) -> p m d", d=DH), AX_X, ALU.max).then_inc(q["mx"], 1)
                    for i, n in ((0, P), (1, K)):
                        dve.wait_ge(q["mx"], g * 2 + (i + 1))
                        nc.vector.tensor_tensor(DD[0:n, i].rearrange("p b (h d) -> p (b h) d", h=H), PS[0:n, 1 + i, :].rearrange("p (m d) -> p m d", d=DH),
                                                mx[0:n, i, :].rearrange("p (m o) -> p m o", o=1).to_broadcast([n, GB * H, DH]), ALU.subtract).then_inc(q["d"], 1)
                    for i, n in ((0, P), (1, K)):
                        dve.wait_ge(q["e"], g * 2 + (i + 1))
                        nc.vector.tensor_reduce(mx[0:n, i, :], E[0:n, i].rearrange("p b (h d) -> p (b h) d", h=H), AX_X, ALU.add).then_inc(q["sm"], 1)
                    dve.wait_ge(q["sm"], g * 2 + 2)
                    if K == P:
                        nc.vector.reciprocal(sm[:, :, :], mx[:, :, :]).then_inc(q["rc"], 1)
                        rcs = 1
                    else:
                        nc.vector.reciprocal(sm[:, 0, :], mx[:, 0, :])
                        nc.vector.reciprocal(sm[0:K, 1, :], mx[0:K, 1, :]).then_inc(q["rc"], 1)
                    dve.wait_ge(q["rc"], g + 1)
                    nc.vector.tensor_tensor(DD[:, 0].rearrange("p b (h d) -> p (b h) d", h=H), E[:, 0].rearrange("p b (h d) -> p (b h) d", h=H),
                                            sm[:, 0, :].rearrange("p (m o) -> p m o", o=1).to_broadcast([P, GB * H, DH]), ALU.mult).then_inc(q["pq"], 1)
                    dve.wait_ge(q["a"], g + 1)
                    nc.vector.tensor_tensor(BDA[:, :, :], bd(bank(4)), row(W["bdm"][:, :]), ALU.mult).then_inc(q["bda"], 1)
                    dve.wait_ge(q["bm"], g + 1)
                    nc.vector.transpose(TT[:, :, :, :].rearrange("p w m a -> p m w a"), bank(6).rearrange("p (m w a) -> p m w a", w=2, a=W16)).then_inc(q["tt"], 1)
                    dve.wait_ge(q["o"], g + 1)
                    nc.vector.tensor_tensor(flat(Y2[:, :, :]), bank(7), flat(Y[:, :, :]), ALU.add).then_inc(q["y2"], 1)
                    post_norm(q, W[f"g{k}"][:, :], W[f"b{k}"][:, :])
                dve.wait_ge(f["ex"], g + 1)
                nc.vector.tensor_scalar(hs[:, 1, :], hs[:, 0, :], 1.0, None, ALU.add).then_inc(f["p1"], 1)
                dve.wait_ge(f["p1"], g + 1)
                nc.vector.reciprocal(hs[:, 2, :], hs[:, 1, :]).then_inc(f["rc"], 1)
                dve.wait_ge(f["rc"], g + 1)
                nc.vector.tensor_tensor(hs[:, 0, :], bank(2), hs[:, 2, :], ALU.mult).then_inc(f["hs"], 1)
                dve.wait_ge(f["d2"], g + 1)
                nc.vector.tensor_tensor(flat(Y2[:, :, :]), bank(4), flat(Y[:, :, :]), ALU.add).then_inc(f["y2"], 1)
                post_norm(f, W["g3"][:, :], W["b3"][:, :])
                dve.wait_ge(f["b"], g + 1)
                nc.vector.tensor_tensor(Y2[:, :, :], Y[:, :, :], group(c, g), ALU.add).then_inc(o["y2"], 1)
                dve.wait_ge(o["y2"], g + 1)
                ln_stats(dve, nc, Y2, ln, o, g + 1)
                ln_apply(dve, nc, group(c, g), Y2, ln, o, g + 1, o["x"])

        @block.tensor
        def _(pe):
            pe.wait_ge(wsem, wcount)
            with pe.Fori(0, NG) as g:

                def transposes(i, src, done, rows=P):
                    for b in range(GB):
                        ins = nc.tensor.transpose(PS[:, i, b * rows:(b + 1) * rows], src[0:rows, b, :], c.identf[0:rows, 0:rows])
                    ins.then_inc(done, 1)

                pe.wait_ge(cs, 16 * g + 16)
                transposes(7, Cs, cTp, S2)
                for k in (1, 2):
                    q, K = s[k], KL[k]
                    if k == 1:
                        pe.wait_ge(ys, g + 1)
                    else:
                        pe.wait_ge(s[1]["b"], g + 1)
                    transposes(0, Y, q["yTp"])
                    pe.wait_ge(q["yT"], g + 1)
                    for b in range(GB):
                        tok = YT[:, b * P:(b + 1) * P]
                        ins = nc.tensor.matmul(PS[:, 1, b * D:(b + 1) * D], tok, W[f"wq{k}"][:, :], start=True, stop=k == 2)
                        if k == 1:
                            ins = nc.tensor.matmul(PS[:, 1, b * D:(b + 1) * D], c.identb[:, :], W["qmask"][:, :], start=False, stop=True)
                    ins.then_inc(q["q"], 1)
                    if k == 2:
                        pe.wait_ge(cT, g + 1)
                    for i in (0, 1):
                        for b in range(GB):
                            src = YT[:, b * P:(b + 1) * P] if k == 1 else cTt[:, b, :]
                            ins = nc.tensor.matmul(PS[0:K, 2 + i, b * D:(b + 1) * D], src, W[f"wkv{k}"][:, i, :], start=True, stop=True)
                    ins.then_inc(q["kv"], 1)
                    pe.wait_ge(q["pq"], g + 1)
                    transposes(5, DD[:, 0], q["sTp"])
                    pe.wait_ge(q["pk"], g + 1)
                    pe.wait_ge(q["vs"], g + 1)
                    for b in range(GB):
                        ins = nc.tensor.matmul(PS[:, 4, b * D:(b + 1) * D], DD[0:K, 1, b, :], V[0:K, b, :], start=True, stop=True)
                    ins.then_inc(q["a"], 1)
                    pe.wait_ge(q["sT"], g + 1)
                    pe.wait_ge(q["bda"], g + 1)
                    for b in range(GB):
                        ins = nc.tensor.matmul(PS[:, 6, b * D:(b + 1) * D], sT[:, b * P:(b + 1) * P], BDA[:, b, :], start=True, stop=True)
                    ins.then_inc(q["bm"], 1)
                    pe.wait_ge(q["tt"], g + 1)
                    if k == 1:
                        pe.wait_ge(cT, g + 1)
                    for b in range(GB):
                        for hl in (0, 1):
                            for w in (0, 1):
                                rows = TT[:, w, 4 * b:4 * b + 4, :].rearrange("p f a -> p (f a)")
                                ins = nc.tensor.matmul(PS[64 * hl:64 * hl + 64, 7, b * D:(b + 1) * D], rows, W[f"wo{k}"][:, hl, w, :],
                                                       start=(w == 0), stop=(w == 1))
                    ins.then_inc(q["o"], 1)
                pe.wait_ge(s[2]["b"], g + 1)
                transposes(0, Y, f["yTp"])
                pe.wait_ge(f["yT"], g + 1)
                nc.tensor.matmul(bank(1, BN), W["e1"][:, :], YT[:, :], start=True, stop=True).then_inc(f["e1"], 1)
                pe.wait_ge(f["h1"], g + 1)
                nc.tensor.matmul(bank(2), W["d1"][:, :], h1[:, :], start=True, stop=True).then_inc(f["d1"], 1)
                pe.wait_ge(f["hs"], g + 1)
                nc.tensor.matmul(bank(3, BN), W["e2"][:, :], hs[:, 0, :], start=True, stop=True).then_inc(f["e2"], 1)
                pe.wait_ge(f["h2"], g + 1)
                for b in range(GB):
                    ins = nc.tensor.matmul(PS[:, 4, b * D:(b + 1) * D], h2[:, b * P:(b + 1) * P], W["d2"][:, :], start=True, stop=True)
                ins.then_inc(f["d2"], 1)
    c.end_phase(ctx)


PHASES[2] = linear_attention_block



def top2(dve, nc, sel, t, s, base):
    n = sel.shape[1]
    idx = t["idx"][:, :].rearrange("p (o e) -> p o e", o=1).to_broadcast([P, n, 8])
    bc = lambda ap: ap.rearrange("p (n o) -> p n o", o=1).to_broadcast([P, n, 8])
    at = 0

    def step(ins):
        nonlocal at
        at += 1
        ins.then_inc(s["t"], 1)
        dve.wait_ge(s["t"], base + at)

    for src, oh in ((sel, t["oh1"]), (t["sel2"][:, :, :], t["oh2"])):
        step(nc.vector.tensor_reduce(t["m"][:, :], src, AX_X, ALU.max))
        step(nc.vector.tensor_tensor(t["key"][:, :, :], src, bc(t["m"][:, :]), ALU.is_equal))
        step(nc.vector.tensor_tensor(t["key"][:, :, :], t["key"][:, :, :], idx, ALU.mult))
        step(nc.vector.tensor_reduce(t["m"][:, :], t["key"][:, :, :], AX_X, ALU.max))
        step(nc.vector.tensor_tensor(oh[:, :, :], t["key"][:, :, :], bc(t["m"][:, :]), ALU.is_equal))
        if oh is t["oh1"]:
            step(nc.vector.scalar_tensor_tensor(t["sel2"][:, :, :], oh[:, :, :], -BIG, src, ALU.mult, ALU.add))


TOP2 = 11



def routed_ffn(c, W, wsem, wcount, out):
    nc, X, PS = c.nc, c.X, c.PS
    NE, SC = 8, 2
    s = c.sems("f_", "xs xTp xT lg h1 h3 ex p1 rc hs h t gate comb y0 acc0 ep ge ey acc x " + LN_SEMS)
    ctx = ExitStack()
    sb = lambda n, sh, dt=F32: c.sb("f_" + n, sh, dt, ctx)
    Xs = sb("Xs", [P, GB, D])
    xT = sb("xT", [D, T])
    eh = sb("eh", [P, SC, T])
    sg = sb("sg", [P, SC, T])
    hs = sb("hs", [P, SC, T])
    el = sb("el", [P, GB, NE])
    sc = sb("sc", [P, GB, NE])
    sel = sb("sel", [P, GB, NE])
    t = {"m": sb("m", [P, GB]), "idx": W["idx"]}
    for n in ("key", "sel2", "oh1", "oh2", "ss"):
        t[n] = sb(n, [P, GB, NE])
    den = sb("den", [P, 4, GB])
    comb = sb("comb", [P, GB, NE])
    G = sb("G", [P, 2, T])
    Acc = sb("Acc", [P, GB, D])
    ln = c.ln
    bank = lambda i, r=P: PS[0:r, i, :]
    bc = lambda ap: ap.rearrange("p (n o) -> p n o", o=1).to_broadcast([P, GB, NE])
    SR = TOP2 + 15

    with nc.Block() as block:

        @block.gpsimd
        def _(pool):
            nc.gpsimd.tensor_copy(Xs[:, :, :], X[:, 0:GB, :]).then_inc(s["xs"], 1)
            with pool.Fori(0, NG - 1) as g:
                pool.wait_ge(s["acc0"], g + 1)
                nc.gpsimd.tensor_copy(Xs[:, :, :], group(c, g + 1)).then_inc(s["xs"], 1)
                ln_rstd(pool, nc, ln, s, g + 1)
            ln_rstd(pool, nc, ln, s, NG)

        @block.scalar
        def _(act):
            act.wait_ge(wsem, wcount)
            with act.Fori(0, NG) as g:
                act.wait_ge(s["xTp"], g + 1)
                nc.scalar.copy(xT[:, :], bank(0)).then_inc(s["xT"], 1)
                act.wait_ge(s["lg"], g + 1)
                nc.scalar.activation(el[:, :, :].rearrange("p b e -> p (b e)"), PS[:, 1, 0:GB * NE], ACT.Exp, scale=-1.0).then_inc(s["ex"], 1)
                act.wait_ge(s["h1"], g + 1)
                nc.scalar.activation(eh[:, :, :], PS[:, 2:4, :], ACT.Exp, scale=-1.0).then_inc(s["ex"], 1)
                for e in range(NE):
                    act.wait_ge(s["ep"], g * NE + (e + 1))
                    if e >= 2:
                        act.wait_ge(s["ey"], g * NE + (e - 1))
                    nc.scalar.activation(G[:, e % 2, :], bank(6 + e % 2), ACT.Gelu).then_inc(s["ge"], 1)

        @block.vector
        def _(dve):
            dve.wait_ge(wsem, wcount)
            dve.sem_inc(s["acc"], 1)
            with dve.Fori(0, NG) as g:
                k = 0

                def step(ins):
                    nonlocal k
                    k += 1
                    ins.then_inc(s["t"], 1)
                    dve.wait_ge(s["t"], g * SR + k)

                dve.wait_ge(s["ex"], g * 2 + 1)
                step(nc.vector.tensor_scalar(el[:, :, :], el[:, :, :], 1.0, None, ALU.add))
                step(nc.vector.reciprocal(sc[:, :, :], el[:, :, :]))
                step(nc.vector.tensor_tensor(sel[:, :, :], sc[:, :, :], W["rb"][:, :].rearrange("p (o e) -> p o e", o=1).to_broadcast([P, GB, NE]), ALU.add))
                top2(dve, nc, sel[:, :, :], t, s, g * SR + k)
                k += TOP2
                step(nc.vector.tensor_tensor(t["key"][:, :, :], t["oh1"][:, :, :], t["oh2"][:, :, :], ALU.add))
                step(nc.vector.tensor_tensor(t["ss"][:, :, :], t["key"][:, :, :], sc[:, :, :], ALU.mult))
                step(nc.vector.tensor_reduce(den[:, 0, :], t["ss"][:, :, :], AX_X, ALU.add))
                step(nc.vector.tensor_scalar(den[:, 1, :], den[:, 0, :], 1e-9, None, ALU.add))
                step(nc.vector.reciprocal(den[:, 2, :], den[:, 1, :]))
                step(nc.vector.tensor_scalar(den[:, 3, :], den[:, 0, :], 1e-9, None, ALU.is_gt))
                step(nc.vector.tensor_tensor(den[:, 2, :], den[:, 2, :], den[:, 3, :], ALU.mult))
                step(nc.vector.tensor_scalar(den[:, 3, :], den[:, 3, :], -0.5, 0.5, ALU.mult, ALU.add))
                step(nc.vector.tensor_tensor(t["ss"][:, :, :], t["ss"][:, :, :], bc(den[:, 2, :]), ALU.mult))
                step(nc.vector.tensor_tensor(t["key"][:, :, :], t["key"][:, :, :], bc(den[:, 3, :]), ALU.mult))
                step(nc.vector.tensor_tensor(comb[:, :, :], t["ss"][:, :, :], t["key"][:, :, :], ALU.add))
                dve.wait_ge(s["ex"], g * 2 + 2)
                step(nc.vector.tensor_scalar(eh[:, :, :], eh[:, :, :], 1.0, None, ALU.add))
                assert k == SR
                nc.vector.reciprocal(sg[:, :, :], eh[:, :, :]).then_inc(s["rc"], 1)
                dve.wait_ge(s["rc"], g + 1)
                nc.vector.tensor_tensor(hs[:, :, :], PS[:, 2:4, :], sg[:, :, :], ALU.mult).then_inc(s["hs"], 1)
                dve.wait_ge(s["hs"], g + 1)
                dve.wait_ge(s["h3"], g + 1)
                nc.vector.tensor_tensor(hs[:, :, :], PS[:, 4:6, :], hs[:, :, :], ALU.mult).then_inc(s["h"], 1)
                dve.wait_ge(s["y0"], g + 1)
                nc.vector.tensor_tensor(flat(Acc[:, :, :]), bank(1), flat(Xs[:, :, :]), ALU.add).then_inc(s["acc0"], 1)
                dve.wait_ge(s["acc0"], g + 1)
                for e in range(NE):
                    dve.wait_ge(s["ey"], g * NE + (e + 1))
                    if e >= 1:
                        dve.wait_ge(s["acc"], g * NE + (e + 1))
                    for b in range(GB):
                        ins = nc.vector.scalar_tensor_tensor(Acc[:, b, :], PS[:, 4 + e % 2, b * D:(b + 1) * D], comb[:, b, e:e + 1], Acc[:, b, :], ALU.mult, ALU.add)
                    ins.then_inc(s["acc"], 1)
                dve.wait_ge(s["acc"], g * NE + (NE + 1))
                ln_stats(dve, nc, Acc, ln, s, g + 1)
                ln_apply(dve, nc, group(c, g), Acc, ln, s, g + 1, s["x"])

        @block.tensor
        def _(pe):
            pe.wait_ge(wsem, wcount)
            with pe.Fori(0, NG) as g:
                pe.wait_ge(s["xs"], g + 1)
                for b in range(GB):
                    ins = nc.tensor.transpose(PS[:, 0, b * P:(b + 1) * P], Xs[:, b, :], c.identf[:, :])
                ins.then_inc(s["xTp"], 1)
                pe.wait_ge(s["xT"], g + 1)
                for b in range(GB):
                    ins = nc.tensor.matmul(PS[:, 1, b * NE:(b + 1) * NE], xT[:, b * P:(b + 1) * P], W["rw"][:, :], start=True, stop=True)
                ins.then_inc(s["lg"], 1)
                for i in range(SC):
                    ins = nc.tensor.matmul(bank(2 + i), W["sw1"][:, i * P:(i + 1) * P], xT[:, :], start=True, stop=True)
                ins.then_inc(s["h1"], 1)

                def hidden(e):
                    if e >= 2:
                        pe.wait_ge(s["ge"], g * NE + (e - 1))
                    nc.tensor.matmul(bank(6 + e % 2), W["ew1"][:, e, :], xT[:, :], start=True, stop=True).then_inc(s["ep"], 1)

                pe.wait_ge(s["acc"], g * NE + 1)
                for i in range(SC):
                    ins = nc.tensor.matmul(bank(4 + i), W["sw3"][:, i * P:(i + 1) * P], xT[:, :], start=True, stop=True)
                ins.then_inc(s["h3"], 1)
                hidden(0)
                hidden(1)
                pe.wait_ge(s["h"], g + 1)
                for b in range(GB):
                    for i in range(SC):
                        ins = nc.tensor.matmul(PS[:, 1, b * D:(b + 1) * D], hs[:, i, b * P:(b + 1) * P], W["sw2"][:, i, :], start=(i == 0), stop=(i == SC - 1))
                ins.then_inc(s["y0"], 1)
                for e in range(NE):
                    pe.wait_ge(s["ge"], g * NE + (e + 1))
                    if e >= 2:
                        pe.wait_ge(s["acc"], g * NE + e)
                    for b in range(GB):
                        ins = nc.tensor.matmul(PS[:, 4 + e % 2, b * D:(b + 1) * D], G[:, e % 2, b * P:(b + 1) * P], W["ew2"][:, e, :], start=True, stop=True)
                    ins.then_inc(s["ey"], 1)
                    if e + 2 < NE:
                        hidden(e + 2)
    c.end_phase(ctx)


PHASES[3] = routed_ffn



def state_space(c, W, wsem, wcount, out):
    nc, X, PS = c.nc, c.X, c.PS
    CH, NS, DC = 2, 16, 4
    NI = NS * CH
    s = c.sems("m_", "A xp0 z0 n xnp xnT xp xpc z ez zr sz cv eu ur u dtp dtr bcp hi r sp dv ab e w l t cc m dt du "
                     "B C dA dBu h Cs hC yacc y1 y2 yp r2 x " + LN_SEMS + " ist imv ilv irs")
    si = {k: s["i" + k] for k in LN_SEMS.split()}
    ctx = ExitStack()
    sb = lambda n, sh, dt=F32: c.sb("m_" + n, sh, dt, ctx)
    Xn = sb("Xn", [P, GB, D])
    xnT = sb("xnT", [D, T])
    xp = sb("xp", [P, CH, GB, DC - 1 + P])
    U = sb("U", [P, CH, T])
    U2 = sb("U2", [P, CH, T])
    SZ = sb("SZ", [P, CH, T])
    E1 = sb("E1", [P, CH, T])
    E2 = sb("E2", [P, CH, T])
    dtr = sb("dtr", [8, T])
    hi = sb("hi", [96, T], BF16)
    R = sb("R", [96, T])
    DT = sb("DT", [P, CH, T])
    DU = sb("DU", [P, CH, T])
    A = sb("A", [P, CH, NS])
    dA = sb("dA", [P, 2, GB, P])
    dBu = sb("dBu", [P, 2, T])
    hst = sb("h", [P, 2, T])
    Cs = sb("Cs", [P, 2, T])
    hC = sb("hC", [P, 2, T])
    ln, iln = c.ln, {k: (c.sb("m_i" + k, v.shape, F32, ctx) if k not in ("half", "eps") else v) for k, v in c.ln.items()}
    bank = lambda i, r=P: PS[0:r, i, :]
    bl = lambda ap: ap.rearrange("p (b l) -> p b l", b=GB)

    with nc.Block() as block:

        @block.gpsimd
        def _(pool):
            nc.gpsimd.memset(xp[:, :, :, 0:DC - 1], 0.0).then_inc(s["xp0"], 1)
            nc.gpsimd.memset(dA[:, :, :, 0:1], 0.0).then_inc(s["z0"], 1)
            with pool.Fori(0, NG) as g:
                ln_rstd(pool, nc, iln, si, g + 1)
                pool.wait_ge(s["dt"], g + 1)
                pool.wait_ge(s["u"], g + 1)
                nc.gpsimd.tensor_tensor(DU[:, :, :], DT[:, :, :], U2[:, :, :], ALU.mult).then_inc(s["du"], 1)
                for i in range(NI):
                    n = i // CH
                    pool.wait_ge(s["h"], g * NI + (i + 1))
                    pool.wait_ge(s["Cs"], g * NS + (n + 1))
                    if i >= 2:
                        pool.wait_ge(s["yacc"], g * NI + (i - 1))
                    nc.gpsimd.tensor_tensor(hC[:, i % 2, :], hst[:, i % 2, :], Cs[:, n % 2, :], ALU.mult).then_inc(s["hC"], 1)
                ln_rstd(pool, nc, ln, s, g + 1)

        @block.scalar
        def _(act):
            act.wait_ge(wsem, wcount)
            act.wait_ge(s["xp0"], 1)
            act.wait_ge(s["z0"], 1)
            nc.scalar.activation(A[:, :, :], W["alog"][:, :, :], ACT.Exp).then_inc(s["A"], 1)
            act.wait_ge(s["A"], 1)
            nc.scalar.activation(A[:, :, :], A[:, :, :], ACT.Copy, scale=-1.0).then_inc(s["A"], 1)
            act.wait_ge(s["A"], 2)
            with act.Fori(0, NG) as g:
                act.wait_ge(s["xnp"], g + 1)
                nc.scalar.activation(xnT[:, :], bank(0), ACT.Identity, scale=W["lnw"][:, 0:1], bias=W["lnb"][:, 0:1]).then_inc(s["xnT"], 1)
                act.wait_ge(s["xpc"], g + 1)
                nc.scalar.copy(xp[:, :, :, DC - 1:DC - 1 + P], PS[:, 1:3, :].rearrange("p c (b l) -> p c b l", b=GB)).then_inc(s["xp"], 1)
                act.wait_ge(s["z"], g + 1)
                nc.scalar.activation(E1[:, :, :], PS[:, 3:5, :], ACT.Exp, scale=-1.0).then_inc(s["ez"], 1)
                act.wait_ge(s["cv"], g * 8 + 8)
                nc.scalar.activation(E2[:, :, :], U[:, :, :], ACT.Exp, scale=-1.0).then_inc(s["eu"], 1)
                act.wait_ge(s["dtp"], g + 1)
                nc.scalar.copy(dtr[:, :], bank(5, 8)).then_inc(s["dtr"], 1)
                act.wait_ge(s["bcp"], g + 1)
                nc.scalar.copy(hi[:, :], bank(6, 96)).then_inc(s["hi"], 1)
                act.wait_ge(s["dv"], g + 1)
                for ch, bk in ((0, 7), (1, 0)):
                    nc.scalar.activation(DT[:, ch, :], bank(bk), ACT.Identity, bias=W["bdt"][:, ch:ch + 1]).then_inc(s["ab"], 1)
                act.wait_ge(s["ab"], g * 3 + 2)
                nc.scalar.activation(U[:, :, :], DT[:, :, :], ACT.Abs).then_inc(s["ab"], 1)
                act.wait_ge(s["ab"], g * 3 + 3)
                nc.scalar.activation(E1[:, :, :], U[:, :, :], ACT.Exp, scale=-1.0).then_inc(s["e"], 1)
                act.wait_ge(s["w"], g + 1)
                nc.scalar.activation(U[:, :, :], E2[:, :, :], ACT.Ln).then_inc(s["l"], 1)
                act.wait_ge(s["dt"], g + 1)
                for i in range(NI):
                    n, ch = i // CH, i % CH
                    if i >= 2:
                        act.wait_ge(s["h"], g * NI + (i - 1))
                    nc.scalar.activation(dA[:, i % 2, :, 1:P], bl(DT[:, ch, :])[:, :, 1:P], ACT.Exp, scale=A[:, ch, n:n + 1]).then_inc(s["dA"], 1)
                    if ch == 0:
                        act.wait_ge(s["C"], g * NS + (n + 1))
                        if n >= 2:
                            act.wait_ge(s["hC"], g * NI + 2 * (n - 1))
                        nc.scalar.copy(Cs[:, n % 2, :], bank(3 + n % 2)).then_inc(s["Cs"], 1)

        @block.vector
        def _(dve):
            dve.wait_ge(wsem, wcount)
            dve.wait_ge(s["xp0"], 1)
            dve.wait_ge(s["z0"], 1)
            with dve.Fori(0, NG) as g:
                ln_stats(dve, nc, group(c, g), iln, si, g + 1)
                ln_apply(dve, nc, Xn, group(c, g), iln, si, g + 1, s["n"])
                dve.wait_ge(s["xp"], g + 1)
                for ch in range(CH):
                    nc.vector.tensor_scalar(bl(U[:, ch, :]), xp[:, ch, :, 0:P], W["cw"][:, ch, 0:1], W["cb"][:, ch:ch + 1], ALU.mult, ALU.add).then_inc(s["cv"], 1)
                for k in range(1, DC):
                    for ch in range(CH):
                        dve.wait_ge(s["cv"], g * 8 + (2 * k + ch - 1))
                        nc.vector.scalar_tensor_tensor(bl(U[:, ch, :]), xp[:, ch, :, k:k + P], W["cw"][:, ch, k:k + 1], bl(U[:, ch, :]), ALU.mult, ALU.add).then_inc(s["cv"], 1)
                dve.wait_ge(s["ez"], g + 1)
                nc.vector.tensor_scalar(E1[:, :, :], E1[:, :, :], 1.0, None, ALU.add).then_inc(s["zr"], 1)
                dve.wait_ge(s["zr"], g * 2 + 1)
                nc.vector.reciprocal(SZ[:, :, :], E1[:, :, :]).then_inc(s["zr"], 1)
                dve.wait_ge(s["zr"], g * 2 + 2)
                nc.vector.tensor_tensor(SZ[:, :, :], PS[:, 3:5, :], SZ[:, :, :], ALU.mult).then_inc(s["sz"], 1)
                dve.wait_ge(s["eu"], g + 1)
                nc.vector.tensor_scalar(E2[:, :, :], E2[:, :, :], 1.0, None, ALU.add).then_inc(s["ur"], 1)
                dve.wait_ge(s["ur"], g * 2 + 1)
                nc.vector.reciprocal(U2[:, :, :], E2[:, :, :]).then_inc(s["ur"], 1)
                dve.wait_ge(s["ur"], g * 2 + 2)
                nc.vector.tensor_tensor(U2[:, :, :], U[:, :, :], U2[:, :, :], ALU.mult).then_inc(s["u"], 1)
                dve.wait_ge(s["hi"], g + 1)
                nc.vector.tensor_tensor(R[:, :], bank(6, 96), hi[:, :], ALU.subtract).then_inc(s["r"], 1)
                dve.wait_ge(s["r"], g * 2 + 1)
                nc.vector.tensor_copy(hi[32:64, :], R[32:64, :]).then_inc(s["sp"], 1)
                nc.vector.tensor_copy(hi[64:96, :], R[64:96, :]).then_inc(s["sp"], 1)
                dve.wait_ge(s["sp"], g * 3 + 2)
                nc.vector.tensor_tensor(R[64:96, :], R[64:96, :], hi[64:96, :], ALU.subtract).then_inc(s["r"], 1)
                dve.wait_ge(s["r"], g * 2 + 2)
                nc.vector.tensor_copy(hi[64:96, :], R[64:96, :]).then_inc(s["sp"], 1)
                dve.wait_ge(s["e"], g + 1)
                nc.vector.tensor_scalar(E2[:, :, :], E1[:, :, :], 1.0, None, ALU.add).then_inc(s["w"], 1)
                dve.wait_ge(s["w"], g + 1)
                nc.vector.scalar_tensor_tensor(E1[:, :, :], E2[:, :, :], -1.0, E1[:, :, :], ALU.add, ALU.subtract).then_inc(s["t"], 1)
                dve.wait_ge(s["l"], g + 1)
                nc.vector.scalar_tensor_tensor(DT[:, :, :], DT[:, :, :], 0.0, U[:, :, :], ALU.max, ALU.add).then_inc(s["m"], 1)
                dve.wait_ge(s["m"], g + 1)
                dve.wait_ge(s["t"], g + 1)
                nc.vector.tensor_tensor(DT[:, :, :], DT[:, :, :], E1[:, :, :], ALU.subtract).then_inc(s["dt"], 1)
                dve.wait_ge(s["du"], g + 1)
                for i in range(NI):
                    n, ch = i // CH, i % CH
                    dve.wait_ge(s["B"], g * NS + (n + 1))
                    if i >= 2:
                        dve.wait_ge(s["h"], g * NI + (i - 1))
                    nc.vector.tensor_tensor(dBu[:, i % 2, :], bank(1 + n % 2), DU[:, ch, :], ALU.mult).then_inc(s["dBu"], 1)
                    dve.wait_ge(s["dBu"], g * NI + (i + 1))
                    dve.wait_ge(s["dA"], g * NI + (i + 1))
                    if i >= 2:
                        dve.wait_ge(s["hC"], g * NI + (i - 1))
                    nc.vector.tensor_tensor_scan(hst[:, i % 2, :], dA[:, i % 2].rearrange("p b l -> p (b l)"), dBu[:, i % 2, :], 0.0, ALU.mult, ALU.add).then_inc(s["h"], 1)
                for ch in range(CH):
                    if ch == 0:
                        dve.wait_ge(s["yacc"], g * NI + NI)
                    nc.vector.scalar_tensor_tensor(U[:, ch, :], U2[:, ch, :], W["dp"][:, ch:ch + 1], bank(5 + ch), ALU.mult, ALU.add).then_inc(s["y1"], 1)
                dve.wait_ge(s["y1"], g * 2 + 2)
                nc.vector.tensor_tensor(U[:, :, :], U[:, :, :], SZ[:, :, :], ALU.mult).then_inc(s["y2"], 1)
                dve.wait_ge(s["yp"], g + 1)
                nc.vector.scalar_tensor_tensor(flat(Xn[:, :, :]), flat(group(c, g)), 2.0, bank(7), ALU.mult, ALU.add).then_inc(s["r2"], 1)
                dve.wait_ge(s["r2"], g + 1)
                ln_stats(dve, nc, Xn, ln, s, g + 1)
                ln_apply(dve, nc, group(c, g), Xn, ln, s, g + 1, s["x"])

        @block.tensor
        def _(pe):
            pe.wait_ge(wsem, wcount)
            with pe.Fori(0, NG) as g:
                pe.wait_ge(s["n"], g + 1)
                for b in range(GB):
                    ins = nc.tensor.transpose(PS[:, 0, b * P:(b + 1) * P], Xn[:, b, :], c.identf[:, :])
                ins.then_inc(s["xnp"], 1)
                pe.wait_ge(s["xnT"], g + 1)
                for i in range(2 * CH):
                    ins = nc.tensor.matmul(bank(1 + i), W["win"][:, i * P:(i + 1) * P], xnT[:, :], start=True, stop=True)
                    if i == CH - 1:
                        ins.then_inc(s["xpc"], 1)
                ins.then_inc(s["z"], 1)
                pe.wait_ge(s["u"], g + 1)
                for ch in range(CH):
                    ins = nc.tensor.matmul(bank(5, 8), W["wxd"][:, ch, :], U2[:, ch, :], start=(ch == 0), stop=(ch == CH - 1))
                ins.then_inc(s["dtp"], 1)
                for ch in range(CH):
                    ins = nc.tensor.matmul(bank(6, 96), W["wxb"][:, ch, :], U2[:, ch, :], start=(ch == 0), stop=(ch == CH - 1))
                ins.then_inc(s["bcp"], 1)
                pe.wait_ge(s["dtr"], g + 1)
                for ch, bk in ((0, 7), (1, 0)):
                    ins = nc.tensor.matmul(bank(bk), W["wdt"][:, ch * P:(ch + 1) * P], dtr[:, :], start=True, stop=True)
                ins.then_inc(s["dv"], 1)
                pe.wait_ge(s["sp"], g * 3 + 3)
                pe.wait_ge(s["sz"], g + 1)

                def spread(n):
                    if n >= 2:
                        pe.wait_ge(s["dBu"], g * NI + 2 * (n - 1))
                        pe.wait_ge(s["Cs"], g * NS + (n - 1))
                    nc.tensor.matmul(bank(1 + n % 2), W["sel"][:, n, :], hi[:, :], start=True, stop=True).then_inc(s["B"], 1)
                    nc.tensor.matmul(bank(3 + n % 2), W["sel"][:, NS + n, :], hi[:, :], start=True, stop=True).then_inc(s["C"], 1)

                spread(0)
                spread(1)
                for i in range(NI):
                    n, ch = i // CH, i % CH
                    pe.wait_ge(s["hC"], g * NI + (i + 1))
                    nc.tensor.matmul(bank(5 + ch), c.identf[:, :], hC[:, i % 2, :], start=(n == 0), stop=(n == NS - 1)).then_inc(s["yacc"], 1)
                    if ch == CH - 1 and n + 2 < NS:
                        spread(n + 2)
                pe.wait_ge(s["y2"], g + 1)
                for b in range(GB):
                    for ch in range(CH):
                        ins = nc.tensor.matmul(PS[:, 7, b * D:(b + 1) * D], U[:, ch, b * P:(b + 1) * P], W["wout"][:, ch, :], start=(ch == 0), stop=(ch == CH - 1))
                ins.then_inc(s["yp"], 1)
    c.end_phase(ctx)


PHASES[4] = state_space


def context_attention(c, W, wsem, wcount, out):
    attention(c, "k_", True, W, wsem, wcount)


PHASES[5] = context_attention



def sinkhorn_ffn(c, W, wsem, wcount, out):
    nc, X, PS = c.nc, c.X, c.PS
    NE, FC, ITERS, SK_EPS = 8, 4, 20, 0.05
    ctx = ExitStack()
    sb = lambda n, sh, dt=F32: c.sb("e_" + n, sh, dt, ctx)
    s = c.sems("e_", "xs xTp xT lg la rm rd re rs rl ra cm cT gm dg gM cd ce cs ct cl ca t w "
                     "gp up sg h ey acc x st mv lv rs2 out")
    sl = {"st": s["st"], "mv": s["mv"], "lv": s["lv"], "rs": s["rs2"]}
    XT = sb("XT", [D, B, P])
    comb = sb("comb", [P, B, NE])
    ln = c.ln
    bank = lambda i, r=P: PS[0:r, i, :]

    rctx = ExitStack()
    rb = lambda n, sh, dt=F32: c.sb("e_" + n, sh, dt, rctx)
    Xs = rb("Xs", [P, 2, GB, D])
    LA = rb("LA", [P, B, NE])
    E = rb("E", [P, B, NE])
    rm = rb("rm", [P, B])
    rs = rb("rs", [P, B])
    rl = rb("rl", [P, B])
    cm = rb("cm", [P, NE])
    cs = rb("cs", [P, NE])
    cl = rb("cl", [P, NE])
    gm = rb("gm", [NE, 1])
    dg = rb("dg", [NE, NE])
    t = {"m": rm, "idx": W["idx"]}
    for n in ("key", "sel2", "oh1", "oh2"):
        t[n] = rb(n, [P, B, NE])
    rows = lambda ap: ap.rearrange("p (b o) -> p b o", o=1).to_broadcast([P, B, NE])
    cols = lambda ap: ap.rearrange("p (o e) -> p o e", o=1).to_broadcast([P, B, NE])
    byexp = lambda ap: ap.rearrange("p b e -> p e b")

    with nc.Block() as block:

        @block.gpsimd
        def _(pool):
            nc.gpsimd.tensor_copy(Xs[:, 0], X[:, 0:GB, :]).then_inc(s["xs"], 1)
            with pool.Fori(0, NG - 1) as g:
                pool.wait_ge(s["xTp"], g + 1)
                nc.gpsimd.tensor_copy(Xs[:, 0], group(c, g + 1)).then_inc(s["xs"], 1)

        @block.scalar
        def _(act):
            with act.Fori(0, NG) as g:
                act.wait_ge(s["xTp"], g + 1)
                nc.scalar.copy(XT[:, bass.ds(g * GB, GB), :].rearrange("p b d -> p (b d)"), bank(0)).then_inc(s["xT"], 1)
                nc.scalar.copy(Xs[:, 1].rearrange("p b d -> p (b d)"), bank(0)).then_inc(s["xT"], 1)
            with act.Fori(0, ITERS) as k:
                act.wait_ge(s["rd"], k + 1)
                nc.scalar.activation(E[:, :, :], LA[:, :, :], ACT.Exp).then_inc(s["re"], 1)
                act.wait_ge(s["rs"], k + 1)
                nc.scalar.activation(rl[:, :], rs[:, :], ACT.Ln).then_inc(s["rl"], 1)
                act.wait_ge(s["cd"], k + 1)
                nc.scalar.activation(E[:, :, :], LA[:, :, :], ACT.Exp).then_inc(s["ce"], 1)
                act.wait_ge(s["ct"], k + 1)
                nc.scalar.activation(cl[:, :], PS[:, 3, 0:NE], ACT.Ln).then_inc(s["cl"], 1)
            act.wait_ge(s["ca"], ITERS)
            nc.scalar.activation(E[:, :, :], LA[:, :, :], ACT.Exp).then_inc(s["re"], 1)

        @block.vector
        def _(dve):
            dve.wait_ge(wsem, wcount)
            with dve.Fori(0, NG) as g:
                dve.wait_ge(s["lg"], g + 1)
                nc.vector.tensor_scalar(LA[:, bass.ds(g * GB, GB), :], PS[:, 1, 0:GB * NE].rearrange("p (b e) -> p b e", b=GB), -1.0 / SK_EPS, None, ALU.mult).then_inc(s["la"], 1)
            dve.wait_ge(s["la"], NG)
            with dve.Fori(0, ITERS) as k:
                nc.vector.tensor_reduce(rm[:, :], LA[:, :, :], AX_X, ALU.max).then_inc(s["rm"], 1)
                dve.wait_ge(s["rm"], k + 1)
                nc.vector.tensor_tensor(LA[:, :, :], LA[:, :, :], rows(rm[:, :]), ALU.subtract).then_inc(s["rd"], 1)
                dve.wait_ge(s["re"], k + 1)
                nc.vector.tensor_reduce(rs[:, :], E[:, :, :], AX_X, ALU.add).then_inc(s["rs"], 1)
                dve.wait_ge(s["rl"], k + 1)
                nc.vector.tensor_tensor(LA[:, :, :], LA[:, :, :], rows(rl[:, :]), ALU.subtract).then_inc(s["ra"], 1)
                dve.wait_ge(s["ra"], k + 1)
                nc.vector.tensor_reduce(cm[:, :], byexp(LA[:, :, :]), AX_X, ALU.max).then_inc(s["cm"], 1)
                dve.wait_ge(s["cT"], k + 1)
                nc.vector.tensor_reduce(gm[:, :], PS[0:NE, 1, 0:P], AX_X, ALU.max).then_inc(s["gm"], 1)
                dve.wait_ge(s["gm"], k + 1)
                nc.vector.tensor_scalar(dg[:, :], c.identf[0:NE, 0:NE], gm[:, 0:1], None, ALU.mult).then_inc(s["dg"], 1)
                dve.wait_ge(s["gM"], k + 1)
                nc.vector.tensor_tensor(LA[:, :, :], LA[:, :, :], cols(PS[:, 2, 0:NE]), ALU.subtract).then_inc(s["cd"], 1)
                dve.wait_ge(s["ce"], k + 1)
                nc.vector.tensor_reduce(cs[:, :], byexp(E[:, :, :]), AX_X, ALU.add).then_inc(s["cs"], 1)
                dve.wait_ge(s["cl"], k + 1)
                nc.vector.tensor_tensor(LA[:, :, :], LA[:, :, :], cols(cl[:, :]), ALU.subtract).then_inc(s["ca"], 1)
                dve.wait_ge(s["ca"], k + 1)
            dve.wait_ge(s["re"], ITERS + 1)
            nc.vector.tensor_scalar(LA[:, :, :], E[:, :, :], float(np.finfo(np.float32).tiny), None, ALU.is_ge).then_inc(s["w"], 1)
            dve.wait_ge(s["w"], 1)
            nc.vector.tensor_tensor(E[:, :, :], E[:, :, :], LA[:, :, :], ALU.mult).then_inc(s["w"], 1)
            dve.wait_ge(s["w"], 2)
            top2(dve, nc, E[:, :, :], t, s, 0)
            for k, oh in enumerate((t["oh1"], t["oh2"])):
                nc.vector.tensor_tensor(oh[:, :, :], oh[:, :, :], E[:, :, k:k + 1].to_broadcast([P, B, NE]), ALU.mult).then_inc(s["w"], 1)
            dve.wait_ge(s["w"], 4)
            nc.vector.tensor_tensor(comb[:, :, :], t["oh1"][:, :, :], t["oh2"][:, :, :], ALU.add).then_inc(s["w"], 1)

        @block.tensor
        def _(pe):
            pe.wait_ge(wsem, wcount)
            with pe.Fori(0, NG) as g:
                pe.wait_ge(s["xs"], g + 1)
                for b in range(GB):
                    ins = nc.tensor.transpose(PS[:, 0, b * P:(b + 1) * P], Xs[:, 0, b, :], c.identf[:, :])
                ins.then_inc(s["xTp"], 1)
                pe.wait_ge(s["xT"], 2 * g + 2)
                for b in range(GB):
                    ins = nc.tensor.matmul(PS[:, 1, b * NE:(b + 1) * NE], Xs[:, 1, b, :], W["gw"][:, :], start=True, stop=True)
                ins.then_inc(s["lg"], 1)
                pe.wait_ge(s["la"], g + 1)
            with pe.Fori(0, ITERS) as k:
                pe.wait_ge(s["cm"], k + 1)
                nc.tensor.transpose(PS[0:NE, 1, 0:P], cm[:, :], c.identf[:, :]).then_inc(s["cT"], 1)
                pe.wait_ge(s["dg"], k + 1)
                nc.tensor.matmul(PS[:, 2, 0:NE], W["ones"][0:NE, :], dg[:, :], start=True, stop=True).then_inc(s["gM"], 1)
                pe.wait_ge(s["cs"], k + 1)
                nc.tensor.matmul(PS[:, 3, 0:NE], W["ones"][:, :], cs[:, :], start=True, stop=True).then_inc(s["ct"], 1)

    rctx.close()
    Sg = sb("Sg", [P, 2, T])
    Hh = sb("Hh", [P, 2, FC, T])
    Acc = sb("Acc", [P, GB, D])
    wg = sb("wg", [P, 2, GB, NE])
    NF = NE * FC
    with nc.Block() as block:

        @block.sync
        def _(sp):
            with sp.Fori(0, NG) as g:
                sp.wait_ge(s["x"], g + 1)
                sp.dma_start(out[bass.ds(g * GB, GB), :, :].rearrange("b p d -> p b d"), group(c, g)).then_inc(s["out"], 16)
            sp.wait_ge(s["out"], 16 * NG)

        @block.gpsimd
        def _(pool):
            with pool.Fori(0, NG) as g:
                ln_rstd(pool, nc, ln, sl, g + 1)

        @block.scalar
        def _(act):
            with act.Fori(0, NG) as g:
                for i in range(NF):
                    act.wait_ge(s["gp"], g * NF + (i + 1))
                    if i >= 2:
                        act.wait_ge(s["h"], g * NF + (i - 1))
                    nc.scalar.activation(Sg[:, i % 2, :], bank(i % 2), ACT.Silu).then_inc(s["sg"], 1)

        @block.vector
        def _(dve):
            dve.sem_inc(s["acc"], 1)
            with dve.Fori(0, NG) as g:

                def add(e):
                    dve.wait_ge(s["ey"], g * NE + (e + 1))
                    dve.wait_ge(s["acc"], g * NE + (e + 1))
                    for b in range(GB):
                        prior = Acc[:, b, :] if e else X[:, bass.ds(g * GB + b, 1), :].rearrange("p o d -> p (o d)")
                        ins = nc.vector.scalar_tensor_tensor(Acc[:, b, :], PS[:, 4 + e % 2, b * D:(b + 1) * D], wg[:, 0, b, e:e + 1], prior, ALU.mult, ALU.add)
                    ins.then_inc(s["acc"], 1)

                nc.vector.tensor_copy(wg[:, 0], comb[:, bass.ds(g * GB, GB), :]).then_inc(s["w"], 1)
                dve.wait_ge(s["w"], g + 6)
                for i in range(NF):
                    e = i // FC
                    dve.wait_ge(s["sg"], g * NF + (i + 1))
                    dve.wait_ge(s["up"], g * NF + (i + 1))
                    if e >= 2:
                        dve.wait_ge(s["ey"], g * NE + (e - 1))
                    nc.vector.tensor_tensor(Hh[:, e % 2, i % FC, :], bank(2 + i % 2), Sg[:, i % 2, :], ALU.mult).then_inc(s["h"], 1)
                    if i % FC == FC - 1 and e >= 1:
                        add(e - 1)
                add(NE - 1)
                dve.wait_ge(s["acc"], g * NE + (NE + 1))
                ln_stats(dve, nc, Acc, ln, sl, g + 1)
                ln_apply(dve, nc, group(c, g), Acc, ln, sl, g + 1, s["x"])

        @block.tensor
        def _(pe):
            with pe.Fori(0, NG) as g:
                rhs = XT[:, bass.ds(g * GB, GB), :].rearrange("p b d -> p (b d)")

                def down(e):
                    pe.wait_ge(s["h"], g * NF + FC * (e + 1))
                    pe.wait_ge(s["acc"], g * NE + (e if e >= 2 else 1))
                    for b in range(GB):
                        for f in range(FC):
                            ins = nc.tensor.matmul(PS[:, 4 + e % 2, b * D:(b + 1) * D], Hh[:, e % 2, f, b * P:(b + 1) * P], W["wd"][:, e, f, :], start=(f == 0), stop=(f == FC - 1))
                    ins.then_inc(s["ey"], 1)

                for i in range(NF):
                    e, f = i // FC, i % FC
                    if i >= 2:
                        pe.wait_ge(s["h"], g * NF + (i - 1))
                    nc.tensor.matmul(bank(i % 2), W["wg"][:, e, f * P:(f + 1) * P], rhs, start=True, stop=True).then_inc(s["gp"], 1)
                    nc.tensor.matmul(bank(2 + i % 2), W["wu"][:, e, f * P:(f + 1) * P], rhs, start=True, stop=True).then_inc(s["up"], 1)
                    if f == 0 and e >= 1:
                        down(e - 1)
                down(NE - 1)
    c.end_phase(ctx)


PHASES[6] = sinkhorn_ffn




def plan_weights():
    return {
        1: {"wq": [D, D], "wqp": [D, D], "wk": [D, D], "wkp": [D, D], "wv": [D, D], "wo": [D, D],
            "cos": [D, P], "sin": [D, P], "hmask": [D, 4], "cmask": ([P, P], BF16)},
        2: {"wq1": [D, D], "wkv1": [D, 2, D], "wo1": [D, 2, 2, D], "wq2": [D, D], "wkv2": [D, 2, D], "wo2": [D, 2, 2, D],
            "e1": [D, 64], "d1": [64, D], "e2": [D, 64], "d2": [64, D], "bdm": [D, D], "qmask": ([P, D], BF16),
            "g1": [P, D], "b1": [P, D], "g2": [P, D], "b2": [P, D], "g3": [P, D], "b3": [P, D]},
        3: {"rw": [D, 8], "rb": [P, 8], "idx": [P, 8], "sw1": [D, 256], "sw3": [D, 256], "sw2": [P, 2, D], "ew1": [D, 8, P], "ew2": [P, 8, D]},
        4: {"lnw": [D, 1], "lnb": [D, 1], "win": [D, 512], "cw": [P, 2, 4], "cb": [P, 2], "wxd": [P, 2, 8], "wxb": [P, 2, 96], "wdt": [8, 256],
            "bdt": [P, 2], "alog": [P, 2, 16], "dp": [P, 2], "wout": [P, 2, D], "sel": ([96, 32, P], BF16)},
        5: {"wq": [D, D], "wk": [D, D], "wv": [D, D], "wo": [D, D], "bq": [D, 1], "bk": [D, 1], "bv": [P, D], "bo": [P, D],
            "hmask": [D, 4], "amask": [P, S2], "pad": ([P, B, S2], mybir.dt.uint8)},
        6: {"gw": [D, 8], "idx": [P, 8], "ones": [P, P], "wg": [D, 8, 512], "wu": [D, 8, 512], "wd": [P, 8, 4, D]},
    }


def program(nc, dram, out):
    ctx = ExitStack()
    with ctx:
        c = Core(nc, ctx, dram)
        c.X = c.sb("X", [P, B, D])
        c.identf = c.sb("identf", [P, P])
        c.identb = c.sb("identb", [P, P], BF16)
        c.ln = {"st": c.sb("ln_st", [P, GB, 6]), "mv": c.sb("ln_mv", [P, GB, 2]), "lv": c.sb("ln_lv", [P, GB]),
                "rs": c.sb("ln_rs", [P, GB]), "half": c.sb("ln_half", [P, GB]), "eps": c.sb("ln_eps", [P, GB])}
        c.PS = ctx.enter_context(nc.psum_tensor("PS", [P, 8, 512], F32))
        plan = plan_weights()
        Ws, sem, count = {}, {}, {}
        for ph, ws in plan.items():
            Ws[ph] = {}
            for n, sh in ws.items():
                sh, dt = sh if isinstance(sh, tuple) else (sh, F32)
                Ws[ph][n] = c.sb(f"w{ph}_{n}", sh, dt)
            sem[ph] = c.sem(f"weights{ph}")
            count[ph] = 16 * len(ws)
        s_x = c.sem("x_loaded")
        s_set = c.sem("constants_set")
        count[1] += 32

        with nc.Block() as block:
            @block.sync
            def _(sp):
                sp.dma_start(c.X[:, 0:GB, :], dram["x"][:, 0:GB, :]).then_inc(s_x, 16)
                sp.dma_start(c.identf[:, :], dram["identf"]).then_inc(sem[1], 16)
                sp.dma_start(c.identb[:, :], dram["identb"]).then_inc(sem[1], 16)
                for ph, ws in Ws.items():
                    for n, t in ws.items():
                        full = tuple(slice(None) for _ in t.shape)
                        sp.dma_start(t[full], dram[f"w{ph}_{n}"]).then_inc(sem[ph], 16)
                    if ph == 1:
                        sp.wait_ge(s_x, 16)
                        sp.dma_start(c.X[:, GB:B, :], dram["x"][:, GB:B, :]).then_inc(s_x, 16)

            @block.vector
            def _(dve):
                nc.vector.memset(c.ln["eps"][:, :], EPS)
                nc.vector.memset(c.ln["half"][:, :], -0.5).then_inc(s_set, 1)

        attention(c, "a_", False, Ws[1], sem[1], count[1], s_x)
        if UPTO >= 2:
            for ph in range(2, UPTO + 1):
                PHASES[ph](c, Ws[ph], sem[ph], count[ph], out)
        if UPTO < 6:
            s_out = c.sem("stored")
            with nc.Block() as block:
                @block.sync
                def _(sp):
                    sp.dma_start(out.rearrange("b p d -> p b d"), c.X[:, :, :]).then_inc(s_out, 16)
                    sp.wait_ge(s_out, 16)


def layout(a):
    f = np.float32
    bf = mybir.dt.np(BF16)
    w = {}
    w["x"] = a["x"].transpose(1, 0, 2)
    w["ctx"] = a["ctx_1024"].transpose(1, 0, 2)
    w["identf"] = np.eye(P, dtype=f)
    w["identb"] = np.eye(P).astype(bf)
    swap = np.arange(D) ^ 1
    w["w1_wq"], w["w1_wk"], w["w1_wv"], w["w1_wo"] = (a["L0_attn_" + n].T for n in ("wq", "wk", "wv", "wo"))
    w["w1_wqp"], w["w1_wkp"] = a["L0_attn_wq"].T[:, swap], a["L0_attn_wk"].T[:, swap]
    freqs = (f(1.0) / f(10000.0) ** (np.arange(0, 8, 2, dtype=f) / f(8))).astype(f)
    ang = np.outer(np.arange(P, dtype=f), freqs).astype(f)
    i = (np.arange(D) % 8) // 2
    w["w1_cos"] = np.cos(ang)[:, i].T.astype(f)
    w["w1_sin"] = (np.sin(ang)[:, i].T * np.where(np.arange(D) % 2, 1, -1)[:, None]).astype(f)
    w["w1_hmask"] = (np.arange(D)[:, None] % 32 // 8 == np.arange(4)[None, :]).astype(f)
    w["w1_cmask"] = np.where(np.arange(P)[None, :] > np.arange(P)[:, None], -BIG, 0.0).astype(bf)
    order = np.array([4 * (i % 2) + i // 2 for i in range(8)])
    head = lambda m: m[order].transpose(1, 0, 2).reshape(D, D)
    for k in (1, 2):
        w[f"w2_wq{k}"] = head(a[f"L0_xattn_Wq{k}"])
        w[f"w2_wkv{k}"] = np.stack([head(a[f"L0_xattn_Wk{k}"]), head(a[f"L0_xattn_Wv{k}"])], 1)
        wo = a[f"L0_xattn_Wo{k}"].T.reshape(4, 2, 16, D)
        z = np.zeros((4, 2, 16, 2, 2, D), f)
        for hl in (0, 1):
            for t in (0, 1):
                z[:, hl, :, hl, t, :] = wo[:, t]
        w[f"w2_wo{k}"] = z.reshape(D, 2, 2, D)
    w["w2_e1"], w["w2_d1"], w["w2_e2"], w["w2_d2"] = (a["L0_xattn_" + n].T for n in ("E1", "D1", "E2", "D2"))
    w["w2_bdm"] = (np.arange(D)[:, None] // 16 == np.arange(D)[None, :] // 16).astype(f)
    tok = np.arange(P) % 16 * 8 + np.arange(P) // 16
    w["w2_qmask"] = np.where(np.arange(D)[None, :] % 16 > tok[:, None], -BIG, 0.0).astype(bf)
    for n in ("g1", "b1", "g2", "b2", "g3", "b3"):
        w["w2_" + n] = np.tile(a["L0_xattn_" + n], (P, 1))
    w["w3_rw"] = a["L0_ffn_router_w"].T
    w["w3_rb"] = np.tile(a["L0_ffn_router_bias"], (P, 1))
    w["w3_idx"] = np.tile(np.arange(8, 0, -1, dtype=f), (P, 1))
    w["w3_sw1"], w["w3_sw3"] = a["L0_ffn_sw1"], a["L0_ffn_sw3"]
    w["w3_sw2"] = a["L0_ffn_sw2"].reshape(2, P, D).transpose(1, 0, 2)
    w["w3_ew1"], w["w3_ew2"] = a["L0_ffn_ew1"].transpose(1, 0, 2), a["L0_ffn_ew2"].transpose(1, 0, 2)
    ch = lambda m: m.reshape(2, P, -1).transpose(1, 0, 2)
    w["w4_lnw"], w["w4_lnb"] = a["L1_attn_ln_w"][:, None], a["L1_attn_ln_b"][:, None]
    w["w4_win"], w["w4_wdt"] = a["L1_attn_W_in"], a["L1_attn_W_dt"]
    w["w4_cw"] = ch(a["L1_attn_conv_w"])
    w["w4_cb"], w["w4_bdt"], w["w4_dp"] = (ch(a["L1_attn_" + n])[:, :, 0] for n in ("conv_b", "b_dt", "D_param"))
    w["w4_alog"], w["w4_wout"] = ch(a["L1_attn_A_log"]), ch(a["L1_attn_W_out"])
    wx = ch(a["L1_attn_W_xproj"])
    w["w4_wxd"], w["w4_wxb"] = wx[:, :, 0:8], np.tile(wx[:, :, 8:40], (1, 1, 3))
    w["w4_sel"] = np.broadcast_to((np.arange(96)[:, None] % 32 == np.arange(32)[None, :])[:, :, None], (96, 32, P)).astype(bf)
    for n in ("q", "k", "v", "o"):
        w["w5_w" + n] = a["L1_xattn_W" + n].T
    w["w5_bq"], w["w5_bk"] = a["L1_xattn_bq"][:, None], a["L1_xattn_bk"][:, None]
    w["w5_bv"], w["w5_bo"] = np.tile(a["L1_xattn_bv"], (P, 1)), np.tile(a["L1_xattn_bo"], (P, 1))
    w["w5_hmask"], w["w5_amask"] = w["w1_hmask"], a["fside_SxS2_0"]
    w["w5_pad"] = np.broadcast_to(a["mask_BxS2_bf0"][None], (P, B, S2))
    w["w6_gw"], w["w6_idx"], w["w6_ones"] = a["L1_ffn_gate_W"].T, w["w3_idx"], np.ones((P, P), f)
    w["w6_wg"], w["w6_wu"] = (a["L1_ffn_W_" + n].transpose(2, 0, 1) for n in ("gate", "up"))
    w["w6_wd"] = a["L1_ffn_W_down"].transpose(2, 0, 1).reshape(4, P, 8, D).transpose(1, 2, 0, 3)
    return w


def kernel(**inputs):
    import concourse.bacc as _bacc
    from concourse.bass_utils import run_bass_kernel_spmd as _run

    a = {k: np.asarray(v) for k, v in inputs.items()}
    lay = layout(a)
    need = ["x", "ctx", "identf", "identb"] + [f"w{ph}_{n}" for ph, ws in plan_weights().items() for n in ws]
    nc = _bacc.Bacc("TRN2", target_bir_lowering=False, num_devices=1)
    arrays, dram = {}, {}
    for name in need:
        v = np.ascontiguousarray(lay[name])
        arrays[f"in_{name}"] = v
        dram[name] = nc.dram_tensor(f"in_{name}", v.shape, mybir.dt.from_np(v.dtype), kind="ExternalInput").ap()
    out = nc.dram_tensor("out_0_dram", (B, P, D), F32, kind="ExternalOutput").ap()
    program(nc, dram, out)
    r = _run(nc, [arrays], core_ids=[0])
    return r.results[0]["out_0_dram"]
```

```python
from contextlib import ExitStack

import concourse.bass as bass
import numpy as np
from concourse import mybir

F32 = mybir.dt.float32
BF16 = mybir.dt.bfloat16
ALU = mybir.AluOpType
ACT = mybir.ActivationFunctionType
AX_X = mybir.AxisListType.X

P = 128
B = 32
D = 128
GB = 4
NG = B // GB
T = GB * P
S2 = 77
EPS = 1e-5
BIG = 1e30
UPTO = 6


class Core:

    def __init__(self, nc, ctx, dram):
        self.nc, self.ctx, self.dram, self.phase = nc, ctx, dram, []

    def sb(self, name, shape, dt=F32, ctx=None):
        return (ctx or self.ctx).enter_context(self.nc.sbuf_tensor(name, shape, dt))

    def sem(self, name):
        return self.ctx.enter_context(self.nc.semaphore(name))

    def sems(self, prefix, names):
        made = {n: self.nc.alloc_semaphore(name=prefix + n) for n in names.split()}
        self.phase += made.values()
        return made

    def end_phase(self, ctx):
        ctx.close()
        self.nc.clear_and_free_semaphores(self.phase)
        self.nc.all_engine_barrier()
        self.phase = []


def group(c, g):
    return c.X[:, bass.ds(g * GB, GB), :]


def flat(ap):
    return ap.rearrange("p b d -> p (b d)")



def ln_stats(dve, nc, src, ln, s, n):
    for b in range(GB):
        ins = nc.vector.bn_stats(ln["st"][:, b, :], src[:, b, :])
    dve.drain()
    for b in range(GB):
        ins = nc.vector.bn_aggr(ln["mv"][:, b, :], ln["st"][:, b, :])
    ins.then_inc(s["mv"], 1)


def ln_rstd(pool, nc, ln, s, n):
    pool.wait_ge(s["mv"], n)
    nc.gpsimd.tensor_tensor(ln["lv"][:, :], ln["mv"][:, :, 1], ln["eps"][:, :], ALU.add).then_inc(s["lv"], 1)
    pool.wait_ge(s["lv"], n)
    nc.gpsimd.tensor_tensor(ln["rs"][:, :], ln["lv"][:, :], ln["half"][:, :], ALU.pow).then_inc(s["rs"], 1)


def ln_apply(dve, nc, out, src, ln, s, n, done):
    dve.wait_ge(s["rs"], n)
    for b in range(GB):
        ins = nc.vector.tensor_scalar(out[:, b, :], src[:, b, :], ln["mv"][:, b, 0:1], ln["rs"][:, b:b + 1],
                                      ALU.subtract, ALU.mult)
    ins.then_inc(done, 1)


LN_SEMS = "st mv lv rs"


def pipeline(eng, slot, shift, n, setup, early, prepare, step, end):
    def body(g, par, left):
        for i in range(shift, n):
            step(g, par, i, left)
            for name, stage in prepare.items():
                if left and slot[name] == i:
                    stage(g + 1, 1 - par)
            for name, stage in early.items():
                if left == 2 and slot[name] == i:
                    stage(g + 2, par)
        for i in range(shift):
            if left:
                step(g + 1, 1 - par, i, left)
            for name, stage in end.items():
                if slot[name] == i:
                    stage(g, par)

    setup()
    for stages, g in ((early, 0), (prepare, 0), (early, 1)):
        for stage in stages.values():
            stage(g, g)
    for i in range(shift):
        step(0, 0, i, 2)
    with eng.Fori(0, NG // 2 - 1) as k:
        body(k * 2, 0, 2)
        body(k * 2 + 1, 1, 2)
    body(NG - 2, 0, 1)
    body(NG - 1, 1, 0)



def attention(c, tag, cross, W, wsem, wcount, xsem=None, loads=None):
    nc, X, PS = c.nc, c.X, c.PS
    H, DH, HG = 16, 8, 4
    KL = S2 if cross else P
    HU = 8
    UN = 2 * GB
    VB = HG * (32 + DH)
    SCALE = DH ** -0.5
    s = c.sems(tag, "xs xTp xT kp rot qs q k bd vp v z s_ready mx ma d e sm rr ex rTp ptp pt o_ready oT yp yr y2 xw cs cTp cT am rc amg " + LN_SEMS)
    ctx = ExitStack()
    sb = lambda n, sh, dt=F32: c.sb(tag + n, sh, dt, ctx)
    Xs = sb("Xs", [P, GB, D])
    xT = sb("xT", [D, T])
    QM = sb("QM", [D, 2, 4, T])
    kT = sb("kT", [D, GB, KL])
    BD = sb("BD", [D, 2, HG, GB, KL])
    V = sb("V", [KL, 2, GB * 4, VB])
    R = sb("R", [D, 4, T])
    DD = sb("DD", [P, 2, HU, KL])
    E = sb("E", [P, 2, HU, KL])
    PT = sb("PT", [KL, 2, HU, P])
    mx = sb("mx", [P, 2, HU])
    sm = sb("sm", [P, GB * H])
    rr = sb("rr", [P, GB * H])
    rx = sb("rx", [P, GB, D])
    rT = sb("rT", [D, T])
    one = sb("one", [P, 1])
    oT = sb("oT", [D, T])
    Y = sb("Y", [P, GB, D])
    if not cross:
        qT = sb("qT", [D, T])
    if cross:
        bqm = sb("bqm", [D, 4])
        Cs = sb("Cs", [S2, GB, D])
        cT = sb("cT", [D, GB, S2])
        am8 = sb("am8", [P, S2])
        padr = sb("padr", [P, B, S2])
        am = sb("am", [P, 2, GB, S2])
    ln = c.ln

    AUX, OUT = 7, 6

    def bank(i, rows=P, n=512):
        return PS[0:rows, i, 0:n]

    def scores(gp):
        return PS[:, gp, 0:HG * KL].rearrange("p (j k) -> p j k", j=HG)

    def units(hf):
        return PS[:, 2 * hf:2 * hf + 2, 0:HG * KL].rearrange("p i (j k) -> p i j k", j=HG)

    def schedule(eng, prelude, body):
        prelude()
        with eng.Fori(0, NG // 2 - 1) as i:
            body(i * 2, 0, 2)
            body(i * 2 + 1, 1, 2)
        body(NG - 2, 0, 1)
        body(NG - 1, 1, 0)

    with nc.Block() as block:

        @block.sync
        def _(sp):
            if loads is not None:
                loads(sp)
            if cross:
                sp.dma_start(Cs[:, :, :], c.dram["ctx"][:, 0:GB, :]).then_inc(s["cs"], 16)
                with sp.Fori(1, NG) as g:
                    sp.wait_ge(s["cTp"], g)
                    sp.dma_start(Cs[:, :, :], c.dram["ctx"][:, bass.ds(g * GB, GB), :]).then_inc(s["cs"], 16)

        @block.gpsimd
        def _(pool):

            def rows(g):
                nc.gpsimd.tensor_copy(Xs[:, :, :], group(c, g)).then_inc(s["xs"], 1)

            def keys(g, par):
                if cross:
                    nc.gpsimd.tensor_tensor(am[:, par], padr[:, bass.ds(g * GB, GB), :], am8[:, :].rearrange("p (o k) -> p o k", o=1).to_broadcast([P, GB, S2]), ALU.add).then_inc(s["amg"], 1)
                    pool.wait_ge(s["k"], g + 1)
                else:
                    pool.wait_ge(s["rot"], g * 4 + 2)
                    nc.gpsimd.tensor_tensor(flat(kT[:, :, :]), R[:, 0, :], R[:, 1, :], ALU.add).then_inc(s["k"], 1)
                    pool.wait_ge(s["k"], g + 1)
                for j in range(HG):
                    nc.gpsimd.tensor_tensor(flat(BD[:, par, j]), flat(kT[:, :, :]), W["hmask"][:, j:j + 1].to_broadcast([D, GB * KL]), ALU.mult).then_inc(s["bd"], 1)
                if not cross:
                    pool.wait_ge(s["rot"], g * 4 + 4)
                    nc.gpsimd.tensor_tensor(qT[:, :], R[:, 2, :], R[:, 3, :], ALU.add).then_inc(s["qs"], 1)

            def prelude():
                nc.gpsimd.memset(one[:, :], 1.0).then_inc(s["z"], 1)
                nc.gpsimd.memset(V[:, :, :, :], 0.0).then_inc(s["z"], 1)
                pool.wait_ge(s["z"], 1)
                if xsem is not None:
                    pool.wait_ge(xsem[0], 16)
                rows(0)
                pool.wait_ge(wsem, wcount)
                if cross:
                    nc.gpsimd.tensor_scalar(am8[:, :], W["amask"][:, :], float(np.sqrt(DH)), 0.0, ALU.mult, ALU.add).then_inc(s["am"], 1)
                    nc.gpsimd.tensor_scalar(padr[:, :, :], W["pad"][:, :, :], -BIG, 0.0, ALU.mult, ALU.add).then_inc(s["am"], 1)
                    nc.gpsimd.tensor_tensor(bqm[:, :], W["gmask"][:, :], W["bq"][:, :].to_broadcast([D, 4]), ALU.mult).then_inc(s["am"], 1)
                    pool.wait_ge(s["am"], 2)
                keys(0, 0)
                if xsem is not None:
                    pool.wait_ge(xsem[1], 16)
                pool.wait_ge(s["xTp"], 1)
                rows(1)

            def body(g, par, left):
                if left:
                    if left == 2:
                        pool.wait_ge(s["xTp"], g + 2)
                        rows(g + 2)
                    keys(g + 1, 1 - par)
                pool.wait_ge(s["rr"], g + 1)
                nc.gpsimd.tensor_tensor(rx[:, :, :].rearrange("p b (h d) -> p (b h) d", d=DH), rr[:, :].rearrange("p (m o) -> p m o", o=1).to_broadcast([P, GB * H, DH]),
                                        one[:, :].rearrange("p (m o) -> p m o", o=1).to_broadcast([P, GB * H, DH]), ALU.mult).then_inc(s["ex"], 1)
                ln_rstd(pool, nc, ln, s, g + 1)

            schedule(pool, prelude, body)

        @block.scalar
        def _(act):

            def exps(g, u):
                act.wait_ge(s["d"], g * UN + u + 1)
                nc.scalar.activation(E[:, u % 2], DD[:, u % 2], ACT.Exp, scale=SCALE).then_inc(s["e"], 1)

            def x_transposed(g):
                act.wait_ge(s["xTp"], g + 1)
                nc.scalar.copy(xT[:, :], bank(AUX)).then_inc(s["xT"], 1)

            def values(g, par):
                act.wait_ge(s["vp"], g + 1)
                nc.scalar.copy(V[:, par].rearrange("p m (j c) -> p m j c", c=32 + DH)[:, :, :, 0:DH], bank(AUX).rearrange("p (m j d) -> p m j d", j=HG, d=DH)).then_inc(s["v"], 1)

            def context(g):
                act.wait_ge(s["cTp"], g + 1)
                nc.scalar.copy(flat(cT[:, :, :]), bank(AUX, D, GB * S2)).then_inc(s["cT"], 1)

            def keys(g):
                act.wait_ge(s["kp"], g * 2 + 1)
                act.wait_ge(s["bd"], g * HG)
                nc.scalar.activation(flat(kT[:, :, :]), bank(AUX, D, GB * S2), ACT.Identity, bias=W["bk"][:, 0:1]).then_inc(s["k"], 1)

            def queries(g, par):
                if cross:
                    act.wait_ge(s["kp"], g * 2 + 2)
                else:
                    act.wait_ge(s["qs"], g + 1)
                for gp in range(4):
                    if cross:
                        ins = nc.scalar.activation(QM[:, par, gp, :], bank(AUX), ACT.Identity, scale=W["gmask"][:, gp:gp + 1], bias=bqm[:, gp:gp + 1])
                    else:
                        ins = nc.scalar.activation(QM[:, par, gp, :], qT[:, :], ACT.Copy, scale=W["gmask"][:, gp:gp + 1])
                ins.then_inc(s["q"], 1)

            def first_keys():
                act.wait_ge(s["kp"], 1)
                nc.scalar.activation(flat(kT[:, :, :]), bank(AUX, D, GB * S2), ACT.Identity, bias=W["bk"][:, 0:1]).then_inc(s["k"], 1)

            def slot(g, u, left):
                act.wait_ge(s["ptp"], g * UN + u + 1)
                act.wait_ge(s["o_ready"], g * UN + (u if u else 0))
                nc.scalar.copy(PT[:, u % 2], PS[0:KL, 4:6, :].rearrange("p i (h q) -> p (i h) q", q=P)).then_inc(s["pt"], 1)
                if u + 1 < UN or left:
                    act.wait_ge(s["sm"], g * UN + u)
                    exps(g + (u + 1) // UN, (u + 1) % UN)

            def prelude():
                act.wait_ge(wsem, wcount)
                act.sem_inc(s["o_ready"], 1)
                act.wait_ge(s["z"], 2)
                x_transposed(0)
                if cross:
                    context(0)
                    act.wait_ge(s["am"], 3)
                    first_keys()
                    queries(0, 0)
                else:
                    values(0, 0)
                    queries(0, 0)
                exps(0, 0)
                act.wait_ge(s["ptp"], 1)
                nc.scalar.copy(PT[:, 0], PS[0:KL, 4:6, :].rearrange("p i (h q) -> p (i h) q", q=P)).then_inc(s["pt"], 1)
                exps(0, 1)
                x_transposed(1)

            def body(g, par, left):
                for u in range(1, UN):
                    slot(g, u, left)
                    if left:
                        if cross:
                            if u == 1:
                                context(g + 1)
                            if u == 2:
                                keys(g + 1)
                            if u == 3:
                                queries(g + 1, 1 - par)
                        elif u == 5:
                            queries(g + 1, 1 - par)
                        elif u == 6:
                            values(g + 1, 1 - par)
                if left:
                    slot(g + 1, 0, left)
                if left == 2:
                    x_transposed(g + 2)

            schedule(act, prelude, body)

        @block.vector
        def _(dve):

            def less_max(g, par, u):
                hf, b = u % 2, u // 2
                at = g * UN + u + 1
                d = DD[:, u % 2].rearrange("p (i j) k -> p i j k", i=2)
                m = mx[:, u % 2, :].rearrange("p (i j) -> p i j", i=2)
                mb = mx[:, u % 2, :].rearrange("p (i j o) -> p i j o", i=2, o=1).to_broadcast([P, 2, HG, KL])
                dve.wait_ge(s["s_ready"], at)
                if not (isinstance(g, int) and g == 0 and u < 2):
                    dve.wait_ge(s["e"], at - 2)
                if cross:
                    if u == 0:
                        dve.wait_ge(s["amg"], g + 1)
                    amb = am[:, par, b, :].rearrange("p (i j k) -> p i j k", i=1, j=1).to_broadcast([P, 2, HG, KL])
                    nc.vector.tensor_tensor(d, units(hf), amb, ALU.add).then_inc(s["ma"], 1)
                    dve.wait_ge(s["ma"], at)
                    nc.vector.tensor_reduce(m, d, AX_X, ALU.max).then_inc(s["mx"], 1)
                    dve.wait_ge(s["mx"], at)
                    nc.vector.tensor_tensor(d, d, mb, ALU.subtract).then_inc(s["d"], 1)
                else:
                    nc.vector.tensor_reduce(m, units(hf), AX_X, ALU.max).then_inc(s["mx"], 1)
                    dve.wait_ge(s["mx"], at)
                    nc.vector.tensor_tensor(d, units(hf), mb, ALU.subtract).then_inc(s["d"], 1)

            def sums(g, u):
                dve.wait_ge(s["e"], g * UN + u + 1)
                nc.vector.tensor_reduce(sm[:, u * HU:(u + 1) * HU], E[:, u % 2], AX_X, ALU.add).then_inc(s["sm"], 1)

            def rotate(g, i):
                f4 = W["cos" if i % 2 == 0 else "sin"][:, :].rearrange("p (o k) -> p o k", o=1).to_broadcast([D, GB, P])
                t4 = lambda ap: ap.rearrange("p (b k) -> p b k", b=GB)
                dve.wait_ge(s["kp"], g * 4 + i + 1)
                nc.vector.tensor_tensor(t4(R[:, i, :]), t4(bank(AUX)), f4, ALU.mult).then_inc(s["rot"], 1)

            def values(g, par):
                dve.wait_ge(s["vp"], g + 1)
                for b in range(GB):
                    ins = nc.vector.tensor_tensor(V[:, par, 4 * b:4 * b + 4].rearrange("p m (j c) -> p m j c", c=32 + DH)[:, :, :, 0:DH],
                                                  PS[0:KL, AUX, b * D:(b + 1) * D].rearrange("p (m j d) -> p m j d", j=HG, d=DH),
                                                  W["bv"][0:KL, :].rearrange("p (m j d) -> p m j d", j=HG, d=DH), ALU.add)
                ins.then_inc(s["v"], 1)

            def prelude():
                dve.wait_ge(wsem, wcount)
                dve.wait_ge(s["z"], 2)
                if xsem is not None:
                    dve.wait_ge(xsem[0], 16)
                    dve.wait_ge(xsem[1], 16)
                if cross:
                    values(0, 0)
                else:
                    for i in range(4):
                        rotate(0, i)
                less_max(0, 0, 0)
                less_max(0, 0, 1)
                sums(0, 0)
                sums(0, 1)
                less_max(0, 0, 2)
                if not cross:
                    rotate(1, 0)

            def body(g, par, left):
                for u in range(2, UN):
                    sums(g, u)
                    if u == UN - 1:
                        dve.wait_ge(s["sm"], g * UN + UN)
                        nc.vector.reciprocal(rr[:, :], sm[:, :]).then_inc(s["rr"], 1)
                    if u + 1 < UN:
                        less_max(g, par, u + 1)
                    elif left:
                        less_max(g + 1, 1 - par, 0)
                    if left:
                        if cross:
                            if u == 4:
                                values(g + 1, 1 - par)
                        elif u <= 4:
                            rotate(g + 1, u - 1)
                dve.wait_ge(s["rTp"], g + 1)
                nc.vector.tensor_copy(rT[:, :], bank(AUX)).then_inc(s["rc"], 1)
                dve.wait_ge(s["rc"], g + 1)
                dve.wait_ge(s["o_ready"], g * UN + UN + 1)
                nc.vector.tensor_tensor(oT[:, :], bank(OUT), rT[:, :], ALU.mult).then_inc(s["oT"], 1)
                if left:
                    less_max(g + 1, 1 - par, 1)
                    dve.wait_ge(s["rr"], g + 1)
                    sums(g + 1, 0)
                dve.wait_ge(s["yp"], g + 1)
                nc.vector.tensor_tensor(flat(Y[:, :, :]), bank(AUX), flat(group(c, g)), ALU.add).then_inc(s["yr"], 1)
                dve.wait_ge(s["yr"], g + 1)
                if cross:
                    nc.vector.tensor_tensor(Y[:, :, :], Y[:, :, :], W["bo"][:, :].rearrange("p (o d) -> p o d", o=1).to_broadcast([P, GB, D]), ALU.add).then_inc(s["y2"], 1)
                    dve.wait_ge(s["y2"], g + 1)
                ln_stats(dve, nc, Y, ln, s, g + 1)
                if left:
                    sums(g + 1, 1)
                    less_max(g + 1, 1 - par, 2)
                    if left == 2 and not cross:
                        rotate(g + 2, 0)
                ln_apply(dve, nc, group(c, g), Y, ln, s, g + 1, s["xw"])

            schedule(dve, prelude, body)

        @block.tensor
        def _(pe):

            def transpose_x(g):
                pe.wait_ge(s["xs"], g + 1)
                for b in range(GB):
                    ins = nc.tensor.transpose(PS[:, AUX, b * P:(b + 1) * P], Xs[:, b, :], c.identf[:, :])
                ins.then_inc(s["xTp"], 1)

            def transpose_context(g):
                pe.wait_ge(s["cs"], g * 16 + 16)
                pe.wait_ge(s["xT"], g + 1)
                for b in range(GB):
                    ins = nc.tensor.transpose(PS[0:D, AUX, b * S2:(b + 1) * S2], Cs[:, b, :], c.identf[0:S2, 0:S2])
                ins.then_inc(s["cTp"], 1)

            def project(g, i):
                if cross:
                    if i == 0:
                        pe.wait_ge(s["cT"], g + 1)
                        nc.tensor.matmul(bank(AUX, D, GB * S2), W["wk"][:, :], flat(cT[:, :, :]), start=True, stop=True).then_inc(s["kp"], 1)
                    else:
                        pe.wait_ge(s["k"], g + 1)
                        nc.tensor.matmul(bank(AUX), W["wq"][:, :], xT[:, :], start=True, stop=True).then_inc(s["kp"], 1)
                else:
                    if i == 0:
                        pe.wait_ge(s["xT"], g + 1)
                    else:
                        pe.wait_ge(s["rot"], g * 4 + i)
                    nc.tensor.matmul(bank(AUX), W[("wk", "wkp", "wq", "wqp")[i]][:, :], xT[:, :], start=True, stop=True).then_inc(s["kp"], 1)

            def project_values(g):
                if cross:
                    pe.wait_ge(s["q"], g + 1)
                else:
                    pe.wait_ge(s["rot"], g * 4 + 4)
                for b in range(GB):
                    src = cT[:, b, :] if cross else xT[:, b * P:(b + 1) * P]
                    ins = nc.tensor.matmul(PS[0:KL, AUX, b * D:(b + 1) * D], src, W["wv"][:, :], start=True, stop=True)
                ins.then_inc(s["vp"], 1)

            def score(g, par, u):
                hf, b = u % 2, u // 2
                if u == 0:
                    pe.wait_ge(s["q"], g + 1)
                    pe.wait_ge(s["bd"], g * HG + HG)
                if not (isinstance(g, int) and g == 0 and u < 2):
                    pe.wait_ge(s["d"], g * UN + u - 1)
                for gp in (2 * hf, 2 * hf + 1):
                    ins = nc.tensor.matmul(scores(gp), QM[:, par, gp, b * P:(b + 1) * P], BD[:, par, :, b, :], start=True, stop=cross)
                if not cross:
                    for gp in (2 * hf, 2 * hf + 1):
                        ins = nc.tensor.matmul(scores(gp), c.identb[:, :], W["cmask"][:, :].rearrange("p (o k) -> p o k", o=1).to_broadcast([P, HG, P]),
                                               start=False, stop=True)
                ins.then_inc(s["s_ready"], 1)

            def transpose_p(g, u):
                pe.wait_ge(s["e"], g * UN + u + 1)
                for h in range(HU):
                    ins = nc.tensor.transpose(PS[0:KL, 4 + h // 4, (h % 4) * P:(h % 4 + 1) * P], E[:, u % 2, h, :], c.identf[:, :])
                ins.then_inc(s["ptp"], 1)

            def outputs(g, par, u):
                hf, b = u % 2, u // 2
                pe.wait_ge(s["pt"], g * UN + u + 1)
                if u == 0:
                    pe.wait_ge(s["v"], g + 1)
                for h in range(HU):
                    gp, j = 2 * hf + h // HG, h % HG
                    ins = nc.tensor.matmul(PS[32 * gp:32 * gp + 32, OUT, b * P:(b + 1) * P], V[:, par, b * 4 + gp, 32 * j:32 * j + 32], PT[:, u % 2, h, :],
                                           start=(j == 0), stop=(j == HG - 1))
                ins.then_inc(s["o_ready"], 1)

            def prelude():
                pe.wait_ge(wsem, wcount)
                transpose_x(0)
                if cross:
                    transpose_context(0)
                for i in range(2 if cross else 4):
                    project(0, i)
                project_values(0)
                score(0, 0, 0)
                score(0, 0, 1)
                transpose_p(0, 0)
                score(0, 0, 2)
                outputs(0, 0, 0)
                transpose_x(1)

            def body(g, par, left):
                for u in range(1, UN):
                    pe.wait_ge(s["pt"], g * UN + u)
                    transpose_p(g, u)
                    if u + 2 < UN:
                        score(g, par, u + 2)
                    elif left:
                        score(g + 1, 1 - par, u + 2 - UN)
                    if left:
                        if cross:
                            if u == 1:
                                transpose_context(g + 1)
                            if u in (2, 3):
                                project(g + 1, u - 2)
                            if u == 4:
                                project_values(g + 1)
                        elif u <= 4:
                            project(g + 1, u - 1)
                        elif u == 5:
                            project_values(g + 1)
                    if u == UN - 1:
                        pe.wait_ge(s["ex"], g + 1)
                        if left:
                            pe.wait_ge(s["v"], g + 2)
                        for b in range(GB):
                            ins = nc.tensor.transpose(PS[:, AUX, b * P:(b + 1) * P], rx[:, b, :], c.identf[:, :])
                        ins.then_inc(s["rTp"], 1)
                    outputs(g, par, u)
                if left:
                    pe.wait_ge(s["pt"], g * UN + UN)
                    transpose_p(g + 1, 0)
                    score(g + 1, 1 - par, 2)
                pe.wait_ge(s["oT"], g + 1)
                for b in range(GB):
                    ins = nc.tensor.matmul(PS[:, AUX, b * D:(b + 1) * D], oT[:, b * P:(b + 1) * P], W["wo"][:, :], start=True, stop=True)
                ins.then_inc(s["yp"], 1)
                if left:
                    outputs(g + 1, 1 - par, 0)
                if left == 2:
                    pe.wait_ge(s["yr"], g + 1)
                    transpose_x(g + 2)

            schedule(pe, prelude, body)
    c.end_phase(ctx)


PHASES = {}



def linear_attention_block(c, W, wsem, wcount, out):
    nc, X, PS = c.nc, c.X, c.PS
    H, DH, HID, BN = 8, 16, 128, 64
    W8 = 8
    W16 = P // W8
    KL = {1: P, 2: S2}
    LANES = 2
    NI = NG // LANES
    ctx = ExitStack()
    row = lambda ap: ap.rearrange("p (o d) -> p o d", o=1).to_broadcast([P, GB, D])
    bd = lambda ap: ap.rearrange("p (b d) -> p b d", b=GB)
    heads = lambda ap: ap.rearrange("p b (h d) -> p (b h) d", h=H)
    each = lambda ap, n: ap.rearrange("p (m o) -> p m o", o=1).to_broadcast([n, GB * H, DH])

    class Lane:

        def __init__(self, i):
            sb = lambda n, sh, dt=F32: c.sb(f"x{i}_" + n, sh, dt, ctx)
            self.i = i
            self.s = c.sems(f"x{i}_", "ys cs cTp cT yTp yT q kv vs mx d e sm rc pk pq a bda sTp sT bm tt o y2 n b "
                            "e1 h1 d1 hs e2 h2 d2 x " + LN_SEMS)
            self.Y = sb("Y", [P, GB, D])
            self.Y2 = sb("Y2", [P, GB, D])
            self.YT = sb("YT", [D, T])
            self.Cs = sb("Cs", [S2, GB, D])
            self.cT = sb("cT", [D, GB, S2])
            self.DD = sb("DD", [P, 2, GB, D])
            self.E = sb("E", [P, 2, GB, D])
            self.mx = sb("mx", [P, 2, GB * H])
            self.sm = sb("sm", [P, 2, GB * H])
            self.V = sb("V", [P, GB, D])
            self.BDA = sb("BDA", [D, GB, D])
            self.sT = sb("sT", [D, T])
            self.TT = sb("TT", [P, 2, GB * 4, W16])
            self.h1 = sb("h1", [BN, T])
            self.hs = sb("hs", [HID, T])
            self.h2 = sb("h2", [BN, T])
            self.ln = {k: (v if k in ("half", "eps") else sb("ln_" + k, v.shape)) for k, v in c.ln.items()}

        def bank(self, k, r=P):
            return PS[0:r, 4 * self.i + k, :]

        def part(self, k, r, b, n=D):
            return PS[r, 4 * self.i + k, b * n:(b + 1) * n]

    lanes = [Lane(i) for i in range(LANES)]

    def run(eng, setup, stages):
        setup()
        with eng.Fori(0, NI) as g:
            for stage in stages:
                for L in lanes:
                    stage(L, g)

    with nc.Block() as block:

        @block.sync
        def _(sp):
            for L in lanes:
                sp.dma_start(L.Cs[:, :, :], c.dram["ctx"][:, L.i * GB:(L.i + 1) * GB, :]).then_inc(L.s["cs"], 16)
            with sp.Fori(1, NI) as g:
                for L in lanes:
                    sp.wait_ge(L.s["cTp"], g)
                    sp.dma_start(L.Cs[:, :, :], c.dram["ctx"][:, bass.ds((g * LANES + L.i) * GB, GB), :]).then_inc(L.s["cs"], 16)

        @block.gpsimd
        def _(pool):

            def keys(k):
                def stage(L, g):
                    K = KL[k]
                    pool.wait_ge(L.s["rc"], g * 2 + k)
                    nc.gpsimd.tensor_tensor(heads(L.DD[0:K, 1]), heads(L.E[0:K, 1]), each(L.sm[0:K, 1, :], K), ALU.mult).then_inc(L.s["pk"], 1)
                return stage

            def rstd(k):
                def stage(L, g):
                    ln_rstd(pool, nc, L.ln, L.s, g * 4 + k)
                return stage

            def setup():
                for L in lanes:
                    nc.gpsimd.tensor_copy(L.Y[:, :, :], X[:, L.i * GB:(L.i + 1) * GB, :]).then_inc(L.s["ys"], 1)

            def rows(L, g):
                pool.wait_ge(L.s["y2"], g * 4 + 4)
                nc.gpsimd.tensor_copy(L.Y[:, :, :], group(c, g * LANES + (L.i + LANES))).then_inc(L.s["ys"], 1)

            stages = [keys(1), rstd(1), keys(2), rstd(2), rstd(3)]
            setup()
            with pool.Fori(0, NI - 1) as g:
                for stage in stages + [rows, rstd(4)]:
                    for L in lanes:
                        stage(L, g)
            for stage in stages + [rstd(4)]:
                for L in lanes:
                    stage(L, NI - 1)

        @block.scalar
        def _(act):

            def context(L, g):
                act.wait_ge(L.s["cTp"], g + 1)
                nc.scalar.copy(flat(L.cT[:, :, :]), L.bank(2)[:, 0:GB * S2]).then_inc(L.s["cT"], 1)

            def y_transposed(k):
                def stage(L, g):
                    act.wait_ge(L.s["yTp"], g * 3 + k)
                    if k < 3:
                        nc.scalar.copy(L.YT[:, :].rearrange("p (b w a) -> p b w a", b=GB, w=W8), L.bank(3).rearrange("p (b a w) -> p b w a", b=GB, w=W8)).then_inc(L.s["yT"], 1)
                    else:
                        nc.scalar.copy(L.YT[:, :], L.bank(3)).then_inc(L.s["yT"], 1)
                return stage

            def values(k):
                def stage(L, g):
                    act.wait_ge(L.s["kv"], g * 2 + k)
                    nc.scalar.copy(flat(L.V[0:KL[k], :, :]), L.bank(2, KL[k])).then_inc(L.s["vs"], 1)
                return stage

            def exps(k, i):
                def stage(L, g):
                    n = P if i == 0 else KL[k]
                    act.wait_ge(L.s["d"], g * 4 + (2 * k + i - 1))
                    nc.scalar.activation(flat(L.E[0:n, i]), flat(L.DD[0:n, i]), ACT.Exp, scale=DH ** -0.25).then_inc(L.s["e"], 1)
                return stage

            def softmax_transposed(k):
                def stage(L, g):
                    act.wait_ge(L.s["sTp"], g * 2 + k)
                    nc.scalar.copy(L.sT[:, :], L.bank(3)).then_inc(L.s["sT"], 1)
                return stage

            def bottleneck1(L, g):
                act.wait_ge(L.s["e1"], g + 1)
                nc.scalar.copy(L.h1[:, :], L.bank(0, BN)).then_inc(L.s["h1"], 1)

            def hidden(L, g):
                act.wait_ge(L.s["d1"], g + 1)
                nc.scalar.activation(L.hs[:, :], L.bank(1), ACT.Silu).then_inc(L.s["hs"], 1)

            def bottleneck2(L, g):
                act.wait_ge(L.s["e2"], g + 1)
                nc.scalar.copy(L.h2[:, :], L.bank(2, BN)).then_inc(L.s["h2"], 1)

            attend = lambda k: [y_transposed(k), exps(k, 0), exps(k, 1), values(k), softmax_transposed(k)]
            run(act, lambda: act.wait_ge(wsem, wcount), [context] + attend(1) + attend(2) + [y_transposed(3), bottleneck1, hidden, bottleneck2])

        @block.vector
        def _(dve):

            def less_max(k, i):
                def stage(L, g):
                    n = P if i == 0 else KL[k]
                    at = g * 4 + (2 * k + i - 1)
                    src = L.bank(i, n).rearrange("p (m d) -> p m d", d=DH)
                    dve.wait_ge(L.s["q" if i == 0 else "kv"], g * 2 + k)
                    nc.vector.tensor_reduce(L.mx[0:n, i, :], src, AX_X, ALU.max).then_inc(L.s["mx"], 1)
                    dve.wait_ge(L.s["mx"], at)
                    nc.vector.tensor_tensor(heads(L.DD[0:n, i]), src, each(L.mx[0:n, i, :], n), ALU.subtract).then_inc(L.s["d"], 1)
                return stage

            def sums(k):
                def stage(L, g):
                    K = KL[k]
                    for i, n in ((0, P), (1, K)):
                        dve.wait_ge(L.s["e"], g * 4 + (2 * k + i - 1))
                        nc.vector.tensor_reduce(L.mx[0:n, i, :], heads(L.E[0:n, i]), AX_X, ALU.add).then_inc(L.s["sm"], 1)
                    dve.wait_ge(L.s["sm"], g * 4 + 2 * k)
                    if K < P:
                        nc.vector.reciprocal(L.sm[:, 0, :], L.mx[:, 0, :])
                    nc.vector.reciprocal(L.sm[0:K, 1, :] if K < P else L.sm[:, :, :], L.mx[0:K, 1, :] if K < P else L.mx[:, :, :]).then_inc(L.s["rc"], 1)
                    dve.wait_ge(L.s["rc"], g * 2 + k)
                    nc.vector.tensor_tensor(heads(L.DD[:, 0]), heads(L.E[:, 0]), each(L.sm[:, 0, :], P), ALU.mult).then_inc(L.s["pq"], 1)
                return stage

            def diagonal(k):
                def stage(L, g):
                    dve.wait_ge(L.s["a"], g * 2 + k)
                    nc.vector.tensor_tensor(L.BDA[:, :, :], bd(L.bank(2)), row(W["bdm"][:, :]), ALU.mult).then_inc(L.s["bda"], 1)
                return stage

            def reshape(k):
                def stage(L, g):
                    dve.wait_ge(L.s["bm"], g * 2 + k)
                    nc.vector.transpose(L.TT[:, :, :, :].rearrange("p w m a -> p m w a"), L.bank(0).rearrange("p (m w a) -> p m w a", w=2, a=W16)).then_inc(L.s["tt"], 1)
                return stage

            def residual(k, done, bk):
                def stage(L, g):
                    dve.wait_ge(L.s[done], g * (1 if k == 3 else 2) + (1 if k == 3 else k))
                    nc.vector.tensor_tensor(flat(L.Y2[:, :, :]), L.bank(bk), flat(L.Y[:, :, :]), ALU.add).then_inc(L.s["y2"], 1)
                    dve.wait_ge(L.s["y2"], g * 4 + k)
                    ln_stats(dve, nc, L.Y2, L.ln, L.s, g * 4 + k)
                return stage

            def post_norm(k):
                def stage(L, g):
                    dve.wait_ge(L.s["mv"], g * 4 + k)
                    for b in range(GB):
                        ins = nc.vector.scalar_tensor_tensor(L.Y2[:, b, :], L.Y2[:, b, :], L.ln["mv"][:, b, 0:1], W[f"g{k}"][:, :], ALU.subtract, ALU.mult)
                    ins.then_inc(L.s["n"], 1)
                    dve.wait_ge(L.s["n"], g * 3 + k)
                    dve.wait_ge(L.s["rs"], g * 4 + k)
                    for b in range(GB):
                        ins = nc.vector.scalar_tensor_tensor(L.Y[:, b, :], L.Y2[:, b, :], L.ln["rs"][:, b:b + 1], W[f"b{k}"][:, :], ALU.mult, ALU.add)
                    ins.then_inc(L.s["b"], 1)
                return stage

            def outer_sum(L, g):
                dve.wait_ge(L.s["b"], g * 3 + 3)
                nc.vector.tensor_tensor(L.Y2[:, :, :], L.Y[:, :, :], group(c, g * LANES + L.i), ALU.add).then_inc(L.s["y2"], 1)
                dve.wait_ge(L.s["y2"], g * 4 + 4)
                ln_stats(dve, nc, L.Y2, L.ln, L.s, g * 4 + 4)

            def outer_norm(L, g):
                ln_apply(dve, nc, group(c, g * LANES + L.i), L.Y2, L.ln, L.s, g * 4 + 4, L.s["x"])

            attend = lambda k: [less_max(k, 0), less_max(k, 1), sums(k), diagonal(k), reshape(k), residual(k, "o", 1), post_norm(k)]
            run(dve, lambda: dve.wait_ge(wsem, wcount), attend(1) + attend(2) + [residual(3, "d2", 3), post_norm(3), outer_sum, outer_norm])

        @block.tensor
        def _(pe):

            def transposes(L, k, src, done, rows=P):
                for b in range(GB):
                    ins = nc.tensor.transpose(L.part(k, slice(0, P), b, rows), src[0:rows, b, :], c.identf[0:rows, 0:rows])
                ins.then_inc(L.s[done], 1)

            def context(L, g):
                pe.wait_ge(L.s["cs"], g * 16 + 16)
                transposes(L, 2, L.Cs, "cTp", S2)

            def y_transposed(k):
                def stage(L, g):
                    if k == 1:
                        pe.wait_ge(L.s["ys"], g + 1)
                    else:
                        pe.wait_ge(L.s["b"], g * 3 + (k - 1))
                    transposes(L, 3, L.Y, "yTp")
                return stage

            def queries(k):
                def stage(L, g):
                    pe.wait_ge(L.s["yT"], g * 3 + k)
                    for b in range(GB):
                        q = L.part(0, slice(0, P), b)
                        ins = nc.tensor.matmul(q, L.YT[:, b * P:(b + 1) * P], W[f"wq{k}"][:, :], start=True, stop=k == 2)
                        if k == 1:
                            ins = nc.tensor.matmul(q, c.identb[:, :], W["qmask"][:, :], start=False, stop=True)
                    ins.then_inc(L.s["q"], 1)
                return stage

            def keys_values(k):
                def stage(L, g):
                    pe.wait_ge(L.s["cT"], g + 1)
                    for i in (0, 1):
                        for b in range(GB):
                            src = L.YT[:, b * P:(b + 1) * P] if k == 1 else L.cT[:, b, :]
                            ins = nc.tensor.matmul(L.part(1 + i, slice(0, KL[k]), b), src, W[f"wkv{k}"][:, i, :], start=True, stop=True)
                    ins.then_inc(L.s["kv"], 1)
                return stage

            def softmax_transposed(k):
                def stage(L, g):
                    pe.wait_ge(L.s["pq"], g * 2 + k)
                    transposes(L, 3, L.DD[:, 0], "sTp")
                return stage

            def products(k):
                def stage(L, g):
                    K = KL[k]
                    pe.wait_ge(L.s["pk"], g * 2 + k)
                    pe.wait_ge(L.s["vs"], g * 2 + k)
                    for b in range(GB):
                        ins = nc.tensor.matmul(L.part(2, slice(0, P), b), L.DD[0:K, 1, b, :], L.V[0:K, b, :], start=True, stop=True)
                    ins.then_inc(L.s["a"], 1)
                return stage

            def outputs(k):
                def stage(L, g):
                    pe.wait_ge(L.s["sT"], g * 2 + k)
                    pe.wait_ge(L.s["bda"], g * 2 + k)
                    for b in range(GB):
                        ins = nc.tensor.matmul(L.part(0, slice(0, P), b), L.sT[:, b * P:(b + 1) * P], L.BDA[:, b, :], start=True, stop=True)
                    ins.then_inc(L.s["bm"], 1)
                return stage

            def projection(k):
                def stage(L, g):
                    pe.wait_ge(L.s["tt"], g * 2 + k)
                    for b in range(GB):
                        for hl in (0, 1):
                            for w in (0, 1):
                                rows = L.TT[:, w, 4 * b:4 * b + 4, :].rearrange("p f a -> p (f a)")
                                ins = nc.tensor.matmul(L.part(1, slice(64 * hl, 64 * hl + 64), b), rows, W[f"wo{k}"][:, hl, w, :],
                                                       start=(w == 0), stop=(w == 1))
                    ins.then_inc(L.s["o"], 1)
                return stage

            def dense(w, src, before, bk, rows, done, n=1):
                def stage(L, g):
                    pe.wait_ge(L.s[before], g * n + n)
                    nc.tensor.matmul(L.bank(bk, rows), W[w][:, :], src(L)[:, :], start=True, stop=True).then_inc(L.s[done], 1)
                return stage

            def mlp_output(L, g):
                pe.wait_ge(L.s["h2"], g + 1)
                for b in range(GB):
                    ins = nc.tensor.matmul(L.part(3, slice(0, P), b), L.h2[:, b * P:(b + 1) * P], W["d2"][:, :], start=True, stop=True)
                ins.then_inc(L.s["d2"], 1)

            attend = lambda k: [y_transposed(k), queries(k), keys_values(k), softmax_transposed(k), products(k), outputs(k), projection(k)]
            run(pe, lambda: pe.wait_ge(wsem, wcount), [context] + attend(1) + attend(2) + [
                y_transposed(3), dense("e1", lambda L: L.YT, "yT", 0, BN, "e1", 3), dense("d1", lambda L: L.h1, "h1", 1, P, "d1"),
                dense("e2", lambda L: L.hs, "hs", 2, BN, "e2"), mlp_output])
    c.end_phase(ctx)


PHASES[2] = linear_attention_block



def top2(dve, nc, sel, t, s, base):
    n = sel.shape[1]
    idx = t["idx"][:, :].rearrange("p (o e) -> p o e", o=1).to_broadcast([P, n, 8])
    bc = lambda ap: ap.rearrange("p (n o) -> p n o", o=1).to_broadcast([P, n, 8])
    at = 0

    def step(ins):
        nonlocal at
        at += 1
        ins.then_inc(s["t"], 1)
        dve.wait_ge(s["t"], base + at)

    for src, oh in ((sel, t["oh1"]), (t["sel2"][:, :, :], t["oh2"])):
        step(nc.vector.tensor_reduce(t["m"][:, :], src, AX_X, ALU.max))
        step(nc.vector.tensor_tensor(t["key"][:, :, :], src, bc(t["m"][:, :]), ALU.is_equal))
        step(nc.vector.tensor_tensor(t["key"][:, :, :], t["key"][:, :, :], idx, ALU.mult))
        step(nc.vector.tensor_reduce(t["m"][:, :], t["key"][:, :, :], AX_X, ALU.max))
        step(nc.vector.tensor_tensor(oh[:, :, :], t["key"][:, :, :], bc(t["m"][:, :]), ALU.is_equal))
        if oh is t["oh1"]:
            step(nc.vector.scalar_tensor_tensor(t["sel2"][:, :, :], oh[:, :, :], -BIG, src, ALU.mult, ALU.add))


TOP2 = 11



def routed_ffn(c, W, wsem, wcount, out):
    nc, X, PS = c.nc, c.X, c.PS
    NE, SC = 8, 2
    SH = 2
    SLOT = {"stats": 0, "rstd": 0, "norm": 1, "gate": 2, "activate": 3, "other": 4, "product": 4, "route1": 4, "route2": 5, "route3": 6, "route4": 7,
            "shared": 6, "start": 7, "x_T": 6, "x_copy": 7, "rows": 7}
    s = c.sems("f_", "xs xTp xT lg h1 h3 ex sg h t y0 acc0 ep ge ey acc x " + LN_SEMS)
    ctx = ExitStack()
    sb = lambda n, sh, dt=F32: c.sb("f_" + n, sh, dt, ctx)
    Xs = sb("Xs", [P, GB, D])
    xT = sb("xT", [D, 2, T])
    sg = sb("sg", [P, SC, T])
    hs = sb("hs", [P, SC, T])
    el = sb("el", [P, GB, NE])
    sc = sb("sc", [P, GB, NE])
    sel = sb("sel", [P, GB, NE])
    t = {"m": sb("m", [P, GB]), "idx": W["idx"]}
    for n in ("key", "sel2", "oh1", "oh2", "ss"):
        t[n] = sb(n, [P, GB, NE])
    den = sb("den", [P, 4, GB])
    comb = sb("comb", [P, 2, GB, NE])
    G = sb("G", [P, 2, T])
    Acc = sb("Acc", [P, 2, GB, D])
    ln = c.ln
    bank = lambda i, r=P: PS[0:r, i, :]
    bc = lambda ap: ap.rearrange("p (n o) -> p n o", o=1).to_broadcast([P, GB, NE])
    SR = TOP2 + 14

    def first(g, e):
        return isinstance(g, int) and g == 0 and e < 2

    with nc.Block() as block:

        @block.gpsimd
        def _(pool):

            def rows(g, par):
                if not isinstance(g, int) or g > 0:
                    pool.wait_ge(s["xTp"], g)
                nc.gpsimd.tensor_copy(Xs[:, :, :], group(c, g)).then_inc(s["xs"], 1)

            def rstd(g, par):
                ln_rstd(pool, nc, ln, s, g + 1)

            pipeline(pool, SLOT, SH, NE, lambda: None, {"rows": rows}, {}, lambda g, par, e, left: None, {"rstd": rstd})

        @block.scalar
        def _(act):

            def x_copy(g, par):
                act.wait_ge(s["xTp"], g + 1)
                nc.scalar.copy(xT[:, par, :], bank(0)).then_inc(s["xT"], 1)

            def activate(g, par):
                act.wait_ge(s["lg"], g + 1)
                nc.scalar.activation(el[:, :, :].rearrange("p b e -> p (b e)"), PS[:, 1, 0:GB * NE], ACT.Exp, scale=-1.0).then_inc(s["ex"], 1)
                act.wait_ge(s["h1"], g + 1)
                nc.scalar.activation(sg[:, :, :], PS[:, 2:4, :], ACT.Silu).then_inc(s["sg"], 1)

            def step(g, par, e, left):
                act.wait_ge(s["ep"], g * NE + e + 1)
                if not first(g, e):
                    act.wait_ge(s["ey"], g * NE + e - 1)
                nc.scalar.activation(G[:, e % 2, :], bank(6 + e % 2), ACT.Gelu).then_inc(s["ge"], 1)

            pipeline(act, SLOT, SH, NE, lambda: act.wait_ge(wsem, wcount), {"x_copy": x_copy}, {"activate": activate}, step, {})

        @block.vector
        def _(dve):

            def route(part):
                def stage(g, par):
                    base = {1: 0, 2: 3, 3: 3 + TOP2, 4: 3 + TOP2 + 6}[part]
                    k = base

                    def step(ins):
                        nonlocal k
                        k += 1
                        ins.then_inc(s["t"], 1)
                        dve.wait_ge(s["t"], g * SR + k)

                    if part == 1:
                        dve.wait_ge(s["ex"], g + 1)
                        step(nc.vector.tensor_scalar(el[:, :, :], el[:, :, :], 1.0, None, ALU.add))
                        step(nc.vector.reciprocal(sc[:, :, :], el[:, :, :]))
                        step(nc.vector.tensor_tensor(sel[:, :, :], sc[:, :, :], W["rb"][:, :].rearrange("p (o e) -> p o e", o=1).to_broadcast([P, GB, NE]), ALU.add))
                    if part == 2:
                        top2(dve, nc, sel[:, :, :], t, s, g * SR + k)
                    if part == 3:
                        step(nc.vector.tensor_tensor(t["key"][:, :, :], t["oh1"][:, :, :], t["oh2"][:, :, :], ALU.add))
                        step(nc.vector.tensor_tensor(t["ss"][:, :, :], t["key"][:, :, :], sc[:, :, :], ALU.mult))
                        step(nc.vector.tensor_reduce(den[:, 0, :], t["ss"][:, :, :], AX_X, ALU.add))
                        step(nc.vector.tensor_scalar(den[:, 1, :], den[:, 0, :], 1e-9, None, ALU.add))
                        step(nc.vector.reciprocal(den[:, 2, :], den[:, 1, :]))
                        step(nc.vector.tensor_scalar(den[:, 3, :], den[:, 0, :], 1e-9, None, ALU.is_gt))
                    if part == 4:
                        step(nc.vector.tensor_tensor(den[:, 2, :], den[:, 2, :], den[:, 3, :], ALU.mult))
                        step(nc.vector.tensor_scalar(den[:, 3, :], den[:, 3, :], -0.5, 0.5, ALU.mult, ALU.add))
                        step(nc.vector.tensor_tensor(t["ss"][:, :, :], t["ss"][:, :, :], bc(den[:, 2, :]), ALU.mult))
                        step(nc.vector.tensor_tensor(t["key"][:, :, :], t["key"][:, :, :], bc(den[:, 3, :]), ALU.mult))
                        step(nc.vector.tensor_tensor(comb[:, par], t["ss"][:, :, :], t["key"][:, :, :], ALU.add))
                        assert k == SR
                return stage

            def product(g, par):
                dve.wait_ge(s["sg"], g + 1)
                dve.wait_ge(s["h3"], g + 1)
                nc.vector.tensor_tensor(hs[:, :, :], PS[:, 0:2, :], sg[:, :, :], ALU.mult).then_inc(s["h"], 1)

            def start(g, par):
                dve.wait_ge(s["y0"], g + 1)
                nc.vector.tensor_tensor(flat(Acc[:, par]), bank(2), flat(group(c, g)), ALU.add).then_inc(s["acc0"], 1)

            def step(g, par, e, left):
                dve.wait_ge(s["ey"], g * NE + e + 1)
                dve.wait_ge(s["acc0"] if e == 0 else s["acc"], g + 1 if e == 0 else g * NE + e)
                for b in range(GB):
                    ins = nc.vector.scalar_tensor_tensor(Acc[:, par, b, :], PS[:, 4 + e % 2, b * D:(b + 1) * D], comb[:, par, b, e:e + 1], Acc[:, par, b, :], ALU.mult, ALU.add)
                ins.then_inc(s["acc"], 1)

            def stats(g, par):
                dve.wait_ge(s["acc"], g * NE + NE)
                ln_stats(dve, nc, Acc[:, par], ln, s, g + 1)

            def norm(g, par):
                ln_apply(dve, nc, group(c, g), Acc[:, par], ln, s, g + 1, s["x"])

            pipeline(dve, SLOT, SH, NE, lambda: dve.wait_ge(wsem, wcount), {},
                     {"product": product, "route1": route(1), "route2": route(2), "route3": route(3), "route4": route(4), "start": start}, step,
                     {"stats": stats, "norm": norm})

        @block.tensor
        def _(pe):

            def transpose(g, par):
                pe.wait_ge(s["xs"], g + 1)
                if not isinstance(g, int) or g > 0:
                    pe.wait_ge(s["h"], g)
                for b in range(GB):
                    ins = nc.tensor.transpose(PS[:, 0, b * P:(b + 1) * P], Xs[:, b, :], c.identf[:, :])
                ins.then_inc(s["xTp"], 1)

            def gate(g, par):
                pe.wait_ge(s["xT"], g + 1)
                for b in range(GB):
                    ins = nc.tensor.matmul(PS[:, 1, b * NE:(b + 1) * NE], xT[:, par, b * P:(b + 1) * P], W["rw"][:, :], start=True, stop=True)
                ins.then_inc(s["lg"], 1)
                if not isinstance(g, int) or g > 0:
                    pe.wait_ge(s["acc0"], g)
                for i in range(SC):
                    ins = nc.tensor.matmul(bank(2 + i), W["sw1"][:, i * P:(i + 1) * P], xT[:, par, :], start=True, stop=True)
                ins.then_inc(s["h1"], 1)

            def other(g, par):
                pe.wait_ge(s["ex"], g + 1)
                for i in range(SC):
                    ins = nc.tensor.matmul(bank(i), W["sw3"][:, i * P:(i + 1) * P], xT[:, par, :], start=True, stop=True)
                ins.then_inc(s["h3"], 1)

            def shared(g, par):
                pe.wait_ge(s["h"], g + 1)
                for b in range(GB):
                    for i in range(SC):
                        ins = nc.tensor.matmul(PS[:, 2, b * D:(b + 1) * D], hs[:, i, b * P:(b + 1) * P], W["sw2"][:, i, :], start=(i == 0), stop=(i == SC - 1))
                ins.then_inc(s["y0"], 1)

            def hidden(g, par, e):
                if not first(g, e):
                    pe.wait_ge(s["ge"], g * NE + e - 1)
                nc.tensor.matmul(bank(6 + e % 2), W["ew1"][:, e, :], xT[:, par, :], start=True, stop=True).then_inc(s["ep"], 1)

            def step(g, par, e, left):
                if isinstance(g, int) and g == 0 and e == 0:
                    hidden(0, 0, 0)
                    hidden(0, 0, 1)
                pe.wait_ge(s["ge"], g * NE + e + 1)
                if not first(g, e):
                    pe.wait_ge(s["acc"], g * NE + e - 1)
                for b in range(GB):
                    ins = nc.tensor.matmul(PS[:, 4 + e % 2, b * D:(b + 1) * D], G[:, e % 2, b * P:(b + 1) * P], W["ew2"][:, e, :], start=True, stop=True)
                ins.then_inc(s["ey"], 1)
                if e + 2 < NE:
                    hidden(g, par, e + 2)
                elif left:
                    hidden(g + 1, 1 - par, e + 2 - NE)

            pipeline(pe, SLOT, SH, NE, lambda: pe.wait_ge(wsem, wcount), {"x_T": transpose}, {"gate": gate, "other": other, "shared": shared}, step, {})
    c.end_phase(ctx)


PHASES[3] = routed_ffn



def state_space(c, W, wsem, wcount, out):
    nc, X, PS = c.nc, c.X, c.PS
    CH, NS, DC = 2, 16, 4
    NI = NS * CH
    ND = 4
    SH = 8
    s = c.sems("m_", "A xp0 z0 n xnp xnT xp xpc z sz cv u dtp dtr bcp hi r sp dv ab e w l t m dt du "
                     "B C dA dBu h Cs hC yacc y1 y2 yp r2 x " + LN_SEMS + " ist imv ilv irs")
    si = {k: s["i" + k] for k in LN_SEMS.split()}
    ctx = ExitStack()
    sb = lambda n, sh, dt=F32: c.sb("m_" + n, sh, dt, ctx)
    Xn = sb("Xn", [P, GB, D])
    xnT = sb("xnT", [D, T])
    xp = sb("xp", [P, CH, GB, DC - 1 + P])
    U = sb("U", [P, CH, T])
    U2 = sb("U2", [P, 2, CH, T])
    SZ = sb("SZ", [P, 2, CH, T])
    DT = sb("DT", [P, 2, CH, T])
    DU = sb("DU", [P, 2, CH, T])
    hi = sb("hi", [96, 2, T], BF16)
    E1 = sb("E1", [P, CH, T])
    E2 = sb("E2", [P, CH, T])
    L = sb("L", [P, CH, T])
    YG = sb("YG", [P, CH, T])
    dtr = sb("dtr", [8, T])
    R = sb("R", [96, T])
    A = sb("A", [P, CH, NS])
    dA = sb("dA", [P, ND, GB, P])
    dBu = sb("dBu", [P, 2, T])
    hst = sb("h", [P, ND, T])
    Cs = sb("Cs", [P, ND, T])
    hC = sb("hC", [P, ND, T])
    ln, iln = c.ln, {k: (c.sb("m_i" + k, v.shape, F32, ctx) if k not in ("half", "eps") else v) for k, v in c.ln.items()}
    bank = lambda i, r=P: PS[0:r, i, :]
    bl = lambda ap: ap.rearrange("p (b l) -> p b l", b=GB)
    AUX = (7, 0)
    SLOT = {"gated": 2, "output": 0, "residual": 4, "rstd": 4, "norm": 7, "project_z": 8, "silus": 13, "dt_b_c": 11,
            "parts": 19, "rest": 21, "middle": 23, "last": 23, "dt": 21, "dt_bias": 25, "one_more": 28, "logs": 28,
            "rounding": 28, "softplus": 28, "inputs": 28, "inner_stats": 11, "inner_rstd": 12, "inner_norm": 15, "xn_T": 23, "xn_copy": 25,
            "project_x": 24, "xp_copy": 29, "tap0": 28, "tap1": 28, "tap2": 29, "tap3": 30}

    def first(g, i, depth):
        return isinstance(g, int) and g == 0 and i < depth

    with nc.Block() as block:

        @block.gpsimd
        def _(pool):

            def setup():
                nc.gpsimd.memset(xp[:, :, :, 0:DC - 1], 0.0).then_inc(s["xp0"], 1)
                nc.gpsimd.memset(dA[:, :, :, 0:1], 0.0).then_inc(s["z0"], 1)

            def inner_norm(g, par):
                ln_rstd(pool, nc, iln, si, g + 1)

            def inputs(g, par):
                pool.wait_ge(s["dt"], g + 1)
                nc.gpsimd.tensor_tensor(DU[:, par], DT[:, par], U2[:, par], ALU.mult).then_inc(s["du"], 1)

            def step(g, par, i, left):
                n = i // CH
                pool.wait_ge(s["h"], g * NI + i + 1)
                pool.wait_ge(s["Cs"], g * NS + n + 1)
                if not first(g, i, ND):
                    pool.wait_ge(s["yacc"], g * NI + i - ND + 1)
                nc.gpsimd.tensor_tensor(hC[:, i % ND, :], hst[:, i % ND, :], Cs[:, n % ND, :], ALU.mult).then_inc(s["hC"], 1)

            def norm(g, par):
                ln_rstd(pool, nc, ln, s, g + 1)

            pipeline(pool, SLOT, SH, NI, setup, {"inner_rstd": inner_norm}, {"inputs": inputs}, step, {"rstd": norm})

        @block.scalar
        def _(act):

            def setup():
                act.wait_ge(wsem, wcount)
                act.wait_ge(s["xp0"], 1)
                act.wait_ge(s["z0"], 1)
                nc.scalar.activation(A[:, :, :], W["alog"][:, :, :], ACT.Exp).then_inc(s["A"], 1)
                act.wait_ge(s["A"], 1)
                nc.scalar.activation(A[:, :, :], A[:, :, :], ACT.Copy, scale=-1.0).then_inc(s["A"], 1)
                act.wait_ge(s["A"], 2)

            def normalised(g, par):
                act.wait_ge(s["xnp"], g + 1)
                nc.scalar.activation(xnT[:, :], bank(0), ACT.Identity, scale=W["lnw"][:, 0:1], bias=W["lnb"][:, 0:1]).then_inc(s["xnT"], 1)

            def convolved(g, par):
                for ch in range(CH):
                    act.wait_ge(s["xpc"], g * CH + ch + 1)
                    nc.scalar.copy(xp[:, ch, :, DC - 1:DC - 1 + P], bl(bank(AUX[ch]))).then_inc(s["xp"], 1)

            def silus(g, par):
                for ch in range(CH):
                    act.wait_ge(s["z"], g * CH + ch + 1)
                    nc.scalar.activation(SZ[:, par, ch, :], bank(AUX[ch]), ACT.Silu).then_inc(s["sz"], 1)
                act.wait_ge(s["cv"], g * 8 + 8)
                nc.scalar.activation(U2[:, par], U[:, :, :], ACT.Silu).then_inc(s["u"], 1)
                nc.scalar.preload_act_table_set("natural_log_exp_and_others")

            def parts(g, par):
                act.wait_ge(s["dtp"], g + 1)
                nc.scalar.copy(dtr[:, :], bank(7, 8)).then_inc(s["dtr"], 1)
                act.wait_ge(s["bcp"], g + 1)
                nc.scalar.copy(hi[:, par, :], bank(0, 96)).then_inc(s["hi"], 1)

            def step_sizes(g, par):
                for ch in range(CH):
                    act.wait_ge(s["dv"], g * CH + ch + 1)
                    nc.scalar.activation(DT[:, par, ch, :], bank(AUX[ch]), ACT.Identity, bias=W["bdt"][:, ch:ch + 1]).then_inc(s["ab"], 1)
                act.wait_ge(s["ab"], g * 3 + 2)
                nc.scalar.activation(L[:, :, :], DT[:, par], ACT.Abs).then_inc(s["ab"], 1)
                act.wait_ge(s["ab"], g * 3 + 3)
                nc.scalar.activation(E1[:, :, :], L[:, :, :], ACT.Exp, scale=-1.0).then_inc(s["e"], 1)

            def logs(g, par):
                act.wait_ge(s["w"], g + 1)
                nc.scalar.activation(L[:, :, :], E2[:, :, :], ACT.Ln).then_inc(s["l"], 1)

            def step(g, par, i, left):
                n, ch = i // CH, i % CH
                if i == 0:
                    act.wait_ge(s["dt"], g + 1)
                if not first(g, i, ND):
                    act.wait_ge(s["h"], g * NI + i - ND + 1)
                nc.scalar.activation(dA[:, i % ND, :, 1:P], bl(DT[:, par, ch, :])[:, :, 1:P], ACT.Exp, scale=A[:, ch, n:n + 1]).then_inc(s["dA"], 1)
                if ch == 0:
                    act.wait_ge(s["C"], g * NS + n + 1)
                    if not first(g, n, ND):
                        act.wait_ge(s["hC"], g * NI + CH * (n - ND + 1))
                    nc.scalar.copy(Cs[:, n % ND, :], bank(3 + n % 2)).then_inc(s["Cs"], 1)

            pipeline(act, SLOT, SH, NI, setup, {"xn_copy": normalised, "xp_copy": convolved}, {"silus": silus, "parts": parts, "dt_bias": step_sizes, "logs": logs}, step, {})

        @block.vector
        def _(dve):

            def setup():
                dve.wait_ge(wsem, wcount)
                dve.wait_ge(s["xp0"], 1)
                dve.wait_ge(s["z0"], 1)

            def stats(g, par):
                ln_stats(dve, nc, group(c, g), iln, si, g + 1)

            def normalise(g, par):
                ln_apply(dve, nc, Xn, group(c, g), iln, si, g + 1, s["n"])

            def tap(k):
                def conv(g, par):
                    for ch in range(CH):
                        if k == 0:
                            dve.wait_ge(s["xp"], g * CH + ch + 1)
                            nc.vector.tensor_scalar(bl(U[:, ch, :]), xp[:, ch, :, 0:P], W["cw"][:, ch, 0:1], W["cb"][:, ch:ch + 1], ALU.mult, ALU.add).then_inc(s["cv"], 1)
                        else:
                            dve.wait_ge(s["cv"], g * 8 + (2 * k + ch - 1))
                            nc.vector.scalar_tensor_tensor(bl(U[:, ch, :]), xp[:, ch, :, k:k + P], W["cw"][:, ch, k:k + 1], bl(U[:, ch, :]), ALU.mult, ALU.add).then_inc(s["cv"], 1)
                return conv

            def rest(g, par):
                dve.wait_ge(s["hi"], g + 1)
                nc.vector.tensor_tensor(R[:, :], bank(0, 96), hi[:, par, :], ALU.subtract).then_inc(s["r"], 1)

            def middle(g, par):
                dve.wait_ge(s["r"], g * 2 + 1)
                nc.vector.tensor_copy(hi[32:64, par, :], R[32:64, :]).then_inc(s["sp"], 1)
                nc.vector.tensor_copy(hi[64:96, par, :], R[64:96, :]).then_inc(s["sp"], 1)

            def last(g, par):
                dve.wait_ge(s["sp"], g * 3 + 2)
                nc.vector.tensor_tensor(R[64:96, :], R[64:96, :], hi[64:96, par, :], ALU.subtract).then_inc(s["r"], 1)
                dve.wait_ge(s["r"], g * 2 + 2)
                nc.vector.tensor_copy(hi[64:96, par, :], R[64:96, :]).then_inc(s["sp"], 1)

            def one_more(g, par):
                dve.wait_ge(s["e"], g + 1)
                nc.vector.tensor_scalar(E2[:, :, :], E1[:, :, :], 1.0, None, ALU.add).then_inc(s["w"], 1)

            def rounding(g, par):
                dve.wait_ge(s["w"], g + 1)
                nc.vector.scalar_tensor_tensor(E1[:, :, :], E2[:, :, :], -1.0, E1[:, :, :], ALU.add, ALU.subtract).then_inc(s["t"], 1)

            def softplus(g, par):
                dve.wait_ge(s["l"], g + 1)
                nc.vector.scalar_tensor_tensor(DT[:, par], DT[:, par], 0.0, L[:, :, :], ALU.max, ALU.add).then_inc(s["m"], 1)
                dve.wait_ge(s["m"], g + 1)
                dve.wait_ge(s["t"], g + 1)
                nc.vector.tensor_tensor(DT[:, par], DT[:, par], E1[:, :, :], ALU.subtract).then_inc(s["dt"], 1)

            def step(g, par, i, left):
                n, ch = i // CH, i % CH
                if i == 0:
                    dve.wait_ge(s["du"], g + 1)
                dve.wait_ge(s["B"], g * NS + n + 1)
                if not first(g, i, 2):
                    dve.wait_ge(s["h"], g * NI + i - 1)
                nc.vector.tensor_tensor(dBu[:, i % 2, :], bank(1 + n % 2), DU[:, par, ch, :], ALU.mult).then_inc(s["dBu"], 1)
                dve.wait_ge(s["dBu"], g * NI + i + 1)
                dve.wait_ge(s["dA"], g * NI + i + 1)
                if not first(g, i, ND):
                    dve.wait_ge(s["hC"], g * NI + i - ND + 1)
                nc.vector.tensor_tensor_scan(hst[:, i % ND, :], dA[:, i % ND].rearrange("p b l -> p (b l)"), dBu[:, i % 2, :], 0.0, ALU.mult, ALU.add).then_inc(s["h"], 1)

            def gated(g, par):
                dve.wait_ge(s["yacc"], g * NI + NI)
                for ch in range(CH):
                    nc.vector.scalar_tensor_tensor(YG[:, ch, :], U2[:, par, ch, :], W["dp"][:, ch:ch + 1], bank(5 + ch), ALU.mult, ALU.add).then_inc(s["y1"], 1)
                dve.wait_ge(s["y1"], g * 2 + 2)
                nc.vector.tensor_tensor(YG[:, :, :], YG[:, :, :], SZ[:, par], ALU.mult).then_inc(s["y2"], 1)

            def residual(g, par):
                dve.wait_ge(s["yp"], g + 1)
                nc.vector.scalar_tensor_tensor(flat(Xn[:, :, :]), flat(group(c, g)), 2.0, bank(7), ALU.mult, ALU.add).then_inc(s["r2"], 1)
                dve.wait_ge(s["r2"], g + 1)
                ln_stats(dve, nc, Xn, ln, s, g + 1)

            def norm(g, par):
                ln_apply(dve, nc, group(c, g), Xn, ln, s, g + 1, s["x"])

            pipeline(dve, SLOT, SH, NI, setup, {"inner_stats": stats, "inner_norm": normalise, "tap0": tap(0), "tap1": tap(1), "tap2": tap(2), "tap3": tap(3)},
                     {"rest": rest, "middle": middle, "last": last, "one_more": one_more, "rounding": rounding, "softplus": softplus}, step,
                     {"gated": gated, "residual": residual, "norm": norm})

        @block.tensor
        def _(pe):

            def setup():
                pe.wait_ge(wsem, wcount)

            def transposed(g, par):
                pe.wait_ge(s["n"], g + 1)
                if not isinstance(g, int) or g > 0:
                    pe.wait_ge(s["ab"], g * 3)
                for b in range(GB):
                    ins = nc.tensor.transpose(PS[:, 0, b * P:(b + 1) * P], Xn[:, b, :], c.identf[:, :])
                ins.then_inc(s["xnp"], 1)

            def project(first_chunk, done, read):
                def stage(g, par):
                    for ch in range(CH):
                        if read:
                            pe.wait_ge(s[read], g * CH + ch + 1)
                        elif ch == 0:
                            pe.wait_ge(s["xnT"], g + 1)
                        i = first_chunk + ch
                        nc.tensor.matmul(bank(AUX[ch]), W["win"][:, i * P:(i + 1) * P], xnT[:, :], start=True, stop=True).then_inc(s[done], 1)
                return stage

            def dt_b_c(g, par):
                pe.wait_ge(s["u"], g + 1)
                for ch in range(CH):
                    ins = nc.tensor.matmul(bank(7, 8), W["wxd"][:, ch, :], U2[:, par, ch, :], start=(ch == 0), stop=(ch == CH - 1))
                ins.then_inc(s["dtp"], 1)
                for ch in range(CH):
                    ins = nc.tensor.matmul(bank(0, 96), W["wxb"][:, ch, :], U2[:, par, ch, :], start=(ch == 0), stop=(ch == CH - 1))
                ins.then_inc(s["bcp"], 1)

            def step_sizes(g, par):
                pe.wait_ge(s["dtr"], g + 1)
                for ch in range(CH):
                    if ch == 1:
                        pe.wait_ge(s["r"], g * 2 + 1)
                    nc.tensor.matmul(bank(AUX[ch]), W["wdt"][:, ch * P:(ch + 1) * P], dtr[:, :], start=True, stop=True).then_inc(s["dv"], 1)

            def spread(g, par, n):
                if n == 0:
                    pe.wait_ge(s["sp"], g * 3 + 3)
                if not first(g, n, 2):
                    pe.wait_ge(s["dBu"], g * NI + 2 * (n - 1))
                    pe.wait_ge(s["Cs"], g * NS + n - 1)
                nc.tensor.matmul(bank(1 + n % 2), W["sel"][:, n:n + 1].to_broadcast([96, P]), hi[:, par, :], start=True, stop=True).then_inc(s["B"], 1)
                nc.tensor.matmul(bank(3 + n % 2), W["sel"][:, NS + n:NS + n + 1].to_broadcast([96, P]), hi[:, par, :], start=True, stop=True).then_inc(s["C"], 1)

            def step(g, par, i, left):
                n, ch = i // CH, i % CH
                if isinstance(g, int) and g == 0 and i == 0:
                    spread(0, 0, 0)
                    spread(0, 0, 1)
                if n == 0 and not (isinstance(g, int) and g == 0):
                    pe.wait_ge(s["y1"], g * 2 - 1 + ch)
                pe.wait_ge(s["hC"], g * NI + i + 1)
                nc.tensor.matmul(bank(5 + ch), c.identf[:, :], hC[:, i % ND, :], start=(n == 0), stop=(n == NS - 1)).then_inc(s["yacc"], 1)
                if ch == 0:
                    if n + 2 < NS:
                        spread(g, par, n + 2)
                    elif left:
                        spread(g + 1, 1 - par, n + 2 - NS)

            def output(g, par):
                pe.wait_ge(s["y2"], g + 1)
                for b in range(GB):
                    for ch in range(CH):
                        ins = nc.tensor.matmul(PS[:, 7, b * D:(b + 1) * D], YG[:, ch, b * P:(b + 1) * P], W["wout"][:, ch, :], start=(ch == 0), stop=(ch == CH - 1))
                ins.then_inc(s["yp"], 1)

            pipeline(pe, SLOT, SH, NI, setup, {"xn_T": transposed, "project_x": project(0, "xpc", None)}, {"project_z": project(CH, "z", "xp"), "dt_b_c": dt_b_c, "dt": step_sizes}, step,
                     {"output": output})
    c.end_phase(ctx)


PHASES[4] = state_space


def context_attention(c, W, wsem, wcount, out):
    attention(c, "k_", True, W, wsem, wcount)


PHASES[5] = context_attention



def sinkhorn_ffn(c, W, wsem, wcount, out):
    nc, X, PS = c.nc, c.X, c.PS
    NE, FC, ITERS, SK_EPS = 8, 4, 20, 0.05
    ctx = ExitStack()
    sb = lambda n, sh, dt=F32: c.sb("e_" + n, sh, dt, ctx)
    s = c.sems("e_", "xs xTp xT lg la rm rd re rs rl ra cm cT gm dg gM cd ce cs ct cl ca t w "
                     "gp up sg h ey acc x st mv lv rs2 out")
    sl = {"st": s["st"], "mv": s["mv"], "lv": s["lv"], "rs": s["rs2"]}
    XT = sb("XT", [D, B, P])
    comb = sb("comb", [P, B, NE])
    ln = c.ln
    bank = lambda i, r=P: PS[0:r, i, :]

    rctx = ExitStack()
    rb = lambda n, sh, dt=F32: c.sb("e_" + n, sh, dt, rctx)
    Xs = rb("Xs", [P, 2, GB, D])
    LA = rb("LA", [P, B, NE])
    E = rb("E", [P, B, NE])
    rm = rb("rm", [P, B])
    rs = rb("rs", [P, B])
    rl = rb("rl", [P, B])
    cm = rb("cm", [P, NE])
    cs = rb("cs", [P, NE])
    cl = rb("cl", [P, NE])
    gm = rb("gm", [NE, 1])
    dg = rb("dg", [NE, NE])
    t = {"m": rm, "idx": W["idx"]}
    for n in ("key", "sel2", "oh1", "oh2"):
        t[n] = rb(n, [P, B, NE])
    rows = lambda ap: ap.rearrange("p (b o) -> p b o", o=1).to_broadcast([P, B, NE])
    cols = lambda ap: ap.rearrange("p (o e) -> p o e", o=1).to_broadcast([P, B, NE])
    byexp = lambda ap: ap.rearrange("p b e -> p e b")

    with nc.Block() as block:

        @block.gpsimd
        def _(pool):
            nc.gpsimd.tensor_copy(Xs[:, 0], X[:, 0:GB, :]).then_inc(s["xs"], 1)
            with pool.Fori(0, NG - 1) as g:
                pool.wait_ge(s["xTp"], g + 1)
                nc.gpsimd.tensor_copy(Xs[:, 0], group(c, g + 1)).then_inc(s["xs"], 1)

        @block.scalar
        def _(act):
            with act.Fori(0, NG) as g:
                act.wait_ge(s["xTp"], g + 1)
                nc.scalar.copy(XT[:, bass.ds(g * GB, GB), :].rearrange("p b d -> p (b d)"), bank(0)).then_inc(s["xT"], 1)
                nc.scalar.copy(Xs[:, 1].rearrange("p b d -> p (b d)"), bank(0)).then_inc(s["xT"], 1)
            nc.scalar.preload_act_table_set("natural_log_exp_and_others")
            with act.Fori(0, ITERS) as k:
                act.wait_ge(s["rd"], k + 1)
                nc.scalar.activation(E[:, :, :], LA[:, :, :], ACT.Exp).then_inc(s["re"], 1)
                act.wait_ge(s["rs"], k + 1)
                nc.scalar.activation(rl[:, :], rs[:, :], ACT.Ln).then_inc(s["rl"], 1)
                act.wait_ge(s["cd"], k + 1)
                nc.scalar.activation(E[:, :, :], LA[:, :, :], ACT.Exp).then_inc(s["ce"], 1)
                act.wait_ge(s["ct"], k + 1)
                nc.scalar.activation(cl[:, :], PS[:, 3, 0:NE], ACT.Ln).then_inc(s["cl"], 1)
            act.wait_ge(s["ca"], ITERS)
            nc.scalar.activation(E[:, :, :], LA[:, :, :], ACT.Exp).then_inc(s["re"], 1)

        @block.vector
        def _(dve):
            dve.wait_ge(wsem, wcount)
            with dve.Fori(0, NG) as g:
                dve.wait_ge(s["lg"], g + 1)
                nc.vector.tensor_scalar(LA[:, bass.ds(g * GB, GB), :], PS[:, 1, 0:GB * NE].rearrange("p (b e) -> p b e", b=GB), -1.0 / SK_EPS, None, ALU.mult).then_inc(s["la"], 1)
            dve.wait_ge(s["la"], NG)
            with dve.Fori(0, ITERS) as k:
                nc.vector.tensor_reduce(rm[:, :], LA[:, :, :], AX_X, ALU.max).then_inc(s["rm"], 1)
                dve.wait_ge(s["rm"], k + 1)
                nc.vector.tensor_tensor(LA[:, :, :], LA[:, :, :], rows(rm[:, :]), ALU.subtract).then_inc(s["rd"], 1)
                dve.wait_ge(s["re"], k + 1)
                nc.vector.tensor_reduce(rs[:, :], E[:, :, :], AX_X, ALU.add).then_inc(s["rs"], 1)
                dve.wait_ge(s["rl"], k + 1)
                nc.vector.tensor_tensor(LA[:, :, :], LA[:, :, :], rows(rl[:, :]), ALU.subtract).then_inc(s["ra"], 1)
                dve.wait_ge(s["ra"], k + 1)
                nc.vector.tensor_reduce(cm[:, :], byexp(LA[:, :, :]), AX_X, ALU.max).then_inc(s["cm"], 1)
                dve.wait_ge(s["cT"], k + 1)
                nc.vector.tensor_reduce(gm[:, :], PS[0:NE, 1, 0:P], AX_X, ALU.max).then_inc(s["gm"], 1)
                dve.wait_ge(s["gm"], k + 1)
                nc.vector.tensor_scalar(dg[:, :], c.identf[0:NE, 0:NE], gm[:, 0:1], None, ALU.mult).then_inc(s["dg"], 1)
                dve.wait_ge(s["gM"], k + 1)
                nc.vector.tensor_tensor(LA[:, :, :], LA[:, :, :], cols(PS[:, 2, 0:NE]), ALU.subtract).then_inc(s["cd"], 1)
                dve.wait_ge(s["ce"], k + 1)
                nc.vector.tensor_reduce(cs[:, :], byexp(E[:, :, :]), AX_X, ALU.add).then_inc(s["cs"], 1)
                dve.wait_ge(s["cl"], k + 1)
                nc.vector.tensor_tensor(LA[:, :, :], LA[:, :, :], cols(cl[:, :]), ALU.subtract).then_inc(s["ca"], 1)
                dve.wait_ge(s["ca"], k + 1)
            dve.wait_ge(s["re"], ITERS + 1)
            nc.vector.tensor_scalar(LA[:, :, :], E[:, :, :], float(np.finfo(np.float32).tiny), None, ALU.is_ge).then_inc(s["w"], 1)
            dve.wait_ge(s["w"], 1)
            nc.vector.tensor_tensor(E[:, :, :], E[:, :, :], LA[:, :, :], ALU.mult).then_inc(s["w"], 1)
            dve.wait_ge(s["w"], 2)
            top2(dve, nc, E[:, :, :], t, s, 0)
            for k, oh in enumerate((t["oh1"], t["oh2"])):
                nc.vector.tensor_tensor(oh[:, :, :], oh[:, :, :], E[:, :, k:k + 1].to_broadcast([P, B, NE]), ALU.mult).then_inc(s["w"], 1)
            dve.wait_ge(s["w"], 4)
            nc.vector.tensor_tensor(comb[:, :, :], t["oh1"][:, :, :], t["oh2"][:, :, :], ALU.add).then_inc(s["w"], 1)

        @block.tensor
        def _(pe):
            pe.wait_ge(wsem, wcount)
            with pe.Fori(0, NG) as g:
                pe.wait_ge(s["xs"], g + 1)
                for b in range(GB):
                    ins = nc.tensor.transpose(PS[:, 0, b * P:(b + 1) * P], Xs[:, 0, b, :], c.identf[:, :])
                ins.then_inc(s["xTp"], 1)
                pe.wait_ge(s["xT"], 2 * g + 2)
                for b in range(GB):
                    ins = nc.tensor.matmul(PS[:, 1, b * NE:(b + 1) * NE], Xs[:, 1, b, :], W["gw"][:, :], start=True, stop=True)
                ins.then_inc(s["lg"], 1)
                pe.wait_ge(s["la"], g + 1)
            with pe.Fori(0, ITERS) as k:
                pe.wait_ge(s["cm"], k + 1)
                nc.tensor.transpose(PS[0:NE, 1, 0:P], cm[:, :], c.identf[:, :]).then_inc(s["cT"], 1)
                pe.wait_ge(s["dg"], k + 1)
                nc.tensor.matmul(PS[:, 2, 0:NE], W["ones"][0:NE, :], dg[:, :], start=True, stop=True).then_inc(s["gM"], 1)
                pe.wait_ge(s["cs"], k + 1)
                nc.tensor.matmul(PS[:, 3, 0:NE], W["ones"][:, :], cs[:, :], start=True, stop=True).then_inc(s["ct"], 1)

    rctx.close()
    Sg = sb("Sg", [P, 2, T])
    Hh = sb("Hh", [P, 2, FC, T])
    Acc = sb("Acc", [P, GB, D])
    wg = sb("wg", [P, 2, GB, NE])
    NF = NE * FC
    with nc.Block() as block:

        @block.sync
        def _(sp):
            with sp.Fori(0, NG) as g:
                sp.wait_ge(s["x"], g + 1)
                sp.dma_start(out[bass.ds(g * GB, GB), :, :].rearrange("b p d -> p b d"), group(c, g)).then_inc(s["out"], 16)
            sp.wait_ge(s["out"], 16 * NG)

        @block.gpsimd
        def _(pool):
            with pool.Fori(0, NG) as g:
                ln_rstd(pool, nc, ln, sl, g + 1)

        @block.scalar
        def _(act):
            with act.Fori(0, NG) as g:
                for i in range(NF):
                    act.wait_ge(s["gp"], g * NF + (i + 1))
                    if i >= 2:
                        act.wait_ge(s["h"], g * NF + (i - 1))
                    nc.scalar.activation(Sg[:, i % 2, :], bank(i % 2), ACT.Silu).then_inc(s["sg"], 1)

        @block.vector
        def _(dve):
            dve.sem_inc(s["acc"], 1)
            with dve.Fori(0, NG) as g:

                def add(e):
                    dve.wait_ge(s["ey"], g * NE + (e + 1))
                    dve.wait_ge(s["acc"], g * NE + (e + 1))
                    for b in range(GB):
                        prior = Acc[:, b, :] if e else X[:, bass.ds(g * GB + b, 1), :].rearrange("p o d -> p (o d)")
                        ins = nc.vector.scalar_tensor_tensor(Acc[:, b, :], PS[:, 4 + e % 2, b * D:(b + 1) * D], wg[:, 0, b, e:e + 1], prior, ALU.mult, ALU.add)
                    ins.then_inc(s["acc"], 1)

                nc.vector.tensor_copy(wg[:, 0], comb[:, bass.ds(g * GB, GB), :]).then_inc(s["w"], 1)
                dve.wait_ge(s["w"], g + 6)
                for i in range(NF):
                    e = i // FC
                    dve.wait_ge(s["sg"], g * NF + (i + 1))
                    dve.wait_ge(s["up"], g * NF + (i + 1))
                    if e >= 2:
                        dve.wait_ge(s["ey"], g * NE + (e - 1))
                    nc.vector.tensor_tensor(Hh[:, e % 2, i % FC, :], bank(2 + i % 2), Sg[:, i % 2, :], ALU.mult).then_inc(s["h"], 1)
                    if i % FC == FC - 1 and e >= 1:
                        add(e - 1)
                add(NE - 1)
                dve.wait_ge(s["acc"], g * NE + (NE + 1))
                ln_stats(dve, nc, Acc, ln, sl, g + 1)
                ln_apply(dve, nc, group(c, g), Acc, ln, sl, g + 1, s["x"])

        @block.tensor
        def _(pe):
            with pe.Fori(0, NG) as g:
                rhs = XT[:, bass.ds(g * GB, GB), :].rearrange("p b d -> p (b d)")

                def down(e):
                    pe.wait_ge(s["h"], g * NF + FC * (e + 1))
                    pe.wait_ge(s["acc"], g * NE + (e if e >= 2 else 1))
                    for b in range(GB):
                        for f in range(FC):
                            ins = nc.tensor.matmul(PS[:, 4 + e % 2, b * D:(b + 1) * D], Hh[:, e % 2, f, b * P:(b + 1) * P], W["wd"][:, e, f, :], start=(f == 0), stop=(f == FC - 1))
                    ins.then_inc(s["ey"], 1)

                for i in range(NF):
                    e, f = i // FC, i % FC
                    if i >= 2:
                        pe.wait_ge(s["h"], g * NF + (i - 1))
                    nc.tensor.matmul(bank(i % 2), W["wg"][:, e, f * P:(f + 1) * P], rhs, start=True, stop=True).then_inc(s["gp"], 1)
                    nc.tensor.matmul(bank(2 + i % 2), W["wu"][:, e, f * P:(f + 1) * P], rhs, start=True, stop=True).then_inc(s["up"], 1)
                    if f == 0 and e >= 1:
                        down(e - 1)
                down(NE - 1)
    c.end_phase(ctx)


PHASES[6] = sinkhorn_ffn




def plan_weights():
    return {
        1: {"wq": [D, D], "wqp": [D, D], "wk": [D, D], "wkp": [D, D], "wv": [D, D], "wo": [D, D],
            "cos": [D, P], "sin": [D, P], "hmask": [D, 4], "gmask": [D, 4], "cmask": ([P, P], BF16)},
        2: {"wq1": [D, D], "wkv1": [D, 2, D], "wo1": [D, 2, 2, D], "wq2": [D, D], "wkv2": [D, 2, D], "wo2": [D, 2, 2, D],
            "e1": [D, 64], "d1": [64, D], "e2": [D, 64], "d2": [64, D], "bdm": [D, D], "qmask": ([P, D], BF16),
            "g1": [P, D], "b1": [P, D], "g2": [P, D], "b2": [P, D], "g3": [P, D], "b3": [P, D]},
        3: {"rw": [D, 8], "rb": [P, 8], "idx": [P, 8], "sw1": [D, 256], "sw3": [D, 256], "sw2": [P, 2, D], "ew1": [D, 8, P], "ew2": [P, 8, D]},
        4: {"lnw": [D, 1], "lnb": [D, 1], "win": [D, 512], "cw": [P, 2, 4], "cb": [P, 2], "wxd": [P, 2, 8], "wxb": [P, 2, 96], "wdt": [8, 256],
            "bdt": [P, 2], "alog": [P, 2, 16], "dp": [P, 2], "wout": [P, 2, D], "sel": ([96, 32], BF16)},
        5: {"wq": [D, D], "wk": [D, D], "wv": [D, D], "wo": [D, D], "bq": [D, 1], "bk": [D, 1], "bv": [P, D], "bo": [P, D],
            "hmask": [D, 4], "gmask": [D, 4], "amask": [P, S2], "pad": ([P, B, S2], mybir.dt.uint8)},
        6: {"gw": [D, 8], "idx": [P, 8], "ones": [P, P], "wg": [D, 8, 512], "wu": [D, 8, 512], "wd": [P, 8, 4, D]},
    }


def program(nc, dram, out):
    ctx = ExitStack()
    with ctx:
        c = Core(nc, ctx, dram)
        c.X = c.sb("X", [P, B, D])
        c.identf = c.sb("identf", [P, P])
        c.identb = c.sb("identb", [P, P], BF16)
        c.ln = {"st": c.sb("ln_st", [P, GB, 6]), "mv": c.sb("ln_mv", [P, GB, 2]), "lv": c.sb("ln_lv", [P, GB]),
                "rs": c.sb("ln_rs", [P, GB]), "half": c.sb("ln_half", [P, GB]), "eps": c.sb("ln_eps", [P, GB])}
        c.PS = ctx.enter_context(nc.psum_tensor("PS", [P, 8, 512], F32))
        plan = {ph: ws for ph, ws in plan_weights().items() if ph <= UPTO}
        Ws, sem, count = {}, {}, {}
        for ph, ws in plan.items():
            Ws[ph] = {}
            for n, sh in ws.items():
                sh, dt = sh if isinstance(sh, tuple) else (sh, F32)
                Ws[ph][n] = c.sb(f"w{ph}_{n}", sh, dt)
            sem[ph] = c.sem(f"weights{ph}")
            count[ph] = 16 * len(ws)
        s_x, s_rest = c.sem("x_loaded"), c.sem("x_rest_loaded")
        s_set = c.sem("constants_set")
        count[1] += 32

        def load(sp, ph):
            for n, t in Ws[ph].items():
                full = tuple(slice(None) for _ in t.shape)
                sp.dma_start(t[full], dram[f"w{ph}_{n}"]).then_inc(sem[ph], 16)

        def later_loads(sp):
            sp.dma_start(c.X[:, GB:B, :], dram["x"][:, GB:B, :]).then_inc(s_rest, 16)
            for ph in list(plan)[1:]:
                load(sp, ph)

        with nc.Block() as block:
            @block.sync
            def _(sp):
                sp.dma_start(c.X[:, 0:GB, :], dram["x"][:, 0:GB, :]).then_inc(s_x, 16)
                sp.dma_start(c.identf[:, :], dram["identf"]).then_inc(sem[1], 16)
                sp.dma_start(c.identb[:, :], dram["identb"]).then_inc(sem[1], 16)
                load(sp, 1)

            @block.vector
            def _(dve):
                nc.vector.memset(c.ln["eps"][:, :], EPS)
                nc.vector.memset(c.ln["half"][:, :], -0.5).then_inc(s_set, 1)

        attention(c, "a_", False, Ws[1], sem[1], count[1], (s_x, s_rest), later_loads)
        if UPTO >= 2:
            for ph in range(2, UPTO + 1):
                PHASES[ph](c, Ws[ph], sem[ph], count[ph], out)
        if UPTO < 6:
            s_out = c.sem("stored")
            with nc.Block() as block:
                @block.sync
                def _(sp):
                    sp.dma_start(out.rearrange("b p d -> p b d"), c.X[:, :, :]).then_inc(s_out, 16)
                    sp.wait_ge(s_out, 16)


def layout(a):
    f = np.float32
    bf = mybir.dt.np(BF16)
    w = {}
    w["x"] = a["x"].transpose(1, 0, 2)
    w["ctx"] = a["ctx_1024"].transpose(1, 0, 2)
    w["identf"] = np.eye(P, dtype=f)
    w["identb"] = np.eye(P).astype(bf)
    swap = np.arange(D) ^ 1
    w["w1_wq"], w["w1_wk"], w["w1_wv"], w["w1_wo"] = (a["L0_attn_" + n].T for n in ("wq", "wk", "wv", "wo"))
    w["w1_wqp"], w["w1_wkp"] = a["L0_attn_wq"].T[:, swap], a["L0_attn_wk"].T[:, swap]
    freqs = (f(1.0) / f(10000.0) ** (np.arange(0, 8, 2, dtype=f) / f(8))).astype(f)
    ang = np.outer(np.arange(P, dtype=f), freqs).astype(f)
    i = (np.arange(D) % 8) // 2
    w["w1_cos"] = np.cos(ang)[:, i].T.astype(f)
    w["w1_sin"] = (np.sin(ang)[:, i].T * np.where(np.arange(D) % 2, 1, -1)[:, None]).astype(f)
    w["w1_hmask"] = (np.arange(D)[:, None] % 32 // 8 == np.arange(4)[None, :]).astype(f)
    w["w1_gmask"] = w["w5_gmask"] = (np.arange(D)[:, None] // 32 == np.arange(4)[None, :]).astype(f)
    w["w1_cmask"] = np.where(np.arange(P)[None, :] > np.arange(P)[:, None], -BIG, 0.0).astype(bf)
    order = np.array([4 * (i % 2) + i // 2 for i in range(8)])
    head = lambda m: m[order].transpose(1, 0, 2).reshape(D, D)
    for k in (1, 2):
        w[f"w2_wq{k}"] = head(a[f"L0_xattn_Wq{k}"])
        w[f"w2_wkv{k}"] = np.stack([head(a[f"L0_xattn_Wk{k}"]), head(a[f"L0_xattn_Wv{k}"])], 1)
        wo = a[f"L0_xattn_Wo{k}"].T.reshape(4, 2, 16, D)
        z = np.zeros((4, 2, 16, 2, 2, D), f)
        for hl in (0, 1):
            for t in (0, 1):
                z[:, hl, :, hl, t, :] = wo[:, t]
        w[f"w2_wo{k}"] = z.reshape(D, 2, 2, D)
    w["w2_e1"], w["w2_d1"], w["w2_e2"], w["w2_d2"] = (a["L0_xattn_" + n].T for n in ("E1", "D1", "E2", "D2"))
    w["w2_bdm"] = (np.arange(D)[:, None] // 16 == np.arange(D)[None, :] // 16).astype(f)
    tok = np.arange(P) % 16 * 8 + np.arange(P) // 16
    w["w2_qmask"] = np.where(np.arange(D)[None, :] % 16 > tok[:, None], -BIG, 0.0).astype(bf)
    for n in ("g1", "b1", "g2", "b2", "g3", "b3"):
        w["w2_" + n] = np.tile(a["L0_xattn_" + n], (P, 1))
    w["w3_rw"] = a["L0_ffn_router_w"].T
    w["w3_rb"] = np.tile(a["L0_ffn_router_bias"], (P, 1))
    w["w3_idx"] = np.tile(np.arange(8, 0, -1, dtype=f), (P, 1))
    w["w3_sw1"], w["w3_sw3"] = a["L0_ffn_sw1"], a["L0_ffn_sw3"]
    w["w3_sw2"] = a["L0_ffn_sw2"].reshape(2, P, D).transpose(1, 0, 2)
    w["w3_ew1"], w["w3_ew2"] = a["L0_ffn_ew1"].transpose(1, 0, 2), a["L0_ffn_ew2"].transpose(1, 0, 2)
    ch = lambda m: m.reshape(2, P, -1).transpose(1, 0, 2)
    w["w4_lnw"], w["w4_lnb"] = a["L1_attn_ln_w"][:, None], a["L1_attn_ln_b"][:, None]
    w["w4_win"], w["w4_wdt"] = a["L1_attn_W_in"], a["L1_attn_W_dt"]
    w["w4_cw"] = ch(a["L1_attn_conv_w"])
    w["w4_cb"], w["w4_bdt"], w["w4_dp"] = (ch(a["L1_attn_" + n])[:, :, 0] for n in ("conv_b", "b_dt", "D_param"))
    w["w4_alog"], w["w4_wout"] = ch(a["L1_attn_A_log"]), ch(a["L1_attn_W_out"])
    wx = ch(a["L1_attn_W_xproj"])
    w["w4_wxd"], w["w4_wxb"] = wx[:, :, 0:8], np.tile(wx[:, :, 8:40], (1, 1, 3))
    w["w4_sel"] = (np.arange(96)[:, None] % 32 == np.arange(32)[None, :]).astype(bf)
    for n in ("q", "k", "v", "o"):
        w["w5_w" + n] = a["L1_xattn_W" + n].T
    w["w5_bq"], w["w5_bk"] = a["L1_xattn_bq"][:, None], a["L1_xattn_bk"][:, None]
    w["w5_bv"], w["w5_bo"] = np.tile(a["L1_xattn_bv"], (P, 1)), np.tile(a["L1_xattn_bo"], (P, 1))
    w["w5_hmask"], w["w5_amask"] = w["w1_hmask"], a["fside_SxS2_0"]
    w["w5_pad"] = np.broadcast_to(a["mask_BxS2_bf0"][None], (P, B, S2))
    w["w6_gw"], w["w6_idx"], w["w6_ones"] = a["L1_ffn_gate_W"].T, w["w3_idx"], np.ones((P, P), f)
    w["w6_wg"], w["w6_wu"] = (a["L1_ffn_W_" + n].transpose(2, 0, 1) for n in ("gate", "up"))
    w["w6_wd"] = a["L1_ffn_W_down"].transpose(2, 0, 1).reshape(4, P, 8, D).transpose(1, 2, 0, 3)
    return w


def kernel(**inputs):
    import concourse.bacc as _bacc
    from concourse.bass_utils import run_bass_kernel_spmd as _run

    a = {k: np.asarray(v) for k, v in inputs.items()}
    lay = layout(a)
    need = ["x", "ctx", "identf", "identb"] + [f"w{ph}_{n}" for ph, ws in plan_weights().items() for n in ws]
    nc = _bacc.Bacc("TRN2", target_bir_lowering=False, num_devices=1)
    arrays, dram = {}, {}
    for name in need:
        v = np.ascontiguousarray(lay[name])
        arrays[f"in_{name}"] = v
        dram[name] = nc.dram_tensor(f"in_{name}", v.shape, mybir.dt.from_np(v.dtype), kind="ExternalInput").ap()
    out = nc.dram_tensor("out_0_dram", (B, P, D), F32, kind="ExternalOutput").ap()
    program(nc, dram, out)
    r = _run(nc, [arrays], core_ids=[0])
    return r.results[0]["out_0_dram"]
```

```python
from contextlib import ExitStack

import concourse.bass as bass
import numpy as np
from concourse import mybir

F32 = mybir.dt.float32
BF16 = mybir.dt.bfloat16
ALU = mybir.AluOpType
ACT = mybir.ActivationFunctionType
AX_X = mybir.AxisListType.X

P = 128
B = 32
D = 128
GB = 4
NG = B // GB
T = GB * P
S2 = 77
EPS = 1e-5
BIG = 1e30
UPTO = 6


class Core:

    def __init__(self, nc, ctx, dram):
        self.nc, self.ctx, self.dram, self.phase = nc, ctx, dram, []

    def sb(self, name, shape, dt=F32, ctx=None):
        return (ctx or self.ctx).enter_context(self.nc.sbuf_tensor(name, shape, dt))

    def sem(self, name):
        return self.ctx.enter_context(self.nc.semaphore(name))

    def sems(self, prefix, names):
        made = {n: self.nc.alloc_semaphore(name=prefix + n) for n in names.split()}
        self.phase += made.values()
        return made

    def end_phase(self, ctx):
        ctx.close()
        self.nc.clear_and_free_semaphores(self.phase)
        self.nc.all_engine_barrier()
        self.phase = []


def group(c, g):
    return c.X[:, bass.ds(g * GB, GB), :]


def flat(ap):
    return ap.rearrange("p b d -> p (b d)")



def ln_stats(dve, nc, src, ln, s, n):
    for b in range(GB):
        ins = nc.vector.bn_stats(ln["st"][:, b, :], src[:, b, :])
    dve.drain()
    for b in range(GB):
        ins = nc.vector.bn_aggr(ln["mv"][:, b, :], ln["st"][:, b, :])
    ins.then_inc(s["mv"], 1)


def ln_rstd(pool, nc, ln, s, n):
    pool.wait_ge(s["mv"], n)
    nc.gpsimd.tensor_tensor(ln["lv"][:, :], ln["mv"][:, :, 1], ln["eps"][:, :], ALU.add).then_inc(s["lv"], 1)
    pool.wait_ge(s["lv"], n)
    nc.gpsimd.tensor_tensor(ln["rs"][:, :], ln["lv"][:, :], ln["half"][:, :], ALU.pow).then_inc(s["rs"], 1)


def ln_apply(dve, nc, out, src, ln, s, n, done):
    dve.wait_ge(s["rs"], n)
    for b in range(GB):
        ins = nc.vector.tensor_scalar(out[:, b, :], src[:, b, :], ln["mv"][:, b, 0:1], ln["rs"][:, b:b + 1],
                                      ALU.subtract, ALU.mult)
    ins.then_inc(done, 1)


LN_SEMS = "st mv lv rs"


def pipeline(eng, slot, shift, n, setup, early, prepare, step, end):
    def body(g, par, left):
        for i in range(shift, n):
            step(g, par, i, left)
            for name, stage in prepare.items():
                if left and slot[name] == i:
                    stage(g + 1, 1 - par)
            for name, stage in early.items():
                if left == 2 and slot[name] == i:
                    stage(g + 2, par)
        for i in range(shift):
            if left:
                step(g + 1, 1 - par, i, left)
            for name, stage in end.items():
                if slot[name] == i:
                    stage(g, par)

    setup()
    for stages, g in ((early, 0), (prepare, 0), (early, 1)):
        for stage in stages.values():
            stage(g, g)
    for i in range(shift):
        step(0, 0, i, 2)
    with eng.Fori(0, NG // 2 - 1) as k:
        body(k * 2, 0, 2)
        body(k * 2 + 1, 1, 2)
    body(NG - 2, 0, 1)
    body(NG - 1, 1, 0)



def attention(c, tag, cross, W, wsem, wcount, xsem=None, loads=None):
    nc, X, PS = c.nc, c.X, c.PS
    H, DH, HG = 16, 8, 4
    KL = S2 if cross else P
    HU = 8
    UN = 2 * GB
    VB = HG * (32 + DH)
    SCALE = DH ** -0.5
    s = c.sems(tag, "xs xTp xT kp rot qs q k bd vp v z s_ready mx ma d e sm rr ex rTp ptp pt o_ready oT yp yr y2 xw cs cTp cT am rc amg " + LN_SEMS)
    ctx = ExitStack()
    sb = lambda n, sh, dt=F32: c.sb(tag + n, sh, dt, ctx)
    Xs = sb("Xs", [P, GB, D])
    xT = sb("xT", [D, T])
    QM = sb("QM", [D, 2, 4, T])
    kT = sb("kT", [D, GB, KL])
    BD = sb("BD", [D, 2, HG, GB, KL])
    V = sb("V", [KL, 2, GB * 4, VB])
    R = sb("R", [D, 4, T])
    DD = sb("DD", [P, 2, HU, KL])
    E = sb("E", [P, 2, HU, KL])
    PT = sb("PT", [KL, 2, HU, P])
    mx = sb("mx", [P, 2, HU])
    sm = sb("sm", [P, GB * H])
    rr = sb("rr", [P, GB * H])
    rx = sb("rx", [P, GB, D])
    rT = sb("rT", [D, T])
    one = sb("one", [P, 1])
    oT = sb("oT", [D, T])
    Y = sb("Y", [P, GB, D])
    if not cross:
        qT = sb("qT", [D, T])
    if cross:
        bqm = sb("bqm", [D, 4])
        XB = sb("XB", [P, GB, D])
        Cs = sb("Cs", [S2, GB, D])
        cT = sb("cT", [D, GB, S2])
        am8 = sb("am8", [P, S2])
        padr = sb("padr", [P, B, S2])
        am = sb("am", [P, 2, GB, S2])
    ln = c.ln

    AUX, OUT = 7, 6

    def bank(i, rows=P, n=512):
        return PS[0:rows, i, 0:n]

    def scores(gp):
        return PS[:, gp, 0:HG * KL].rearrange("p (j k) -> p j k", j=HG)

    def units(hf):
        return PS[:, 2 * hf:2 * hf + 2, 0:HG * KL].rearrange("p i (j k) -> p i j k", j=HG)

    def schedule(eng, prelude, body):
        prelude()
        with eng.Fori(0, NG // 2 - 1) as i:
            body(i * 2, 0, 2)
            body(i * 2 + 1, 1, 2)
        body(NG - 2, 0, 1)
        body(NG - 1, 1, 0)

    with nc.Block() as block:

        @block.sync
        def _(sp):
            if loads is not None:
                loads(sp)
            if cross:
                sp.dma_start(Cs[:, :, :], c.dram["ctx"][:, 0:GB, :]).then_inc(s["cs"], 16)
                with sp.Fori(1, NG) as g:
                    sp.wait_ge(s["cTp"], g)
                    sp.dma_start(Cs[:, :, :], c.dram["ctx"][:, bass.ds(g * GB, GB), :]).then_inc(s["cs"], 16)

        @block.gpsimd
        def _(pool):

            def rows(g):
                nc.gpsimd.tensor_copy(Xs[:, :, :], group(c, g)).then_inc(s["xs"], 1)

            def keys(g, par):
                if cross:
                    nc.gpsimd.tensor_tensor(am[:, par], padr[:, bass.ds(g * GB, GB), :], am8[:, :].rearrange("p (o k) -> p o k", o=1).to_broadcast([P, GB, S2]), ALU.add).then_inc(s["amg"], 1)
                    pool.wait_ge(s["k"], g + 1)
                else:
                    pool.wait_ge(s["rot"], g * 4 + 2)
                    nc.gpsimd.tensor_tensor(flat(kT[:, :, :]), R[:, 0, :], R[:, 1, :], ALU.add).then_inc(s["k"], 1)
                    pool.wait_ge(s["k"], g + 1)
                for j in range(HG):
                    nc.gpsimd.tensor_tensor(flat(BD[:, par, j]), flat(kT[:, :, :]), W["hmask"][:, j:j + 1].to_broadcast([D, GB * KL]), ALU.mult).then_inc(s["bd"], 1)
                if not cross:
                    pool.wait_ge(s["rot"], g * 4 + 4)
                    nc.gpsimd.tensor_tensor(qT[:, :], R[:, 2, :], R[:, 3, :], ALU.add).then_inc(s["qs"], 1)

            def prelude():
                nc.gpsimd.memset(one[:, :], 1.0).then_inc(s["z"], 1)
                nc.gpsimd.memset(V[:, :, :, :], 0.0).then_inc(s["z"], 1)
                pool.wait_ge(s["z"], 1)
                if xsem is not None:
                    pool.wait_ge(xsem[0], 16)
                rows(0)
                pool.wait_ge(wsem, wcount)
                if cross:
                    nc.gpsimd.tensor_scalar(am8[:, :], W["amask"][:, :], float(np.sqrt(DH)), 0.0, ALU.mult, ALU.add).then_inc(s["am"], 1)
                    nc.gpsimd.tensor_scalar(padr[:, :, :], W["pad"][:, :, :], -BIG, 0.0, ALU.mult, ALU.add).then_inc(s["am"], 1)
                    nc.gpsimd.tensor_tensor(bqm[:, :], W["gmask"][:, :], W["bq"][:, :].to_broadcast([D, 4]), ALU.mult).then_inc(s["am"], 1)
                    pool.wait_ge(s["am"], 2)
                keys(0, 0)
                if xsem is not None:
                    pool.wait_ge(xsem[1], 16)
                pool.wait_ge(s["xTp"], 1)
                rows(1)

            def body(g, par, left):
                if left:
                    if left == 2:
                        pool.wait_ge(s["xTp"], g + 2)
                        rows(g + 2)
                    keys(g + 1, 1 - par)
                if cross:
                    nc.gpsimd.tensor_tensor(XB[:, :, :], group(c, g), W["bo"][:, :].rearrange("p (o d) -> p o d", o=1).to_broadcast([P, GB, D]), ALU.add).then_inc(s["y2"], 1)
                pool.wait_ge(s["rr"], g + 1)
                nc.gpsimd.tensor_tensor(rx[:, :, :].rearrange("p b (h d) -> p (b h) d", d=DH), rr[:, :].rearrange("p (m o) -> p m o", o=1).to_broadcast([P, GB * H, DH]),
                                        one[:, :].rearrange("p (m o) -> p m o", o=1).to_broadcast([P, GB * H, DH]), ALU.mult).then_inc(s["ex"], 1)
                ln_rstd(pool, nc, ln, s, g + 1)

            schedule(pool, prelude, body)

        @block.scalar
        def _(act):

            def exps(g, u):
                act.wait_ge(s["d"], g * UN + u + 1)
                nc.scalar.activation(E[:, u % 2], DD[:, u % 2], ACT.Exp, scale=SCALE).then_inc(s["e"], 1)

            def x_transposed(g):
                act.wait_ge(s["xTp"], g + 1)
                nc.scalar.copy(xT[:, :], bank(AUX)).then_inc(s["xT"], 1)

            def values(g, par):
                act.wait_ge(s["vp"], g + 1)
                nc.scalar.copy(V[:, par].rearrange("p m (j c) -> p m j c", c=32 + DH)[:, :, :, 0:DH], bank(AUX).rearrange("p (m j d) -> p m j d", j=HG, d=DH)).then_inc(s["v"], 1)

            def context(g):
                act.wait_ge(s["cTp"], g + 1)
                nc.scalar.copy(flat(cT[:, :, :]), bank(AUX, D, GB * S2)).then_inc(s["cT"], 1)

            def keys(g):
                act.wait_ge(s["kp"], g * 2 + 1)
                act.wait_ge(s["bd"], g * HG)
                nc.scalar.activation(flat(kT[:, :, :]), bank(AUX, D, GB * S2), ACT.Identity, bias=W["bk"][:, 0:1]).then_inc(s["k"], 1)

            def queries(g, par):
                if cross:
                    act.wait_ge(s["kp"], g * 2 + 2)
                else:
                    act.wait_ge(s["qs"], g + 1)
                for gp in range(4):
                    if cross:
                        ins = nc.scalar.activation(QM[:, par, gp, :], bank(AUX), ACT.Identity, scale=W["gmask"][:, gp:gp + 1], bias=bqm[:, gp:gp + 1])
                    else:
                        ins = nc.scalar.activation(QM[:, par, gp, :], qT[:, :], ACT.Copy, scale=W["gmask"][:, gp:gp + 1])
                ins.then_inc(s["q"], 1)

            def first_keys():
                act.wait_ge(s["kp"], 1)
                nc.scalar.activation(flat(kT[:, :, :]), bank(AUX, D, GB * S2), ACT.Identity, bias=W["bk"][:, 0:1]).then_inc(s["k"], 1)

            def slot(g, u, left):
                act.wait_ge(s["ptp"], g * UN + u + 1)
                act.wait_ge(s["o_ready"], g * UN + (u if u else 0))
                nc.scalar.copy(PT[:, u % 2], PS[0:KL, 4:6, :].rearrange("p i (h q) -> p (i h) q", q=P)).then_inc(s["pt"], 1)
                if u + 1 < UN or left:
                    act.wait_ge(s["sm"], g * UN + u)
                    exps(g + (u + 1) // UN, (u + 1) % UN)

            def prelude():
                act.wait_ge(wsem, wcount)
                act.sem_inc(s["o_ready"], 1)
                act.wait_ge(s["z"], 2)
                x_transposed(0)
                if cross:
                    context(0)
                    act.wait_ge(s["am"], 3)
                    first_keys()
                    queries(0, 0)
                else:
                    values(0, 0)
                    queries(0, 0)
                exps(0, 0)
                act.wait_ge(s["ptp"], 1)
                nc.scalar.copy(PT[:, 0], PS[0:KL, 4:6, :].rearrange("p i (h q) -> p (i h) q", q=P)).then_inc(s["pt"], 1)
                exps(0, 1)
                x_transposed(1)

            def body(g, par, left):
                for u in range(1, UN):
                    slot(g, u, left)
                    if left:
                        if cross:
                            if u == 1:
                                context(g + 1)
                            if u == 2:
                                keys(g + 1)
                            if u == 3:
                                queries(g + 1, 1 - par)
                        elif u == 5:
                            queries(g + 1, 1 - par)
                        elif u == 6:
                            values(g + 1, 1 - par)
                act.wait_ge(s["rTp"], g + 1)
                nc.scalar.copy(rT[:, :], bank(AUX)).then_inc(s["rc"], 1)
                if left:
                    slot(g + 1, 0, left)
                if left == 2:
                    x_transposed(g + 2)

            schedule(act, prelude, body)

        @block.vector
        def _(dve):

            def less_max(g, par, u):
                hf, b = u % 2, u // 2
                at = g * UN + u + 1
                d = DD[:, u % 2].rearrange("p (i j) k -> p i j k", i=2)
                m = mx[:, u % 2, :].rearrange("p (i j) -> p i j", i=2)
                mb = mx[:, u % 2, :].rearrange("p (i j o) -> p i j o", i=2, o=1).to_broadcast([P, 2, HG, KL])
                dve.wait_ge(s["s_ready"], at)
                if not (isinstance(g, int) and g == 0 and u < 2):
                    dve.wait_ge(s["e"], at - 2)
                if cross:
                    if u == 0:
                        dve.wait_ge(s["amg"], g + 1)
                    amb = am[:, par, b, :].rearrange("p (i j k) -> p i j k", i=1, j=1).to_broadcast([P, 2, HG, KL])
                    nc.vector.tensor_tensor(d, units(hf), amb, ALU.add).then_inc(s["ma"], 1)
                    dve.wait_ge(s["ma"], at)
                    nc.vector.tensor_reduce(m, d, AX_X, ALU.max).then_inc(s["mx"], 1)
                    dve.wait_ge(s["mx"], at)
                    nc.vector.tensor_tensor(d, d, mb, ALU.subtract).then_inc(s["d"], 1)
                else:
                    nc.vector.tensor_reduce(m, units(hf), AX_X, ALU.max).then_inc(s["mx"], 1)
                    dve.wait_ge(s["mx"], at)
                    nc.vector.tensor_tensor(d, units(hf), mb, ALU.subtract).then_inc(s["d"], 1)

            def sums(g, u):
                dve.wait_ge(s["e"], g * UN + u + 1)
                nc.vector.tensor_reduce(sm[:, u * HU:(u + 1) * HU], E[:, u % 2], AX_X, ALU.add).then_inc(s["sm"], 1)

            def rotate(g, i):
                f4 = W["cos" if i % 2 == 0 else "sin"][:, :].rearrange("p (o k) -> p o k", o=1).to_broadcast([D, GB, P])
                t4 = lambda ap: ap.rearrange("p (b k) -> p b k", b=GB)
                dve.wait_ge(s["kp"], g * 4 + i + 1)
                nc.vector.tensor_tensor(t4(R[:, i, :]), t4(bank(AUX)), f4, ALU.mult).then_inc(s["rot"], 1)

            def values(g, par):
                dve.wait_ge(s["vp"], g + 1)
                for b in range(GB):
                    ins = nc.vector.tensor_tensor(V[:, par, 4 * b:4 * b + 4].rearrange("p m (j c) -> p m j c", c=32 + DH)[:, :, :, 0:DH],
                                                  PS[0:KL, AUX, b * D:(b + 1) * D].rearrange("p (m j d) -> p m j d", j=HG, d=DH),
                                                  W["bv"][0:KL, :].rearrange("p (m j d) -> p m j d", j=HG, d=DH), ALU.add)
                ins.then_inc(s["v"], 1)

            def prelude():
                dve.wait_ge(wsem, wcount)
                dve.wait_ge(s["z"], 2)
                if xsem is not None:
                    dve.wait_ge(xsem[0], 16)
                    dve.wait_ge(xsem[1], 16)
                if cross:
                    values(0, 0)
                else:
                    for i in range(4):
                        rotate(0, i)
                less_max(0, 0, 0)
                less_max(0, 0, 1)
                sums(0, 0)
                less_max(0, 0, 2)
                sums(0, 1)
                if not cross:
                    rotate(1, 0)

            def body(g, par, left):
                for u in range(2, UN):
                    if u + 1 < UN:
                        less_max(g, par, u + 1)
                        sums(g, u)
                    else:
                        sums(g, u)
                        dve.wait_ge(s["sm"], g * UN + UN)
                        nc.vector.reciprocal(rr[:, :], sm[:, :]).then_inc(s["rr"], 1)
                        if left:
                            less_max(g + 1, 1 - par, 0)
                    if left:
                        if cross:
                            if u == 4:
                                values(g + 1, 1 - par)
                        elif u <= 4:
                            rotate(g + 1, u - 1)
                dve.wait_ge(s["rc"], g + 1)
                dve.wait_ge(s["o_ready"], g * UN + UN + 1)
                nc.vector.tensor_tensor(oT[:, :], bank(OUT), rT[:, :], ALU.mult).then_inc(s["oT"], 1)
                if left:
                    less_max(g + 1, 1 - par, 1)
                    dve.wait_ge(s["rr"], g + 1)
                    sums(g + 1, 0)
                dve.wait_ge(s["yp"], g + 1)
                if cross:
                    dve.wait_ge(s["y2"], g + 1)
                nc.vector.tensor_tensor(flat(Y[:, :, :]), bank(AUX), flat(XB[:, :, :] if cross else group(c, g)), ALU.add).then_inc(s["yr"], 1)
                dve.wait_ge(s["yr"], g + 1)
                ln_stats(dve, nc, Y, ln, s, g + 1)
                if left:
                    less_max(g + 1, 1 - par, 2)
                    sums(g + 1, 1)
                    if left == 2 and not cross:
                        rotate(g + 2, 0)
                ln_apply(dve, nc, group(c, g), Y, ln, s, g + 1, s["xw"])

            schedule(dve, prelude, body)

        @block.tensor
        def _(pe):

            def transpose_x(g):
                pe.wait_ge(s["xs"], g + 1)
                for b in range(GB):
                    ins = nc.tensor.transpose(PS[:, AUX, b * P:(b + 1) * P], Xs[:, b, :], c.identf[:, :])
                ins.then_inc(s["xTp"], 1)

            def transpose_context(g):
                pe.wait_ge(s["cs"], g * 16 + 16)
                pe.wait_ge(s["xT"], g + 1)
                for b in range(GB):
                    ins = nc.tensor.transpose(PS[0:D, AUX, b * S2:(b + 1) * S2], Cs[:, b, :], c.identf[0:S2, 0:S2])
                ins.then_inc(s["cTp"], 1)

            def project(g, i):
                if cross:
                    if i == 0:
                        pe.wait_ge(s["cT"], g + 1)
                        nc.tensor.matmul(bank(AUX, D, GB * S2), W["wk"][:, :], flat(cT[:, :, :]), start=True, stop=True).then_inc(s["kp"], 1)
                    else:
                        pe.wait_ge(s["k"], g + 1)
                        nc.tensor.matmul(bank(AUX), W["wq"][:, :], xT[:, :], start=True, stop=True).then_inc(s["kp"], 1)
                else:
                    if i == 0:
                        pe.wait_ge(s["xT"], g + 1)
                    else:
                        pe.wait_ge(s["rot"], g * 4 + i)
                    nc.tensor.matmul(bank(AUX), W[("wk", "wkp", "wq", "wqp")[i]][:, :], xT[:, :], start=True, stop=True).then_inc(s["kp"], 1)

            def project_values(g):
                if cross:
                    pe.wait_ge(s["q"], g + 1)
                else:
                    pe.wait_ge(s["rot"], g * 4 + 4)
                for b in range(GB):
                    src = cT[:, b, :] if cross else xT[:, b * P:(b + 1) * P]
                    ins = nc.tensor.matmul(PS[0:KL, AUX, b * D:(b + 1) * D], src, W["wv"][:, :], start=True, stop=True)
                ins.then_inc(s["vp"], 1)

            def score(g, par, u):
                hf, b = u % 2, u // 2
                if u == 0:
                    pe.wait_ge(s["q"], g + 1)
                    pe.wait_ge(s["bd"], g * HG + HG)
                if not (isinstance(g, int) and g == 0 and u < 2):
                    pe.wait_ge(s["d"], g * UN + u - 1)
                for gp in (2 * hf, 2 * hf + 1):
                    ins = nc.tensor.matmul(scores(gp), QM[:, par, gp, b * P:(b + 1) * P], BD[:, par, :, b, :], start=True, stop=cross)
                if not cross:
                    for gp in (2 * hf, 2 * hf + 1):
                        ins = nc.tensor.matmul(scores(gp), c.identb[:, :], W["cmask"][:, :].rearrange("p (o k) -> p o k", o=1).to_broadcast([P, HG, P]),
                                               start=False, stop=True)
                ins.then_inc(s["s_ready"], 1)

            def transpose_p(g, u):
                pe.wait_ge(s["e"], g * UN + u + 1)
                for h in range(HU):
                    ins = nc.tensor.transpose(PS[0:KL, 4 + h // 4, (h % 4) * P:(h % 4 + 1) * P], E[:, u % 2, h, :], c.identf[:, :])
                ins.then_inc(s["ptp"], 1)

            def outputs(g, par, u):
                hf, b = u % 2, u // 2
                pe.wait_ge(s["pt"], g * UN + u + 1)
                if u == 0:
                    pe.wait_ge(s["v"], g + 1)
                for h in range(HU):
                    gp, j = 2 * hf + h // HG, h % HG
                    ins = nc.tensor.matmul(PS[32 * gp:32 * gp + 32, OUT, b * P:(b + 1) * P], V[:, par, b * 4 + gp, 32 * j:32 * j + 32], PT[:, u % 2, h, :],
                                           start=(j == 0), stop=(j == HG - 1))
                ins.then_inc(s["o_ready"], 1)

            def prelude():
                pe.wait_ge(wsem, wcount)
                transpose_x(0)
                if cross:
                    transpose_context(0)
                for i in range(2 if cross else 4):
                    project(0, i)
                project_values(0)
                score(0, 0, 0)
                score(0, 0, 1)
                transpose_p(0, 0)
                score(0, 0, 2)
                outputs(0, 0, 0)
                transpose_x(1)

            def body(g, par, left):
                for u in range(1, UN):
                    pe.wait_ge(s["pt"], g * UN + u)
                    transpose_p(g, u)
                    if u + 2 < UN:
                        score(g, par, u + 2)
                    elif left:
                        score(g + 1, 1 - par, u + 2 - UN)
                    if left:
                        if cross:
                            if u == 1:
                                transpose_context(g + 1)
                            if u in (2, 3):
                                project(g + 1, u - 2)
                            if u == 4:
                                project_values(g + 1)
                        elif u <= 4:
                            project(g + 1, u - 1)
                        elif u == 5:
                            project_values(g + 1)
                    if u == UN - 1:
                        pe.wait_ge(s["ex"], g + 1)
                        if left:
                            pe.wait_ge(s["v"], g + 2)
                        for b in range(GB):
                            ins = nc.tensor.transpose(PS[:, AUX, b * P:(b + 1) * P], rx[:, b, :], c.identf[:, :])
                        ins.then_inc(s["rTp"], 1)
                    outputs(g, par, u)
                if left:
                    pe.wait_ge(s["pt"], g * UN + UN)
                    transpose_p(g + 1, 0)
                    score(g + 1, 1 - par, 2)
                pe.wait_ge(s["oT"], g + 1)
                for b in range(GB):
                    ins = nc.tensor.matmul(PS[:, AUX, b * D:(b + 1) * D], oT[:, b * P:(b + 1) * P], W["wo"][:, :], start=True, stop=True)
                ins.then_inc(s["yp"], 1)
                if left:
                    outputs(g + 1, 1 - par, 0)
                if left == 2:
                    pe.wait_ge(s["yr"], g + 1)
                    transpose_x(g + 2)

            schedule(pe, prelude, body)
    c.end_phase(ctx)


PHASES = {}



def linear_attention_block(c, W, wsem, wcount, out):
    nc, X, PS = c.nc, c.X, c.PS
    H, DH, HID = 8, 16, 128
    W8 = 8
    W16 = P // W8
    KL = {1: P, 2: S2}
    LANES = 2
    NI = NG // LANES
    ctx = ExitStack()
    row = lambda ap: ap.rearrange("p (o d) -> p o d", o=1).to_broadcast([P, GB, D])
    bd = lambda ap: ap.rearrange("p (b d) -> p b d", b=GB)
    heads = lambda ap: ap.rearrange("p b (h d) -> p (b h) d", h=H)
    each = lambda ap, n: ap.rearrange("p (m o) -> p m o", o=1).to_broadcast([n, GB * H, DH])

    class Lane:

        def __init__(self, i):
            sb = lambda n, sh, dt=F32: c.sb(f"x{i}_" + n, sh, dt, ctx)
            self.i = i
            self.s = c.sems(f"x{i}_", "ys cs cTp cT yTp yT q kv vs mx d e sm rc pk pq a bda sTp sT bm tt o y2 n b "
                            "d1 hs d2 x " + LN_SEMS)
            self.Y = sb("Y", [P, GB, D])
            self.Y2 = sb("Y2", [P, GB, D])
            self.YT = sb("YT", [D, T])
            self.Cs = sb("Cs", [S2, GB, D])
            self.cT = sb("cT", [D, GB, S2])
            self.DD = sb("DD", [P, 2, GB, D])
            self.E = sb("E", [P, 2, GB, D])
            self.mx = sb("mx", [P, 2, GB * H])
            self.sm = sb("sm", [P, 2, GB * H])
            self.V = sb("V", [P, GB, D])
            self.BDA = sb("BDA", [D, GB, D])
            self.sT = sb("sT", [D, T])
            self.TT = sb("TT", [P, 2, GB * 4, W16])
            self.hs = sb("hs", [HID, T])
            self.ln = {k: (v if k in ("half", "eps") else sb("ln_" + k, v.shape)) for k, v in c.ln.items()}

        def bank(self, k, r=P):
            return PS[0:r, 4 * self.i + k, :]

        def part(self, k, r, b, n=D):
            return PS[r, 4 * self.i + k, b * n:(b + 1) * n]

    lanes = [Lane(i) for i in range(LANES)]
    wp, ws = c.sems("x_", "wp ws").values()
    M = c.sb("x_M", [D, 2, HID], F32, ctx)

    def run(eng, setup, stages):
        setup()
        with eng.Fori(0, NI) as g:
            for stage in stages:
                for L in lanes:
                    stage(L, g)

    with nc.Block() as block:

        @block.sync
        def _(sp):
            for L in lanes:
                sp.dma_start(L.Cs[:, :, :], c.dram["ctx"][:, L.i * GB:(L.i + 1) * GB, :]).then_inc(L.s["cs"], 16)
            with sp.Fori(1, NI) as g:
                for L in lanes:
                    sp.wait_ge(L.s["cTp"], g)
                    sp.dma_start(L.Cs[:, :, :], c.dram["ctx"][:, bass.ds((g * LANES + L.i) * GB, GB), :]).then_inc(L.s["cs"], 16)

        @block.gpsimd
        def _(pool):

            def keys(k):
                def stage(L, g):
                    K = KL[k]
                    pool.wait_ge(L.s["rc"], g * 2 + k)
                    nc.gpsimd.tensor_tensor(heads(L.DD[0:K, 1]), heads(L.E[0:K, 1]), each(L.sm[0:K, 1, :], K), ALU.mult).then_inc(L.s["pk"], 1)
                return stage

            def rstd(k):
                def stage(L, g):
                    ln_rstd(pool, nc, L.ln, L.s, g * 4 + k)
                return stage

            def setup():
                for L in lanes:
                    nc.gpsimd.tensor_copy(L.Y[:, :, :], X[:, L.i * GB:(L.i + 1) * GB, :]).then_inc(L.s["ys"], 1)

            def rows(L, g):
                pool.wait_ge(L.s["y2"], g * 4 + 4)
                nc.gpsimd.tensor_copy(L.Y[:, :, :], group(c, g * LANES + (L.i + LANES))).then_inc(L.s["ys"], 1)

            stages = [keys(1), rstd(1), keys(2), rstd(2), rstd(3)]
            setup()
            with pool.Fori(0, NI - 1) as g:
                for stage in stages + [rows, rstd(4)]:
                    for L in lanes:
                        stage(L, g)
            for stage in stages + [rstd(4)]:
                for L in lanes:
                    stage(L, NI - 1)

        @block.scalar
        def _(act):

            def setup():
                act.wait_ge(wsem, wcount)
                act.wait_ge(wp, 2)
                nc.scalar.copy(M[:, :, :], PS[:, 0, 0:2 * D].rearrange("p (i d) -> p i d", i=2)).then_inc(ws, 1)

            def context(L, g):
                act.wait_ge(L.s["cTp"], g + 1)
                nc.scalar.copy(flat(L.cT[:, :, :]), L.bank(2)[:, 0:GB * S2]).then_inc(L.s["cT"], 1)

            def y_transposed(k):
                def stage(L, g):
                    act.wait_ge(L.s["yTp"], g * 3 + k)
                    if k < 3:
                        nc.scalar.copy(L.YT[:, :].rearrange("p (b w a) -> p b w a", b=GB, w=W8), L.bank(3).rearrange("p (b a w) -> p b w a", b=GB, w=W8)).then_inc(L.s["yT"], 1)
                    else:
                        nc.scalar.copy(L.YT[:, :], L.bank(3)).then_inc(L.s["yT"], 1)
                return stage

            def values(k):
                def stage(L, g):
                    act.wait_ge(L.s["kv"], g * 2 + k)
                    nc.scalar.copy(flat(L.V[0:KL[k], :, :]), L.bank(2, KL[k])).then_inc(L.s["vs"], 1)
                return stage

            def exps(k, i):
                def stage(L, g):
                    n = P if i == 0 else KL[k]
                    act.wait_ge(L.s["d"], g * 4 + (2 * k + i - 1))
                    nc.scalar.activation(flat(L.E[0:n, i]), flat(L.DD[0:n, i]), ACT.Exp, scale=DH ** -0.25).then_inc(L.s["e"], 1)
                return stage

            def softmax_transposed(k):
                def stage(L, g):
                    act.wait_ge(L.s["sTp"], g * 2 + k)
                    nc.scalar.copy(L.sT[:, :], L.bank(3)).then_inc(L.s["sT"], 1)
                return stage

            def hidden(L, g):
                act.wait_ge(L.s["d1"], g + 1)
                nc.scalar.activation(L.hs[:, :], L.bank(1), ACT.Silu).then_inc(L.s["hs"], 1)

            attend = lambda k: [y_transposed(k), exps(k, 0), exps(k, 1), values(k), softmax_transposed(k)]
            run(act, setup, [context] + attend(1) + attend(2) + [y_transposed(3), hidden])

        @block.vector
        def _(dve):

            def less_max(k, i):
                def stage(L, g):
                    n = P if i == 0 else KL[k]
                    at = g * 4 + (2 * k + i - 1)
                    src = L.bank(i, n).rearrange("p (m d) -> p m d", d=DH)
                    dve.wait_ge(L.s["q" if i == 0 else "kv"], g * 2 + k)
                    nc.vector.tensor_reduce(L.mx[0:n, i, :], src, AX_X, ALU.max).then_inc(L.s["mx"], 1)
                    dve.wait_ge(L.s["mx"], at)
                    nc.vector.tensor_tensor(heads(L.DD[0:n, i]), src, each(L.mx[0:n, i, :], n), ALU.subtract).then_inc(L.s["d"], 1)
                return stage

            def sums(k):
                def stage(L, g):
                    K = KL[k]
                    for i, n in ((0, P), (1, K)):
                        dve.wait_ge(L.s["e"], g * 4 + (2 * k + i - 1))
                        nc.vector.tensor_reduce(L.mx[0:n, i, :], heads(L.E[0:n, i]), AX_X, ALU.add).then_inc(L.s["sm"], 1)
                    dve.wait_ge(L.s["sm"], g * 4 + 2 * k)
                    if K < P:
                        nc.vector.reciprocal(L.sm[:, 0, :], L.mx[:, 0, :])
                    nc.vector.reciprocal(L.sm[0:K, 1, :] if K < P else L.sm[:, :, :], L.mx[0:K, 1, :] if K < P else L.mx[:, :, :]).then_inc(L.s["rc"], 1)
                    dve.wait_ge(L.s["rc"], g * 2 + k)
                    nc.vector.tensor_tensor(heads(L.DD[:, 0]), heads(L.E[:, 0]), each(L.sm[:, 0, :], P), ALU.mult).then_inc(L.s["pq"], 1)
                return stage

            def diagonal(k):
                def stage(L, g):
                    dve.wait_ge(L.s["a"], g * 2 + k)
                    nc.vector.tensor_tensor(L.BDA[:, :, :], bd(L.bank(2)), row(W["bdm"][:, :]), ALU.mult).then_inc(L.s["bda"], 1)
                return stage

            def reshape(k):
                def stage(L, g):
                    dve.wait_ge(L.s["bm"], g * 2 + k)
                    nc.vector.transpose(L.TT[:, :, :, :].rearrange("p w m a -> p m w a"), L.bank(0).rearrange("p (m w a) -> p m w a", w=2, a=W16)).then_inc(L.s["tt"], 1)
                return stage

            def residual(k, done, bk):
                def stage(L, g):
                    dve.wait_ge(L.s[done], g * (1 if k == 3 else 2) + (1 if k == 3 else k))
                    nc.vector.tensor_tensor(flat(L.Y2[:, :, :]), L.bank(bk), flat(L.Y[:, :, :]), ALU.add).then_inc(L.s["y2"], 1)
                    dve.wait_ge(L.s["y2"], g * 4 + k)
                    ln_stats(dve, nc, L.Y2, L.ln, L.s, g * 4 + k)
                return stage

            def post_norm(k):
                def stage(L, g):
                    dve.wait_ge(L.s["mv"], g * 4 + k)
                    for b in range(GB):
                        ins = nc.vector.scalar_tensor_tensor(L.Y2[:, b, :], L.Y2[:, b, :], L.ln["mv"][:, b, 0:1], W[f"g{k}"][:, :], ALU.subtract, ALU.mult)
                    ins.then_inc(L.s["n"], 1)
                    dve.wait_ge(L.s["n"], g * 3 + k)
                    dve.wait_ge(L.s["rs"], g * 4 + k)
                    for b in range(GB):
                        ins = nc.vector.scalar_tensor_tensor(L.Y[:, b, :], L.Y2[:, b, :], L.ln["rs"][:, b:b + 1], W[f"b{k}"][:, :], ALU.mult, ALU.add)
                    ins.then_inc(L.s["b"], 1)
                return stage

            def outer_sum(L, g):
                dve.wait_ge(L.s["b"], g * 3 + 3)
                nc.vector.tensor_tensor(L.Y2[:, :, :], L.Y[:, :, :], group(c, g * LANES + L.i), ALU.add).then_inc(L.s["y2"], 1)
                dve.wait_ge(L.s["y2"], g * 4 + 4)
                ln_stats(dve, nc, L.Y2, L.ln, L.s, g * 4 + 4)

            def outer_norm(L, g):
                ln_apply(dve, nc, group(c, g * LANES + L.i), L.Y2, L.ln, L.s, g * 4 + 4, L.s["x"])

            attend = lambda k: [less_max(k, 0), less_max(k, 1), sums(k), diagonal(k), reshape(k), residual(k, "o", 1), post_norm(k)]
            run(dve, lambda: dve.wait_ge(wsem, wcount), attend(1) + attend(2) + [residual(3, "d2", 3), post_norm(3), outer_sum, outer_norm])

        @block.tensor
        def _(pe):

            def transposes(L, k, src, done, rows=P):
                for b in range(GB):
                    ins = nc.tensor.transpose(L.part(k, slice(0, P), b, rows), src[0:rows, b, :], c.identf[0:rows, 0:rows])
                ins.then_inc(L.s[done], 1)

            def context(L, g):
                pe.wait_ge(L.s["cs"], g * 16 + 16)
                transposes(L, 2, L.Cs, "cTp", S2)

            def y_transposed(k):
                def stage(L, g):
                    if k == 1:
                        pe.wait_ge(L.s["ys"], g + 1)
                    else:
                        pe.wait_ge(L.s["b"], g * 3 + (k - 1))
                    transposes(L, 3, L.Y, "yTp")
                return stage

            def queries(k):
                def stage(L, g):
                    pe.wait_ge(L.s["yT"], g * 3 + k)
                    for b in range(GB):
                        q = L.part(0, slice(0, P), b)
                        ins = nc.tensor.matmul(q, L.YT[:, b * P:(b + 1) * P], W[f"wq{k}"][:, :], start=True, stop=k == 2)
                        if k == 1:
                            ins = nc.tensor.matmul(q, c.identb[:, :], W["qmask"][:, :], start=False, stop=True)
                    ins.then_inc(L.s["q"], 1)
                return stage

            def keys_values(k):
                def stage(L, g):
                    pe.wait_ge(L.s["cT"], g + 1)
                    for i in (0, 1):
                        for b in range(GB):
                            src = L.YT[:, b * P:(b + 1) * P] if k == 1 else L.cT[:, b, :]
                            ins = nc.tensor.matmul(L.part(1 + i, slice(0, KL[k]), b), src, W[f"wkv{k}"][:, i, :], start=True, stop=True)
                    ins.then_inc(L.s["kv"], 1)
                return stage

            def softmax_transposed(k):
                def stage(L, g):
                    pe.wait_ge(L.s["pq"], g * 2 + k)
                    transposes(L, 3, L.DD[:, 0], "sTp")
                return stage

            def products(k):
                def stage(L, g):
                    K = KL[k]
                    pe.wait_ge(L.s["pk"], g * 2 + k)
                    pe.wait_ge(L.s["vs"], g * 2 + k)
                    for b in range(GB):
                        ins = nc.tensor.matmul(L.part(2, slice(0, P), b), L.DD[0:K, 1, b, :], L.V[0:K, b, :], start=True, stop=True)
                    ins.then_inc(L.s["a"], 1)
                return stage

            def outputs(k):
                def stage(L, g):
                    pe.wait_ge(L.s["sT"], g * 2 + k)
                    pe.wait_ge(L.s["bda"], g * 2 + k)
                    for b in range(GB):
                        ins = nc.tensor.matmul(L.part(0, slice(0, P), b), L.sT[:, b * P:(b + 1) * P], L.BDA[:, b, :], start=True, stop=True)
                    ins.then_inc(L.s["bm"], 1)
                return stage

            def projection(k):
                def stage(L, g):
                    pe.wait_ge(L.s["tt"], g * 2 + k)
                    for b in range(GB):
                        for hl in (0, 1):
                            for w in (0, 1):
                                rows = L.TT[:, w, 4 * b:4 * b + 4, :].rearrange("p f a -> p (f a)")
                                ins = nc.tensor.matmul(L.part(1, slice(64 * hl, 64 * hl + 64), b), rows, W[f"wo{k}"][:, hl, w, :],
                                                       start=(w == 0), stop=(w == 1))
                    ins.then_inc(L.s["o"], 1)
                return stage

            def setup():
                pe.wait_ge(wsem, wcount)
                for i in (1, 2):
                    nc.tensor.matmul(PS[:, 0, (i - 1) * D:i * D], W[f"e{i}"][:, :], W[f"d{i}"][:, :], start=True, stop=True).then_inc(wp, 1)
                pe.wait_ge(ws, 1)

            def hidden(L, g):
                pe.wait_ge(L.s["yT"], g * 3 + 3)
                nc.tensor.matmul(L.bank(1), M[:, 0, :], L.YT[:, :], start=True, stop=True).then_inc(L.s["d1"], 1)

            def mlp_output(L, g):
                pe.wait_ge(L.s["hs"], g + 1)
                for b in range(GB):
                    ins = nc.tensor.matmul(L.part(3, slice(0, P), b), L.hs[:, b * P:(b + 1) * P], M[:, 1, :], start=True, stop=True)
                ins.then_inc(L.s["d2"], 1)

            attend = lambda k: [y_transposed(k), queries(k), keys_values(k), softmax_transposed(k), products(k), outputs(k), projection(k)]
            run(pe, setup, [context] + attend(1) + attend(2) + [y_transposed(3), hidden, mlp_output])
    c.end_phase(ctx)


PHASES[2] = linear_attention_block



def top2(dve, nc, sel, t, s, base):
    n = sel.shape[1]
    idx = t["idx"][:, :].rearrange("p (o e) -> p o e", o=1).to_broadcast([P, n, 8])
    bc = lambda ap: ap.rearrange("p (n o) -> p n o", o=1).to_broadcast([P, n, 8])
    at = 0

    def step(ins):
        nonlocal at
        at += 1
        ins.then_inc(s["t"], 1)
        dve.wait_ge(s["t"], base + at)

    for src, oh in ((sel, t["oh1"]), (t["sel2"][:, :, :], t["oh2"])):
        step(nc.vector.tensor_reduce(t["m"][:, :], src, AX_X, ALU.max))
        step(nc.vector.tensor_tensor(t["key"][:, :, :], src, bc(t["m"][:, :]), ALU.is_equal))
        step(nc.vector.tensor_tensor(t["key"][:, :, :], t["key"][:, :, :], idx, ALU.mult))
        step(nc.vector.tensor_reduce(t["m"][:, :], t["key"][:, :, :], AX_X, ALU.max))
        step(nc.vector.tensor_tensor(oh[:, :, :], t["key"][:, :, :], bc(t["m"][:, :]), ALU.is_equal))
        if oh is t["oh1"]:
            step(nc.vector.scalar_tensor_tensor(t["sel2"][:, :, :], oh[:, :, :], -BIG, src, ALU.mult, ALU.add))


TOP2 = 11



def routed_ffn(c, W, wsem, wcount, out):
    nc, X, PS = c.nc, c.X, c.PS
    NE, SC = 8, 2
    SH = 2
    SLOT = {"stats": 0, "rstd": 0, "norm": 1, "gate": 2, "other": 2, "product": 2, "activate": 3, "route1": 3, "route2": 5, "route3": 6, "route4": 6,
            "shared": 6, "start": 7, "x_T": 5, "x_copy": 7, "rows": 6}
    s = c.sems("f_", "xs xTp xT lg h1 h3 ex sg h t y0 acc0 ep ge ey acc x " + LN_SEMS)
    ctx = ExitStack()
    sb = lambda n, sh, dt=F32: c.sb("f_" + n, sh, dt, ctx)
    Xs = sb("Xs", [P, GB, D])
    xT = sb("xT", [D, 2, T])
    sg = sb("sg", [P, SC, T])
    hs = sb("hs", [P, SC, T])
    el = sb("el", [P, GB, NE])
    sc = sb("sc", [P, GB, NE])
    sel = sb("sel", [P, GB, NE])
    t = {"m": sb("m", [P, GB]), "idx": W["idx"]}
    for n in ("key", "sel2", "oh1", "oh2", "ss"):
        t[n] = sb(n, [P, GB, NE])
    den = sb("den", [P, 4, GB])
    comb = sb("comb", [P, 2, GB, NE])
    G = sb("G", [P, 2, T])
    Acc = sb("Acc", [P, 2, GB, D])
    ln = c.ln
    bank = lambda i, r=P: PS[0:r, i, :]
    bc = lambda ap: ap.rearrange("p (n o) -> p n o", o=1).to_broadcast([P, GB, NE])
    SR = TOP2 + 14

    def first(g, e):
        return isinstance(g, int) and g == 0 and e < 2

    with nc.Block() as block:

        @block.gpsimd
        def _(pool):

            def rows(g, par):
                if not isinstance(g, int) or g > 0:
                    pool.wait_ge(s["xTp"], g)
                nc.gpsimd.tensor_copy(Xs[:, :, :], group(c, g)).then_inc(s["xs"], 1)

            def rstd(g, par):
                ln_rstd(pool, nc, ln, s, g + 1)

            pipeline(pool, SLOT, SH, NE, lambda: None, {"rows": rows}, {}, lambda g, par, e, left: None, {"rstd": rstd})

        @block.scalar
        def _(act):

            def x_copy(g, par):
                act.wait_ge(s["xTp"], g + 1)
                nc.scalar.copy(xT[:, par, :], bank(0)).then_inc(s["xT"], 1)

            def activate(g, par):
                act.wait_ge(s["lg"], g + 1)
                nc.scalar.activation(el[:, :, :].rearrange("p b e -> p (b e)"), PS[:, 1, 0:GB * NE], ACT.Exp, scale=-1.0).then_inc(s["ex"], 1)
                act.wait_ge(s["h1"], g + 1)
                nc.scalar.activation(sg[:, :, :], PS[:, 2:4, :], ACT.Silu).then_inc(s["sg"], 1)

            def step(g, par, e, left):
                act.wait_ge(s["ep"], g * NE + e + 1)
                if not first(g, e):
                    act.wait_ge(s["ey"], g * NE + e - 1)
                nc.scalar.activation(G[:, e % 2, :], bank(6 + e % 2), ACT.Gelu).then_inc(s["ge"], 1)

            pipeline(act, SLOT, SH, NE, lambda: act.wait_ge(wsem, wcount), {"x_copy": x_copy}, {"activate": activate}, step, {})

        @block.vector
        def _(dve):

            def route(part):
                def stage(g, par):
                    base = {1: 0, 2: 3, 3: 3 + TOP2, 4: 3 + TOP2 + 6}[part]
                    k = base

                    def step(ins):
                        nonlocal k
                        k += 1
                        ins.then_inc(s["t"], 1)
                        dve.wait_ge(s["t"], g * SR + k)

                    if part == 1:
                        dve.wait_ge(s["ex"], g + 1)
                        step(nc.vector.tensor_scalar(el[:, :, :], el[:, :, :], 1.0, None, ALU.add))
                        step(nc.vector.reciprocal(sc[:, :, :], el[:, :, :]))
                        step(nc.vector.tensor_tensor(sel[:, :, :], sc[:, :, :], W["rb"][:, :].rearrange("p (o e) -> p o e", o=1).to_broadcast([P, GB, NE]), ALU.add))
                    if part == 2:
                        top2(dve, nc, sel[:, :, :], t, s, g * SR + k)
                    if part == 3:
                        step(nc.vector.tensor_tensor(t["key"][:, :, :], t["oh1"][:, :, :], t["oh2"][:, :, :], ALU.add))
                        step(nc.vector.tensor_tensor(t["ss"][:, :, :], t["key"][:, :, :], sc[:, :, :], ALU.mult))
                        step(nc.vector.tensor_reduce(den[:, 0, :], t["ss"][:, :, :], AX_X, ALU.add))
                        step(nc.vector.tensor_scalar(den[:, 1, :], den[:, 0, :], 1e-9, None, ALU.add))
                        step(nc.vector.reciprocal(den[:, 2, :], den[:, 1, :]))
                        step(nc.vector.tensor_scalar(den[:, 3, :], den[:, 0, :], 1e-9, None, ALU.is_gt))
                    if part == 4:
                        step(nc.vector.tensor_tensor(den[:, 2, :], den[:, 2, :], den[:, 3, :], ALU.mult))
                        step(nc.vector.tensor_scalar(den[:, 3, :], den[:, 3, :], -0.5, 0.5, ALU.mult, ALU.add))
                        step(nc.vector.tensor_tensor(t["ss"][:, :, :], t["ss"][:, :, :], bc(den[:, 2, :]), ALU.mult))
                        step(nc.vector.tensor_tensor(t["key"][:, :, :], t["key"][:, :, :], bc(den[:, 3, :]), ALU.mult))
                        step(nc.vector.tensor_tensor(comb[:, par], t["ss"][:, :, :], t["key"][:, :, :], ALU.add))
                        assert k == SR
                return stage

            def product(g, par):
                dve.wait_ge(s["sg"], g + 1)
                dve.wait_ge(s["h3"], g + 1)
                nc.vector.tensor_tensor(hs[:, :, :], PS[:, 0:2, :], sg[:, :, :], ALU.mult).then_inc(s["h"], 1)

            def start(g, par):
                dve.wait_ge(s["y0"], g + 1)
                nc.vector.tensor_tensor(flat(Acc[:, par]), bank(2), flat(group(c, g)), ALU.add).then_inc(s["acc0"], 1)

            def step(g, par, e, left):
                dve.wait_ge(s["ey"], g * NE + e + 1)
                dve.wait_ge(s["acc0"] if e == 0 else s["acc"], g + 1 if e == 0 else g * NE + e)
                for b in range(GB):
                    ins = nc.vector.scalar_tensor_tensor(Acc[:, par, b, :], PS[:, 4 + e % 2, b * D:(b + 1) * D], comb[:, par, b, e:e + 1], Acc[:, par, b, :], ALU.mult, ALU.add)
                ins.then_inc(s["acc"], 1)

            def stats(g, par):
                dve.wait_ge(s["acc"], g * NE + NE)
                ln_stats(dve, nc, Acc[:, par], ln, s, g + 1)

            def norm(g, par):
                ln_apply(dve, nc, group(c, g), Acc[:, par], ln, s, g + 1, s["x"])

            pipeline(dve, SLOT, SH, NE, lambda: dve.wait_ge(wsem, wcount), {},
                     {"product": product, "route1": route(1), "route2": route(2), "route3": route(3), "route4": route(4), "start": start}, step,
                     {"stats": stats, "norm": norm})

        @block.tensor
        def _(pe):

            def transpose(g, par):
                pe.wait_ge(s["xs"], g + 1)
                if not isinstance(g, int) or g > 0:
                    pe.wait_ge(s["h"], g)
                for b in range(GB):
                    ins = nc.tensor.transpose(PS[:, 0, b * P:(b + 1) * P], Xs[:, b, :], c.identf[:, :])
                ins.then_inc(s["xTp"], 1)

            def gate(g, par):
                pe.wait_ge(s["xT"], g + 1)
                for b in range(GB):
                    ins = nc.tensor.matmul(PS[:, 1, b * NE:(b + 1) * NE], xT[:, par, b * P:(b + 1) * P], W["rw"][:, :], start=True, stop=True)
                ins.then_inc(s["lg"], 1)
                if not isinstance(g, int) or g > 0:
                    pe.wait_ge(s["acc0"], g)
                for i in range(SC):
                    ins = nc.tensor.matmul(bank(2 + i), W["sw1"][:, i * P:(i + 1) * P], xT[:, par, :], start=True, stop=True)
                ins.then_inc(s["h1"], 1)

            def other(g, par):
                pe.wait_ge(s["ex"], g + 1)
                for i in range(SC):
                    ins = nc.tensor.matmul(bank(i), W["sw3"][:, i * P:(i + 1) * P], xT[:, par, :], start=True, stop=True)
                ins.then_inc(s["h3"], 1)

            def shared(g, par):
                pe.wait_ge(s["h"], g + 1)
                for b in range(GB):
                    for i in range(SC):
                        ins = nc.tensor.matmul(PS[:, 2, b * D:(b + 1) * D], hs[:, i, b * P:(b + 1) * P], W["sw2"][:, i, :], start=(i == 0), stop=(i == SC - 1))
                ins.then_inc(s["y0"], 1)

            def hidden(g, par, e):
                if not first(g, e):
                    pe.wait_ge(s["ge"], g * NE + e - 1)
                nc.tensor.matmul(bank(6 + e % 2), W["ew1"][:, e, :], xT[:, par, :], start=True, stop=True).then_inc(s["ep"], 1)

            def step(g, par, e, left):
                if isinstance(g, int) and g == 0 and e == 0:
                    hidden(0, 0, 0)
                    hidden(0, 0, 1)
                pe.wait_ge(s["ge"], g * NE + e + 1)
                if not first(g, e):
                    pe.wait_ge(s["acc"], g * NE + e - 1)
                for b in range(GB):
                    ins = nc.tensor.matmul(PS[:, 4 + e % 2, b * D:(b + 1) * D], G[:, e % 2, b * P:(b + 1) * P], W["ew2"][:, e, :], start=True, stop=True)
                ins.then_inc(s["ey"], 1)
                if e + 2 < NE:
                    hidden(g, par, e + 2)
                elif left:
                    hidden(g + 1, 1 - par, e + 2 - NE)

            pipeline(pe, SLOT, SH, NE, lambda: pe.wait_ge(wsem, wcount), {"x_T": transpose}, {"gate": gate, "other": other, "shared": shared}, step, {})
    c.end_phase(ctx)


PHASES[3] = routed_ffn



def state_space(c, W, wsem, wcount, out):
    nc, X, PS = c.nc, c.X, c.PS
    CH, NS, DC = 2, 16, 4
    NI = NS * CH
    ND = 4
    SH = 8
    s = c.sems("m_", "A xp0 z0 n xnp xnT xp xpc z sz cv u dtp dtr bcp hi r sp dv ab e w l t m dt du "
                     "B C dA dBu h Cs hC yacc y1 y2 yp r2 x " + LN_SEMS + " ist imv ilv irs")
    si = {k: s["i" + k] for k in LN_SEMS.split()}
    ctx = ExitStack()
    sb = lambda n, sh, dt=F32: c.sb("m_" + n, sh, dt, ctx)
    Xn = sb("Xn", [P, GB, D])
    xnT = sb("xnT", [D, T])
    xp = sb("xp", [P, CH, GB, DC - 1 + P])
    U = sb("U", [P, CH, T])
    U2 = sb("U2", [P, 2, CH, T])
    SZ = sb("SZ", [P, 2, CH, T])
    DT = sb("DT", [P, 2, CH, T])
    DU = sb("DU", [P, 2, CH, T])
    hi = sb("hi", [96, 2, T], BF16)
    E1 = sb("E1", [P, CH, T])
    E2 = sb("E2", [P, CH, T])
    L = sb("L", [P, CH, T])
    YG = sb("YG", [P, CH, T])
    dtr = sb("dtr", [8, T])
    R = sb("R", [96, T])
    A = sb("A", [P, CH, NS])
    dA = sb("dA", [P, ND, GB, P])
    dBu = sb("dBu", [P, 2, T])
    hst = sb("h", [P, ND, T])
    Cs = sb("Cs", [P, ND, T])
    hC = sb("hC", [P, ND, T])
    ln, iln = c.ln, {k: (c.sb("m_i" + k, v.shape, F32, ctx) if k not in ("half", "eps") else v) for k, v in c.ln.items()}
    bank = lambda i, r=P: PS[0:r, i, :]
    bl = lambda ap: ap.rearrange("p (b l) -> p b l", b=GB)
    AUX = (7, 0)
    SLOT = {"gated": 3, "output": 0, "residual": 5, "rstd": 4, "norm": 7, "project_z": 8, "silus": 13, "dt_b_c": 11,
            "parts": 19, "rest": 21, "middle": 23, "last": 23, "dt": 21, "dt_bias": 25, "one_more": 28, "logs": 28,
            "rounding": 28, "softplus": 28, "inputs": 28, "inner_stats": 11, "inner_rstd": 12, "inner_norm": 15, "xn_T": 23, "xn_copy": 25,
            "project_x": 24, "xp_copy": 29, "tap0": 28, "tap1": 28, "tap2": 29, "tap3": 29}

    def first(g, i, depth):
        return isinstance(g, int) and g == 0 and i < depth

    with nc.Block() as block:

        @block.gpsimd
        def _(pool):

            def setup():
                nc.gpsimd.memset(xp[:, :, :, 0:DC - 1], 0.0).then_inc(s["xp0"], 1)
                nc.gpsimd.memset(dA[:, :, :, 0:1], 0.0).then_inc(s["z0"], 1)

            def inner_norm(g, par):
                ln_rstd(pool, nc, iln, si, g + 1)

            def inputs(g, par):
                pool.wait_ge(s["dt"], g + 1)
                nc.gpsimd.tensor_tensor(DU[:, par], DT[:, par], U2[:, par], ALU.mult).then_inc(s["du"], 1)

            def step(g, par, i, left):
                n = i // CH
                pool.wait_ge(s["h"], g * NI + i + 1)
                pool.wait_ge(s["Cs"], g * NS + n + 1)
                if not first(g, i, ND):
                    pool.wait_ge(s["yacc"], g * NI + i - ND + 1)
                nc.gpsimd.tensor_tensor(hC[:, i % ND, :], hst[:, i % ND, :], Cs[:, n % ND, :], ALU.mult).then_inc(s["hC"], 1)

            def norm(g, par):
                ln_rstd(pool, nc, ln, s, g + 1)

            pipeline(pool, SLOT, SH, NI, setup, {"inner_rstd": inner_norm}, {"inputs": inputs}, step, {"rstd": norm})

        @block.scalar
        def _(act):

            def setup():
                act.wait_ge(wsem, wcount)
                act.wait_ge(s["xp0"], 1)
                act.wait_ge(s["z0"], 1)
                nc.scalar.activation(A[:, :, :], W["alog"][:, :, :], ACT.Exp).then_inc(s["A"], 1)
                act.wait_ge(s["A"], 1)
                nc.scalar.activation(A[:, :, :], A[:, :, :], ACT.Copy, scale=-1.0).then_inc(s["A"], 1)
                act.wait_ge(s["A"], 2)

            def normalised(g, par):
                act.wait_ge(s["xnp"], g + 1)
                nc.scalar.activation(xnT[:, :], bank(0), ACT.Identity, scale=W["lnw"][:, 0:1], bias=W["lnb"][:, 0:1]).then_inc(s["xnT"], 1)

            def convolved(g, par):
                for ch in range(CH):
                    act.wait_ge(s["xpc"], g * CH + ch + 1)
                    nc.scalar.copy(xp[:, ch, :, DC - 1:DC - 1 + P], bl(bank(AUX[ch]))).then_inc(s["xp"], 1)

            def silus(g, par):
                for ch in range(CH):
                    act.wait_ge(s["z"], g * CH + ch + 1)
                    nc.scalar.activation(SZ[:, par, ch, :], bank(AUX[ch]), ACT.Silu).then_inc(s["sz"], 1)
                act.wait_ge(s["cv"], g * 8 + 8)
                nc.scalar.activation(U2[:, par], U[:, :, :], ACT.Silu).then_inc(s["u"], 1)
                nc.scalar.preload_act_table_set("natural_log_exp_and_others")

            def parts(g, par):
                act.wait_ge(s["dtp"], g + 1)
                nc.scalar.copy(dtr[:, :], bank(7, 8)).then_inc(s["dtr"], 1)
                act.wait_ge(s["bcp"], g + 1)
                nc.scalar.copy(hi[:, par, :], bank(0, 96)).then_inc(s["hi"], 1)

            def step_sizes(g, par):
                for ch in range(CH):
                    act.wait_ge(s["dv"], g * CH + ch + 1)
                    nc.scalar.activation(DT[:, par, ch, :], bank(AUX[ch]), ACT.Identity, bias=W["bdt"][:, ch:ch + 1]).then_inc(s["ab"], 1)
                act.wait_ge(s["ab"], g * 3 + 2)
                nc.scalar.activation(L[:, :, :], DT[:, par], ACT.Abs).then_inc(s["ab"], 1)
                act.wait_ge(s["ab"], g * 3 + 3)
                nc.scalar.activation(E1[:, :, :], L[:, :, :], ACT.Exp, scale=-1.0).then_inc(s["e"], 1)

            def logs(g, par):
                act.wait_ge(s["w"], g + 1)
                nc.scalar.activation(L[:, :, :], E2[:, :, :], ACT.Ln).then_inc(s["l"], 1)

            def step(g, par, i, left):
                n, ch = i // CH, i % CH
                if i == 0:
                    act.wait_ge(s["dt"], g + 1)
                if not first(g, i, ND):
                    act.wait_ge(s["h"], g * NI + i - ND + 1)
                nc.scalar.activation(dA[:, i % ND, :, 1:P], bl(DT[:, par, ch, :])[:, :, 1:P], ACT.Exp, scale=A[:, ch, n:n + 1]).then_inc(s["dA"], 1)
                if ch == 0:
                    act.wait_ge(s["C"], g * NS + n + 1)
                    if not first(g, n, ND):
                        act.wait_ge(s["hC"], g * NI + CH * (n - ND + 1))
                    nc.scalar.copy(Cs[:, n % ND, :], bank(3 + n % 2)).then_inc(s["Cs"], 1)

            pipeline(act, SLOT, SH, NI, setup, {"xn_copy": normalised, "xp_copy": convolved}, {"silus": silus, "parts": parts, "dt_bias": step_sizes, "logs": logs}, step, {})

        @block.vector
        def _(dve):

            def setup():
                dve.wait_ge(wsem, wcount)
                dve.wait_ge(s["xp0"], 1)
                dve.wait_ge(s["z0"], 1)

            def stats(g, par):
                ln_stats(dve, nc, group(c, g), iln, si, g + 1)

            def normalise(g, par):
                ln_apply(dve, nc, Xn, group(c, g), iln, si, g + 1, s["n"])

            def tap(k):
                def conv(g, par):
                    for ch in range(CH):
                        if k == 0:
                            dve.wait_ge(s["xp"], g * CH + ch + 1)
                            nc.vector.tensor_scalar(bl(U[:, ch, :]), xp[:, ch, :, 0:P], W["cw"][:, ch, 0:1], W["cb"][:, ch:ch + 1], ALU.mult, ALU.add).then_inc(s["cv"], 1)
                        else:
                            dve.wait_ge(s["cv"], g * 8 + (2 * k + ch - 1))
                            nc.vector.scalar_tensor_tensor(bl(U[:, ch, :]), xp[:, ch, :, k:k + P], W["cw"][:, ch, k:k + 1], bl(U[:, ch, :]), ALU.mult, ALU.add).then_inc(s["cv"], 1)
                return conv

            def rest(g, par):
                dve.wait_ge(s["hi"], g + 1)
                nc.vector.tensor_tensor(R[:, :], bank(0, 96), hi[:, par, :], ALU.subtract).then_inc(s["r"], 1)

            def middle(g, par):
                dve.wait_ge(s["r"], g * 2 + 1)
                nc.vector.tensor_copy(hi[32:64, par, :], R[32:64, :]).then_inc(s["sp"], 1)
                nc.vector.tensor_copy(hi[64:96, par, :], R[64:96, :]).then_inc(s["sp"], 1)

            def last(g, par):
                dve.wait_ge(s["sp"], g * 3 + 2)
                nc.vector.tensor_tensor(R[64:96, :], R[64:96, :], hi[64:96, par, :], ALU.subtract).then_inc(s["r"], 1)
                dve.wait_ge(s["r"], g * 2 + 2)
                nc.vector.tensor_copy(hi[64:96, par, :], R[64:96, :]).then_inc(s["sp"], 1)

            def one_more(g, par):
                dve.wait_ge(s["e"], g + 1)
                nc.vector.tensor_scalar(E2[:, :, :], E1[:, :, :], 1.0, None, ALU.add).then_inc(s["w"], 1)

            def rounding(g, par):
                dve.wait_ge(s["w"], g + 1)
                nc.vector.scalar_tensor_tensor(E1[:, :, :], E2[:, :, :], -1.0, E1[:, :, :], ALU.add, ALU.subtract).then_inc(s["t"], 1)

            def softplus(g, par):
                dve.wait_ge(s["l"], g + 1)
                nc.vector.scalar_tensor_tensor(DT[:, par], DT[:, par], 0.0, L[:, :, :], ALU.max, ALU.add).then_inc(s["m"], 1)
                dve.wait_ge(s["m"], g + 1)
                dve.wait_ge(s["t"], g + 1)
                nc.vector.tensor_tensor(DT[:, par], DT[:, par], E1[:, :, :], ALU.subtract).then_inc(s["dt"], 1)

            def step(g, par, i, left):
                n, ch = i // CH, i % CH
                if i == 0:
                    dve.wait_ge(s["du"], g + 1)
                dve.wait_ge(s["B"], g * NS + n + 1)
                if not first(g, i, 2):
                    dve.wait_ge(s["h"], g * NI + i - 1)
                nc.vector.tensor_tensor(dBu[:, i % 2, :], bank(1 + n % 2), DU[:, par, ch, :], ALU.mult).then_inc(s["dBu"], 1)
                dve.wait_ge(s["dBu"], g * NI + i + 1)
                dve.wait_ge(s["dA"], g * NI + i + 1)
                if not first(g, i, ND):
                    dve.wait_ge(s["hC"], g * NI + i - ND + 1)
                nc.vector.tensor_tensor_scan(hst[:, i % ND, :], dA[:, i % ND].rearrange("p b l -> p (b l)"), dBu[:, i % 2, :], 0.0, ALU.mult, ALU.add).then_inc(s["h"], 1)

            def gated(g, par):
                dve.wait_ge(s["yacc"], g * NI + NI)
                for ch in range(CH):
                    nc.vector.scalar_tensor_tensor(YG[:, ch, :], U2[:, par, ch, :], W["dp"][:, ch:ch + 1], bank(5 + ch), ALU.mult, ALU.add).then_inc(s["y1"], 1)
                dve.wait_ge(s["y1"], g * 2 + 2)
                nc.vector.tensor_tensor(YG[:, :, :], YG[:, :, :], SZ[:, par], ALU.mult).then_inc(s["y2"], 1)

            def residual(g, par):
                dve.wait_ge(s["yp"], g + 1)
                nc.vector.scalar_tensor_tensor(flat(Xn[:, :, :]), flat(group(c, g)), 2.0, bank(7), ALU.mult, ALU.add).then_inc(s["r2"], 1)
                dve.wait_ge(s["r2"], g + 1)
                ln_stats(dve, nc, Xn, ln, s, g + 1)

            def norm(g, par):
                ln_apply(dve, nc, group(c, g), Xn, ln, s, g + 1, s["x"])

            pipeline(dve, SLOT, SH, NI, setup, {"inner_stats": stats, "inner_norm": normalise, "tap0": tap(0), "tap1": tap(1), "tap2": tap(2), "tap3": tap(3)},
                     {"rest": rest, "middle": middle, "last": last, "one_more": one_more, "rounding": rounding, "softplus": softplus}, step,
                     {"gated": gated, "residual": residual, "norm": norm})

        @block.tensor
        def _(pe):

            def setup():
                pe.wait_ge(wsem, wcount)

            def transposed(g, par):
                pe.wait_ge(s["n"], g + 1)
                if not isinstance(g, int) or g > 0:
                    pe.wait_ge(s["ab"], g * 3)
                for b in range(GB):
                    ins = nc.tensor.transpose(PS[:, 0, b * P:(b + 1) * P], Xn[:, b, :], c.identf[:, :])
                ins.then_inc(s["xnp"], 1)

            def project(first_chunk, done, read):
                def stage(g, par):
                    for ch in range(CH):
                        if read:
                            pe.wait_ge(s[read], g * CH + ch + 1)
                        elif ch == 0:
                            pe.wait_ge(s["xnT"], g + 1)
                        i = first_chunk + ch
                        nc.tensor.matmul(bank(AUX[ch]), W["win"][:, i * P:(i + 1) * P], xnT[:, :], start=True, stop=True).then_inc(s[done], 1)
                return stage

            def dt_b_c(g, par):
                pe.wait_ge(s["u"], g + 1)
                for ch in range(CH):
                    ins = nc.tensor.matmul(bank(7, 8), W["wxd"][:, ch, :], U2[:, par, ch, :], start=(ch == 0), stop=(ch == CH - 1))
                ins.then_inc(s["dtp"], 1)
                for ch in range(CH):
                    ins = nc.tensor.matmul(bank(0, 96), W["wxb"][:, ch, :], U2[:, par, ch, :], start=(ch == 0), stop=(ch == CH - 1))
                ins.then_inc(s["bcp"], 1)

            def step_sizes(g, par):
                pe.wait_ge(s["dtr"], g + 1)
                for ch in range(CH):
                    if ch == 1:
                        pe.wait_ge(s["r"], g * 2 + 1)
                    nc.tensor.matmul(bank(AUX[ch]), W["wdt"][:, ch * P:(ch + 1) * P], dtr[:, :], start=True, stop=True).then_inc(s["dv"], 1)

            def spread(g, par, n):
                if n == 0:
                    pe.wait_ge(s["sp"], g * 3 + 3)
                if not first(g, n, 2):
                    pe.wait_ge(s["dBu"], g * NI + 2 * (n - 1))
                    pe.wait_ge(s["Cs"], g * NS + n - 1)
                nc.tensor.matmul(bank(1 + n % 2), W["sel"][:, n:n + 1].to_broadcast([96, P]), hi[:, par, :], start=True, stop=True).then_inc(s["B"], 1)
                nc.tensor.matmul(bank(3 + n % 2), W["sel"][:, NS + n:NS + n + 1].to_broadcast([96, P]), hi[:, par, :], start=True, stop=True).then_inc(s["C"], 1)

            def step(g, par, i, left):
                n, ch = i // CH, i % CH
                if isinstance(g, int) and g == 0 and i == 0:
                    spread(0, 0, 0)
                    spread(0, 0, 1)
                if n == 0 and not (isinstance(g, int) and g == 0):
                    pe.wait_ge(s["y1"], g * 2 - 1 + ch)
                pe.wait_ge(s["hC"], g * NI + i + 1)
                nc.tensor.matmul(bank(5 + ch), c.identf[:, :], hC[:, i % ND, :], start=(n == 0), stop=(n == NS - 1)).then_inc(s["yacc"], 1)
                if ch == 0:
                    if n + 2 < NS:
                        spread(g, par, n + 2)
                    elif left:
                        spread(g + 1, 1 - par, n + 2 - NS)

            def output(g, par):
                pe.wait_ge(s["y2"], g + 1)
                for b in range(GB):
                    for ch in range(CH):
                        ins = nc.tensor.matmul(PS[:, 7, b * D:(b + 1) * D], YG[:, ch, b * P:(b + 1) * P], W["wout"][:, ch, :], start=(ch == 0), stop=(ch == CH - 1))
                ins.then_inc(s["yp"], 1)

            pipeline(pe, SLOT, SH, NI, setup, {"xn_T": transposed, "project_x": project(0, "xpc", None)}, {"project_z": project(CH, "z", "xp"), "dt_b_c": dt_b_c, "dt": step_sizes}, step,
                     {"output": output})
    c.end_phase(ctx)


PHASES[4] = state_space


def context_attention(c, W, wsem, wcount, out):
    attention(c, "k_", True, W, wsem, wcount)


PHASES[5] = context_attention



def sinkhorn_ffn(c, W, wsem, wcount, out):
    nc, X, PS = c.nc, c.X, c.PS
    NE, FC, ITERS, SK_EPS = 8, 4, 20, 0.05
    NF = NE * FC
    ST = 2
    DEP = 3
    SINK, KEEP = 6, 7
    GAPS = 6
    SLOT = {"softplus": 1, "log_sigmoid": 2, "sigmoid": 2, "gated": 3, "hidden": 4}
    ctx = ExitStack()
    sb = lambda n, sh, dt=F32: c.sb("e_" + n, sh, dt, ctx)
    s = c.sems("e_", "xs xTp xT lg la rm rd re rs rl ra cm cT gm dg gM cd ce cs ct cl ca t w comb "
                     "gp up ab ex ep lo sig hg sg h ey ye acc wg m a x st mv lv rs2 out")
    sl = {"st": s["st"], "mv": s["mv"], "lv": s["lv"], "rs": s["rs2"]}
    XT = sb("XT", [D, B, P])
    comb = sb("comb", [P, B, NE])
    Xs = sb("Xs", [P, 2, GB, D])
    XL = sb("XL", [P, 2, T])
    LA = sb("LA", [P, B, NE])
    E = sb("E", [P, B, NE])
    rm, rs, rl = sb("rm", [P, B]), sb("rs", [P, B]), sb("rl", [P, B])
    cm, cs, cl = sb("cm", [P, NE]), sb("cs", [P, NE]), sb("cl", [P, NE])
    gm, dg = sb("gm", [NE, 1]), sb("dg", [NE, NE])
    t = {"m": rm, "idx": W["idx"]}
    for n in ("key", "sel2", "oh1", "oh2"):
        t[n] = sb(n, [P, B, NE])
    Sg = sb("Sg", [P, DEP, T])
    Hh = sb("Hh", [P, 2, FC, T])
    Ys = sb("Ys", [P, ST, NE, T])
    kept_sum = lambda g: Ys[:, g, 0, :].rearrange("p (b d) -> p b d", b=GB)
    Acc = sb("Acc", [P, GB, D])
    wg = sb("wg", [P, GB, NE])
    ln = c.ln
    bank = lambda i, r=P: PS[0:r, i, :]
    rows = lambda ap: ap.rearrange("p (b o) -> p b o", o=1).to_broadcast([P, B, NE])
    cols = lambda ap: ap.rearrange("p (o e) -> p o e", o=1).to_broadcast([P, B, NE])
    byexp = lambda ap: ap.rearrange("p b e -> p e b")

    def place(ch):
        return ch * ITERS * GAPS // (ST * NF + 2)

    chunks = {}
    for ch in range(ST * NF):
        chunks.setdefault(place(ch), []).append(ch)

    def at(gap):
        return chunks.get(gap, [])

    def order(g):
        if isinstance(g, int):
            return g + NG - 1 - ST if g < ST else NG - 1 if g == NG - 1 else g - ST
        return g - ST

    def stream(eng, step, end):
        SH = FC

        def body(g, left):
            for j in range(SH, NF):
                step(g, j)
            for j in range(SH):
                if left:
                    step(g + 1, j)
                for slot, stage in end:
                    if slot == j:
                        stage(g)

        for j in range(SH):
            step(ST, j)
        with eng.Fori(ST, NG - 1) as g:
            body(g, 1)
        body(NG - 1, 0)

    with nc.Block() as block:

        @block.sync
        def _(sp):

            def store(g, n):
                sp.wait_ge(s["x"], n)
                sp.dma_start(out[bass.ds(g * GB, GB), :, :].rearrange("b p d -> p b d"), group(c, g)).then_inc(s["out"], 16)

            with sp.Fori(ST, NG - 1) as g:
                store(g, g - (ST - 1))
            for g in list(range(ST)) + [NG - 1]:
                store(g, order(g) + 1)
            sp.wait_ge(s["out"], 16 * NG)

        @block.gpsimd
        def _(pool):
            for g in (0, 1):
                nc.gpsimd.tensor_copy(Xs[:, g], group(c, g)).then_inc(s["xs"], 1)
            with pool.Fori(1, NG // 2) as i:
                for par in (0, 1):
                    pool.wait_ge(s["xTp"], i * 2 + (par - 1))
                    nc.gpsimd.tensor_copy(Xs[:, par], group(c, i * 2 + par)).then_inc(s["xs"], 1)
            pool.wait_ge(s["comb"], 1)
            pool.wait_ge(s["ye"], ST * NE)
            for g in range(ST):
                for e in range(NE):
                    y = Ys[:, g, e, :].rearrange("p (b d) -> p b d", b=GB)
                    nc.gpsimd.tensor_tensor(y, y, comb[:, g * GB:(g + 1) * GB, e:e + 1].to_broadcast([P, GB, D]), ALU.mult).then_inc(s["m"], 1)
                    pool.wait_ge(s["m"], g * NE + e + 1)
                    if e > 0:
                        pool.wait_ge(s["a"], g * NE + e)
                    nc.gpsimd.tensor_tensor(kept_sum(g), y, kept_sum(g) if e else group(c, g), ALU.add).then_inc(s["a"], 1)
            with pool.Fori(ST, NG - 1) as g:
                ln_rstd(pool, nc, ln, sl, g - (ST - 1))
            for g in list(range(ST)) + [NG - 1]:
                ln_rstd(pool, nc, ln, sl, order(g) + 1)

        @block.scalar
        def _(act):
            act.wait_ge(wsem, wcount)
            with act.Fori(0, NG // 2) as i:
                for par in (0, 1):
                    act.wait_ge(s["xTp"], i * 2 + (par + 1))
                    nc.scalar.copy(XT[:, bass.ds((i * 2 + par) * GB, GB), :].rearrange("p b d -> p (b d)"), bank(par)).then_inc(s["xT"], 1)
                    nc.scalar.copy(XL[:, par], bank(par)).then_inc(s["xT"], 1)
            nc.scalar.preload_act_table_set("natural_log_exp_and_others")

            def chunk(ch):
                act.wait_ge(s["gp"], ch + 1)
                if ch >= DEP:
                    act.wait_ge(s["hg"], ch - DEP + 1)
                nc.scalar.activation(Sg[:, ch % DEP, :], bank(ch % DEP), ACT.Abs).then_inc(s["ab"], 1)
                act.wait_ge(s["ab"], ch + 1)
                nc.scalar.activation(Sg[:, ch % DEP, :], Sg[:, ch % DEP, :], ACT.Exp, scale=-1.0).then_inc(s["ex"], 1)
                act.wait_ge(s["ex"], ch + 1)
                nc.scalar.activation(Sg[:, ch % DEP, :], Sg[:, ch % DEP, :], ACT.Ln, bias=W["ones"][:, 0:1]).then_inc(s["ep"], 1)

            def sigmoid(ch):
                act.wait_ge(s["lo"], ch + 1)
                nc.scalar.activation(Sg[:, ch % DEP, :], Sg[:, ch % DEP, :], ACT.Exp).then_inc(s["sig"], 1)

            def keep(e):
                act.wait_ge(s["ey"], e + 1)
                nc.scalar.copy(Ys[:, e // NE, e % NE, :], bank(KEEP)).then_inc(s["ye"], 1)

            kept = 0
            for k in range(ITERS):
                for i in range(GAPS):
                    if i == 0:
                        act.wait_ge(s["rd"], k + 1)
                        nc.scalar.activation(E[:, :, :], LA[:, :, :], ACT.Exp).then_inc(s["re"], 1)
                    if i == 1:
                        act.wait_ge(s["rs"], k + 1)
                        nc.scalar.activation(rl[:, :], rs[:, :], ACT.Ln).then_inc(s["rl"], 1)
                    if i == 4:
                        act.wait_ge(s["cd"], k + 1)
                        nc.scalar.activation(E[:, :, :], LA[:, :, :], ACT.Exp).then_inc(s["ce"], 1)
                    if i == 5:
                        act.wait_ge(s["ct"], k + 1)
                        nc.scalar.activation(cl[:, :], PS[:, SINK, 0:NE], ACT.Ln).then_inc(s["cl"], 1)
                    for ch in at(k * GAPS + i - SLOT["sigmoid"]):
                        sigmoid(ch)
                    for ch in at(k * GAPS + i - SLOT["softplus"]):
                        chunk(ch)
                        if ch % FC == FC - 1 and ch > FC:
                            keep(kept)
                            kept += 1
            for gap in range(ITERS * GAPS, ITERS * GAPS + SLOT["sigmoid"] + 1):
                for ch in at(gap - SLOT["sigmoid"]):
                    sigmoid(ch)
                for ch in at(gap - SLOT["softplus"]):
                    chunk(ch)
            act.wait_ge(s["ca"], ITERS)
            nc.scalar.activation(E[:, :, :], LA[:, :, :], ACT.Exp).then_inc(s["re"], 1)
            for e in range(kept, ST * NE):
                keep(e)

            def step(g, j):
                act.wait_ge(s["gp"], g * NF + (j + 1))
                act.wait_ge(s["h"], g * NF + (j - 1))
                nc.scalar.activation(Sg[:, j % 2, :], bank(j % 2), ACT.Silu).then_inc(s["sg"], 1)

            stream(act, step, [])

        @block.vector
        def _(dve):
            dve.wait_ge(wsem, wcount)
            with dve.Fori(0, NG // 2) as i:
                for par in (0, 1):
                    dve.wait_ge(s["lg"], i * 2 + (par + 1))
                    nc.vector.tensor_scalar(LA[:, bass.ds((i * 2 + par) * GB, GB), :], PS[:, 2 + par, 0:GB * NE].rearrange("p (b e) -> p b e", b=GB), -1.0 / SK_EPS, None, ALU.mult).then_inc(s["la"], 1)
            dve.wait_ge(s["la"], NG)

            def log_sigmoid(ch):
                dve.wait_ge(s["ep"], ch + 1)
                nc.vector.scalar_tensor_tensor(Sg[:, ch % DEP, :], bank(ch % DEP), 0.0, Sg[:, ch % DEP, :], ALU.min, ALU.subtract).then_inc(s["lo"], 1)

            def gated(ch):
                dve.wait_ge(s["sig"], ch + 1)
                if ch // FC >= 2:
                    dve.wait_ge(s["ey"], ch // FC - 1)
                nc.vector.tensor_tensor(Hh[:, ch // FC % 2, ch % FC, :], bank(ch % DEP), Sg[:, ch % DEP, :], ALU.mult).then_inc(s["hg"], 1)

            def hidden(ch):
                dve.wait_ge(s["hg"], ch + 1)
                dve.wait_ge(s["up"], ch + 1)
                h = Hh[:, ch // FC % 2, ch % FC, :]
                nc.vector.tensor_tensor(h, bank(DEP + ch % DEP), h, ALU.mult).then_inc(s["h"], 1)

            for k in range(ITERS):
                for i in range(GAPS):
                    if i == 0:
                        nc.vector.tensor_reduce(rm[:, :], LA[:, :, :], AX_X, ALU.max).then_inc(s["rm"], 1)
                        dve.wait_ge(s["rm"], k + 1)
                        nc.vector.tensor_tensor(LA[:, :, :], LA[:, :, :], rows(rm[:, :]), ALU.subtract).then_inc(s["rd"], 1)
                    if i == 1:
                        dve.wait_ge(s["re"], k + 1)
                        nc.vector.tensor_reduce(rs[:, :], E[:, :, :], AX_X, ALU.add).then_inc(s["rs"], 1)
                    if i == 2:
                        dve.wait_ge(s["rl"], k + 1)
                        nc.vector.tensor_tensor(LA[:, :, :], LA[:, :, :], rows(rl[:, :]), ALU.subtract).then_inc(s["ra"], 1)
                        dve.wait_ge(s["ra"], k + 1)
                        nc.vector.tensor_reduce(cm[:, :], byexp(LA[:, :, :]), AX_X, ALU.max).then_inc(s["cm"], 1)
                    if i == 3:
                        dve.wait_ge(s["cT"], k + 1)
                        nc.vector.tensor_reduce(gm[:, :], PS[0:NE, SINK, 0:P], AX_X, ALU.max).then_inc(s["gm"], 1)
                        dve.wait_ge(s["gm"], k + 1)
                        nc.vector.tensor_scalar(dg[:, :], c.identf[0:NE, 0:NE], gm[:, 0:1], None, ALU.mult).then_inc(s["dg"], 1)
                    if i == 4:
                        dve.wait_ge(s["gM"], k + 1)
                        nc.vector.tensor_tensor(LA[:, :, :], LA[:, :, :], cols(PS[:, SINK, 0:NE]), ALU.subtract).then_inc(s["cd"], 1)
                    if i == 5:
                        dve.wait_ge(s["ce"], k + 1)
                        nc.vector.tensor_reduce(cs[:, :], byexp(E[:, :, :]), AX_X, ALU.add).then_inc(s["cs"], 1)
                    gap = k * GAPS + i
                    for ch in at(gap - SLOT["hidden"]):
                        hidden(ch)
                    for ch in at(gap - SLOT["gated"]):
                        gated(ch)
                    for ch in at(gap - SLOT["log_sigmoid"]):
                        log_sigmoid(ch)
                dve.wait_ge(s["cl"], k + 1)
                nc.vector.tensor_tensor(LA[:, :, :], LA[:, :, :], cols(cl[:, :]), ALU.subtract).then_inc(s["ca"], 1)
                dve.wait_ge(s["ca"], k + 1)
            for gap in range(ITERS * GAPS, ITERS * GAPS + SLOT["hidden"] + 1):
                for ch in at(gap - SLOT["hidden"]):
                    hidden(ch)
                for ch in at(gap - SLOT["gated"]):
                    gated(ch)
                for ch in at(gap - SLOT["log_sigmoid"]):
                    log_sigmoid(ch)
            dve.wait_ge(s["re"], ITERS + 1)
            nc.vector.tensor_scalar(LA[:, :, :], E[:, :, :], float(np.finfo(np.float32).tiny), None, ALU.is_ge).then_inc(s["w"], 1)
            dve.wait_ge(s["w"], 1)
            nc.vector.tensor_tensor(E[:, :, :], E[:, :, :], LA[:, :, :], ALU.mult).then_inc(s["w"], 1)
            dve.wait_ge(s["w"], 2)
            top2(dve, nc, E[:, :, :], t, s, 0)
            for k, oh in enumerate((t["oh1"], t["oh2"])):
                nc.vector.tensor_tensor(oh[:, :, :], oh[:, :, :], E[:, :, k:k + 1].to_broadcast([P, B, NE]), ALU.mult).then_inc(s["w"], 1)
            dve.wait_ge(s["w"], 4)
            nc.vector.tensor_tensor(comb[:, :, :], t["oh1"][:, :, :], t["oh2"][:, :, :], ALU.add).then_inc(s["comb"], 1)
            dve.wait_ge(s["comb"], 1)
            dve.sem_inc(s["acc"], 1)

            def add(g, e):
                if e == 0:
                    nc.vector.tensor_copy(wg[:, :, :], comb[:, bass.ds(g * GB, GB), :]).then_inc(s["wg"], 1)
                    dve.wait_ge(s["wg"], g - (ST - 1))
                dve.wait_ge(s["ey"], g * NE + (e + 1))
                dve.wait_ge(s["acc"], g * NE + (e + 1 - ST * NE))
                for b in range(GB):
                    prior = Acc[:, b, :] if e else X[:, bass.ds(g * GB + b, 1), :].rearrange("p o d -> p (o d)")
                    ins = nc.vector.scalar_tensor_tensor(Acc[:, b, :], PS[:, 4 + e % 2, b * D:(b + 1) * D], wg[:, b, e:e + 1], prior, ALU.mult, ALU.add)
                ins.then_inc(s["acc"], 1)

            def step(g, j):
                e, f = j // FC, j % FC
                dve.wait_ge(s["sg"], g * NF + (j + 1 - ST * NF))
                dve.wait_ge(s["up"], g * NF + (j + 1))
                dve.wait_ge(s["ey"], g * NE + (e - 1))
                nc.vector.tensor_tensor(Hh[:, e % 2, f, :], bank(2 + j % 2), Sg[:, j % 2, :], ALU.mult).then_inc(s["h"], 1)
                if f == 2 and e >= 1:
                    add(g, e - 1)
                if isinstance(g, int) and g == NG - 1 and f == 3:
                    if e in (2, 4, 6)[:ST]:
                        kg = e // 2 - 1
                        dve.wait_ge(s["a"], (kg + 1) * NE)
                        ln_stats(dve, nc, kept_sum(kg), ln, sl, order(kg) + 1)
                    if e in (3, 5, 7)[:ST]:
                        kg = e // 2 - 1
                        ln_apply(dve, nc, group(c, kg), kept_sum(kg), ln, sl, order(kg) + 1, s["x"])

            def last(g):
                add(g, NE - 1)
                dve.wait_ge(s["acc"], g * NE + (NE + 1 - ST * NE))
                ln_stats(dve, nc, Acc, ln, sl, order(g) + 1)

            def norm(g):
                ln_apply(dve, nc, group(c, g), Acc, ln, sl, order(g) + 1, s["x"])

            stream(dve, step, [(2, last), (3, norm)])

        @block.tensor
        def _(pe):
            pe.wait_ge(wsem, wcount)
            with pe.Fori(0, NG // 2) as i:
                for par in (0, 1):
                    pe.wait_ge(s["xs"], i * 2 + (par + 1))
                    for b in range(GB):
                        ins = nc.tensor.transpose(PS[:, par, b * P:(b + 1) * P], Xs[:, par, b, :], c.identf[:, :])
                    ins.then_inc(s["xTp"], 1)
                for par in (0, 1):
                    pe.wait_ge(s["xT"], i * 4 + (2 * par + 2))
                    for b in range(GB):
                        ins = nc.tensor.matmul(PS[:, 2 + par, b * NE:(b + 1) * NE], XL[:, par, b * P:(b + 1) * P], W["gw"][:, :], start=True, stop=True)
                    ins.then_inc(s["lg"], 1)
                pe.wait_ge(s["la"], i * 2 + 2)

            def chunk(g, j, gate, up):
                rhs = XT[:, bass.ds(g * GB, GB), :].rearrange("p b d -> p (b d)")
                e, f = j // FC, j % FC
                nc.tensor.matmul(bank(gate), W["wg"][:, e, f * P:(f + 1) * P], rhs, start=True, stop=True).then_inc(s["gp"], 1)
                nc.tensor.matmul(bank(up), W["wu"][:, e, f * P:(f + 1) * P], rhs, start=True, stop=True).then_inc(s["up"], 1)

            def down(g, e, bk):
                pe.wait_ge(s["h"], g * NF + FC * (e + 1))
                for b in range(GB):
                    for f in range(FC):
                        ins = nc.tensor.matmul(PS[:, bk, b * D:(b + 1) * D], Hh[:, e % 2, f, b * P:(b + 1) * P], W["wd"][:, e, f, :], start=(f == 0), stop=(f == FC - 1))
                ins.then_inc(s["ey"], 1)

            def kept(e):
                if e >= 1:
                    pe.wait_ge(s["ye"], e)
                down(e // NE, e % NE, KEEP)

            for k in range(ITERS):
                for i in range(GAPS):
                    if i == 2:
                        pe.wait_ge(s["cm"], k + 1)
                        nc.tensor.transpose(PS[0:NE, SINK, 0:P], cm[:, :], c.identf[:, :]).then_inc(s["cT"], 1)
                    if i == 3:
                        pe.wait_ge(s["dg"], k + 1)
                        nc.tensor.matmul(PS[:, SINK, 0:NE], W["ones"][0:NE, :], dg[:, :], start=True, stop=True).then_inc(s["gM"], 1)
                    if i == 5:
                        pe.wait_ge(s["cs"], k + 1)
                        nc.tensor.matmul(PS[:, SINK, 0:NE], W["ones"][:, :], cs[:, :], start=True, stop=True).then_inc(s["ct"], 1)
                    for ch in at(k * GAPS + i):
                        if ch >= DEP:
                            pe.wait_ge(s["h"], ch - DEP + 1)
                        chunk(ch // NF, ch % NF, ch % DEP, DEP + ch % DEP)
                        if ch % FC == 1 and ch > FC:
                            kept(ch // FC - 1)

            def step(g, j):
                e, f = j // FC, j % FC
                if isinstance(g, int) and g == ST and j == 0:
                    pe.wait_ge(s["h"], ST * NF)
                else:
                    pe.wait_ge(s["h"], g * NF + (j - 1))
                chunk(g, j, j % 2, 2 + j % 2)
                if isinstance(g, int) and g == ST and j == 1:
                    kept(ST * NE - 1)
                if f == 1 and e >= 1:
                    weighted(g, e - 1)

            def weighted(g, e):
                pe.wait_ge(s["acc"], g * NE + ((e if e >= 2 else 1) - ST * NE))
                down(g, e, 4 + e % 2)

            stream(pe, step, [(1, lambda g: weighted(g, NE - 1))])
    c.end_phase(ctx)


PHASES[6] = sinkhorn_ffn


def plan_weights():
    return {
        1: {"wq": [D, D], "wqp": [D, D], "wk": [D, D], "wkp": [D, D], "wv": [D, D], "wo": [D, D],
            "cos": [D, P], "sin": [D, P], "hmask": [D, 4], "gmask": [D, 4], "cmask": ([P, P], BF16)},
        2: {"wq1": [D, D], "wkv1": [D, 2, D], "wo1": [D, 2, 2, D], "wq2": [D, D], "wkv2": [D, 2, D], "wo2": [D, 2, 2, D],
            "e1": [64, D], "d1": [64, D], "e2": [64, D], "d2": [64, D], "bdm": [D, D], "qmask": ([P, D], BF16),
            "g1": [P, D], "b1": [P, D], "g2": [P, D], "b2": [P, D], "g3": [P, D], "b3": [P, D]},
        3: {"rw": [D, 8], "rb": [P, 8], "idx": [P, 8], "sw1": [D, 256], "sw3": [D, 256], "sw2": [P, 2, D], "ew1": [D, 8, P], "ew2": [P, 8, D]},
        4: {"lnw": [D, 1], "lnb": [D, 1], "win": [D, 512], "cw": [P, 2, 4], "cb": [P, 2], "wxd": [P, 2, 8], "wxb": [P, 2, 96], "wdt": [8, 256],
            "bdt": [P, 2], "alog": [P, 2, 16], "dp": [P, 2], "wout": [P, 2, D], "sel": ([96, 32], BF16)},
        5: {"wq": [D, D], "wk": [D, D], "wv": [D, D], "wo": [D, D], "bq": [D, 1], "bk": [D, 1], "bv": [P, D], "bo": [P, D],
            "hmask": [D, 4], "gmask": [D, 4], "amask": [P, S2], "pad": ([P, B, S2], mybir.dt.uint8)},
        6: {"gw": [D, 8], "idx": [P, 8], "ones": [P, P], "wg": [D, 8, 512], "wu": [D, 8, 512], "wd": [P, 8, 4, D]},
    }


def program(nc, dram, out):
    ctx = ExitStack()
    with ctx:
        c = Core(nc, ctx, dram)
        c.X = c.sb("X", [P, B, D])
        c.identf = c.sb("identf", [P, P])
        c.identb = c.sb("identb", [P, P], BF16)
        c.ln = {"st": c.sb("ln_st", [P, GB, 6]), "mv": c.sb("ln_mv", [P, GB, 2]), "lv": c.sb("ln_lv", [P, GB]),
                "rs": c.sb("ln_rs", [P, GB]), "half": c.sb("ln_half", [P, GB]), "eps": c.sb("ln_eps", [P, GB])}
        c.PS = ctx.enter_context(nc.psum_tensor("PS", [P, 8, 512], F32))
        plan = {ph: ws for ph, ws in plan_weights().items() if ph <= UPTO}
        Ws, sem, count = {}, {}, {}
        for ph, ws in plan.items():
            Ws[ph] = {}
            for n, sh in ws.items():
                sh, dt = sh if isinstance(sh, tuple) else (sh, F32)
                Ws[ph][n] = c.sb(f"w{ph}_{n}", sh, dt)
            sem[ph] = c.sem(f"weights{ph}")
            count[ph] = 16 * len(ws)
        s_x, s_rest = c.sem("x_loaded"), c.sem("x_rest_loaded")
        s_set = c.sem("constants_set")
        count[1] += 32

        def load(sp, ph):
            for n, t in Ws[ph].items():
                full = tuple(slice(None) for _ in t.shape)
                sp.dma_start(t[full], dram[f"w{ph}_{n}"]).then_inc(sem[ph], 16)

        def later_loads(sp):
            sp.dma_start(c.X[:, GB:B, :], dram["x"][:, GB:B, :]).then_inc(s_rest, 16)
            for ph in list(plan)[1:]:
                load(sp, ph)

        with nc.Block() as block:
            @block.sync
            def _(sp):
                sp.dma_start(c.X[:, 0:GB, :], dram["x"][:, 0:GB, :]).then_inc(s_x, 16)
                sp.dma_start(c.identf[:, :], dram["identf"]).then_inc(sem[1], 16)
                sp.dma_start(c.identb[:, :], dram["identb"]).then_inc(sem[1], 16)
                load(sp, 1)

            @block.vector
            def _(dve):
                nc.vector.memset(c.ln["eps"][:, :], EPS)
                nc.vector.memset(c.ln["half"][:, :], -0.5).then_inc(s_set, 1)

        attention(c, "a_", False, Ws[1], sem[1], count[1], (s_x, s_rest), later_loads)
        if UPTO >= 2:
            for ph in range(2, UPTO + 1):
                PHASES[ph](c, Ws[ph], sem[ph], count[ph], out)
        if UPTO < 6:
            s_out = c.sem("stored")
            with nc.Block() as block:
                @block.sync
                def _(sp):
                    sp.dma_start(out.rearrange("b p d -> p b d"), c.X[:, :, :]).then_inc(s_out, 16)
                    sp.wait_ge(s_out, 16)


def layout(a):
    f = np.float32
    bf = mybir.dt.np(BF16)
    w = {}
    w["x"] = a["x"].transpose(1, 0, 2)
    w["ctx"] = a["ctx_1024"].transpose(1, 0, 2)
    w["identf"] = np.eye(P, dtype=f)
    w["identb"] = np.eye(P).astype(bf)
    swap = np.arange(D) ^ 1
    w["w1_wq"], w["w1_wk"], w["w1_wv"], w["w1_wo"] = (a["L0_attn_" + n].T for n in ("wq", "wk", "wv", "wo"))
    w["w1_wqp"], w["w1_wkp"] = a["L0_attn_wq"].T[:, swap], a["L0_attn_wk"].T[:, swap]
    freqs = (f(1.0) / f(10000.0) ** (np.arange(0, 8, 2, dtype=f) / f(8))).astype(f)
    ang = np.outer(np.arange(P, dtype=f), freqs).astype(f)
    i = (np.arange(D) % 8) // 2
    w["w1_cos"] = np.cos(ang)[:, i].T.astype(f)
    w["w1_sin"] = (np.sin(ang)[:, i].T * np.where(np.arange(D) % 2, 1, -1)[:, None]).astype(f)
    w["w1_hmask"] = (np.arange(D)[:, None] % 32 // 8 == np.arange(4)[None, :]).astype(f)
    w["w1_gmask"] = w["w5_gmask"] = (np.arange(D)[:, None] // 32 == np.arange(4)[None, :]).astype(f)
    w["w1_cmask"] = np.where(np.arange(P)[None, :] > np.arange(P)[:, None], -BIG, 0.0).astype(bf)
    order = np.array([4 * (i % 2) + i // 2 for i in range(8)])
    head = lambda m: m[order].transpose(1, 0, 2).reshape(D, D)
    for k in (1, 2):
        w[f"w2_wq{k}"] = head(a[f"L0_xattn_Wq{k}"])
        w[f"w2_wkv{k}"] = np.stack([head(a[f"L0_xattn_Wk{k}"]), head(a[f"L0_xattn_Wv{k}"])], 1)
        wo = a[f"L0_xattn_Wo{k}"].T.reshape(4, 2, 16, D)
        z = np.zeros((4, 2, 16, 2, 2, D), f)
        for hl in (0, 1):
            for t in (0, 1):
                z[:, hl, :, hl, t, :] = wo[:, t]
        w[f"w2_wo{k}"] = z.reshape(D, 2, 2, D)
    w["w2_e1"], w["w2_e2"] = a["L0_xattn_E1"], a["L0_xattn_E2"]
    w["w2_d1"], w["w2_d2"] = a["L0_xattn_D1"].T, a["L0_xattn_D2"].T
    w["w2_bdm"] = (np.arange(D)[:, None] // 16 == np.arange(D)[None, :] // 16).astype(f)
    tok = np.arange(P) % 16 * 8 + np.arange(P) // 16
    w["w2_qmask"] = np.where(np.arange(D)[None, :] % 16 > tok[:, None], -BIG, 0.0).astype(bf)
    for n in ("g1", "b1", "g2", "b2", "g3", "b3"):
        w["w2_" + n] = np.tile(a["L0_xattn_" + n], (P, 1))
    w["w3_rw"] = a["L0_ffn_router_w"].T
    w["w3_rb"] = np.tile(a["L0_ffn_router_bias"], (P, 1))
    w["w3_idx"] = np.tile(np.arange(8, 0, -1, dtype=f), (P, 1))
    w["w3_sw1"], w["w3_sw3"] = a["L0_ffn_sw1"], a["L0_ffn_sw3"]
    w["w3_sw2"] = a["L0_ffn_sw2"].reshape(2, P, D).transpose(1, 0, 2)
    w["w3_ew1"], w["w3_ew2"] = a["L0_ffn_ew1"].transpose(1, 0, 2), a["L0_ffn_ew2"].transpose(1, 0, 2)
    ch = lambda m: m.reshape(2, P, -1).transpose(1, 0, 2)
    w["w4_lnw"], w["w4_lnb"] = a["L1_attn_ln_w"][:, None], a["L1_attn_ln_b"][:, None]
    w["w4_win"], w["w4_wdt"] = a["L1_attn_W_in"], a["L1_attn_W_dt"]
    w["w4_cw"] = ch(a["L1_attn_conv_w"])
    w["w4_cb"], w["w4_bdt"], w["w4_dp"] = (ch(a["L1_attn_" + n])[:, :, 0] for n in ("conv_b", "b_dt", "D_param"))
    w["w4_alog"], w["w4_wout"] = ch(a["L1_attn_A_log"]), ch(a["L1_attn_W_out"])
    wx = ch(a["L1_attn_W_xproj"])
    w["w4_wxd"], w["w4_wxb"] = wx[:, :, 0:8], np.tile(wx[:, :, 8:40], (1, 1, 3))
    w["w4_sel"] = (np.arange(96)[:, None] % 32 == np.arange(32)[None, :]).astype(bf)
    for n in ("q", "k", "v", "o"):
        w["w5_w" + n] = a["L1_xattn_W" + n].T
    w["w5_bq"], w["w5_bk"] = a["L1_xattn_bq"][:, None], a["L1_xattn_bk"][:, None]
    w["w5_bv"], w["w5_bo"] = np.tile(a["L1_xattn_bv"], (P, 1)), np.tile(a["L1_xattn_bo"], (P, 1))
    w["w5_hmask"], w["w5_amask"] = w["w1_hmask"], a["fside_SxS2_0"]
    w["w5_pad"] = np.broadcast_to(a["mask_BxS2_bf0"][None], (P, B, S2))
    w["w6_gw"], w["w6_idx"], w["w6_ones"] = a["L1_ffn_gate_W"].T, w["w3_idx"], np.ones((P, P), f)
    w["w6_wg"], w["w6_wu"] = (a["L1_ffn_W_" + n].transpose(2, 0, 1) for n in ("gate", "up"))
    w["w6_wd"] = a["L1_ffn_W_down"].transpose(2, 0, 1).reshape(4, P, 8, D).transpose(1, 2, 0, 3)
    return w


def kernel(**inputs):
    import concourse.bacc as _bacc
    from concourse.bass_utils import run_bass_kernel_spmd as _run

    a = {k: np.asarray(v) for k, v in inputs.items()}
    lay = layout(a)
    need = ["x", "ctx", "identf", "identb"] + [f"w{ph}_{n}" for ph, ws in plan_weights().items() for n in ws]
    nc = _bacc.Bacc("TRN2", target_bir_lowering=False, num_devices=1)
    arrays, dram = {}, {}
    for name in need:
        v = np.ascontiguousarray(lay[name])
        arrays[f"in_{name}"] = v
        dram[name] = nc.dram_tensor(f"in_{name}", v.shape, mybir.dt.from_np(v.dtype), kind="ExternalInput").ap()
    out = nc.dram_tensor("out_0_dram", (B, P, D), F32, kind="ExternalOutput").ap()
    program(nc, dram, out)
    r = _run(nc, [arrays], core_ids=[0])
    return r.results[0]["out_0_dram"]
```
